# Optimizing a Trainium2 kernel written in Bass

```python
import numpy as np
import jax
import jax.numpy as jnp

def _softmax(x, axis=-1):
    return jax.nn.softmax(x, axis=axis)

def _gelu(x):
    return jax.nn.gelu(x, approximate=True)

def _silu(x):
    return jax.nn.silu(x)

def _sigmoid(x):
    return jax.nn.sigmoid(x)

def _layernorm(x, axis=-1, eps=1e-05):
    m = jnp.mean(x, axis=axis, keepdims=True)
    v = jnp.var(x, axis=axis, keepdims=True)
    return (x - m) / jnp.sqrt(v + eps)

def _scatter_add(tgt, idx, src, axis=0):
    return tgt.at[idx].add(src)

def _segment_sum(src, seg, n):
    return jax.ops.segment_sum(src, seg, n)
kernel_name = 'mk_hybrid_d1_jaxref_r8_cbbf56'

def setup_inputs(seed: int=0):
    np.random.seed(seed)
    _w = jnp.asarray

    def _L0_attn_a_setup():
        import jax, jax.numpy as jnp
        import numpy as np
        WINDOWS = (64, 128, 256)
        NUM_HEADS = 16
        DIM = 128
        LN_EPS = 1e-05

        def _layer_norm(x, g, b):
            mu = jnp.mean(x, axis=-1, keepdims=True)
            var = jnp.mean(jnp.square(x - mu), axis=-1, keepdims=True)
            return (x - mu) * jax.lax.rsqrt(var + LN_EPS) * g + b

        def _scale_attention(x, L, ws, Wq, bq, Wk, bk, Wv, bv, Wo, bo, g, beta):
            B, _, D = x.shape
            H = NUM_HEADS
            hd = D // H
            pad = -L % ws
            xp = jnp.pad(x, ((0, 0), (0, pad), (0, 0)))
            Lp = L + pad

            def proj(W, b):
                y = xp @ W.T + b
                return y.reshape(B, Lp, H, hd).transpose(0, 2, 1, 3)
            q = proj(Wq, bq)
            k = proj(Wk, bk)
            v = proj(Wv, bv)
            scores = jnp.einsum('bhqd,bhkd->bhqk', q, k) * jnp.sqrt(jnp.float32(hd))
            causal = jnp.triu(jnp.ones((Lp, Lp), dtype=bool), k=1)
            scores = jnp.where(causal, -jnp.inf, scores)
            m = jnp.max(scores, axis=-1, keepdims=True)
            e = jnp.exp(scores - m)
            e = jnp.where(causal, 0.0, e)
            w = e / (jnp.sum(e, axis=-1, keepdims=True) + 1e-06)
            out = jnp.einsum('bhqk,bhkd->bhqd', w, v)
            out = out.transpose(0, 2, 1, 3).reshape(B, Lp, D)
            out = out @ Wo.T + bo
            out = _layer_norm(out, g, beta)
            return out[:, :L]
        key = jax.random.key(seed)
        ks = jax.random.split(key, 8)
        D, S = (DIM, len(WINDOWS))
        w = lambda k, shape: (0.02 * jax.random.normal(k, shape)).astype(jnp.float32)
        return {'x': jax.random.normal(ks[0], (1, 64, D), dtype=jnp.float32), 'Wq': w(ks[1], (S, D, D)), 'bq': jnp.zeros((S, D), jnp.float32), 'Wk': w(ks[2], (S, D, D)), 'bk': jnp.zeros((S, D), jnp.float32), 'Wv': w(ks[3], (S, D, D)), 'bv': jnp.zeros((S, D), jnp.float32), 'Wo': w(ks[4], (S, D, D)), 'bo': jnp.zeros((S, D), jnp.float32), 'ln_g': jnp.ones((S, D), jnp.float32), 'ln_b': jnp.zeros((S, D), jnp.float32), 'Wout': w(ks[5], (D, S * D)), 'bout': jnp.zeros((D,), jnp.float32), 'ln2_g': jnp.ones((D,), jnp.float32), 'ln2_b': jnp.zeros((D,), jnp.float32)}
    _L0_attn_a_in = _L0_attn_a_setup()

    def _L0_attn_b_setup():
        import math
        import jax, jax.numpy as jnp
        import numpy as np
        B, T, D_MODEL, N_HEADS = (2, 256, 128, 16)
        HEAD_DIM = D_MODEL // N_HEADS

        def _alibi_slopes(n_heads: int) -> np.ndarray:

            def pow2(n):
                start = 2.0 ** (-(8.0 / n))
                return [start * start ** i for i in range(n)]
            if math.log2(n_heads).is_integer():
                s = pow2(n_heads)
            else:
                cp = 2 ** math.floor(math.log2(n_heads))
                base = pow2(cp)
                extra = pow2(2 * cp)[1::2]
                s = base + extra[:n_heads - cp]
            return np.asarray(s, dtype=np.float32)
        SLOPES = jnp.asarray(_alibi_slopes(N_HEADS))
        key = jax.random.key(seed)
        k1, k2, k3 = jax.random.split(key, 3)
        x = jax.random.normal(k1, (B, T, D_MODEL), dtype=jnp.float32)
        Wqkv = jax.random.normal(k2, (D_MODEL, 3 * D_MODEL), dtype=jnp.float32) * 0.02
        Wout = jax.random.normal(k3, (D_MODEL, D_MODEL), dtype=jnp.float32) * 0.02
        return {'x': x, 'Wqkv': Wqkv, 'Wout': Wout}
    _L0_attn_b_in = _L0_attn_b_setup()

    def _L0_ffn_setup():
        import jax, jax.numpy as jnp
        import numpy as np
        DIM = 128
        DEPTH = 6
        HEADS = 16
        DIM_HEAD = 64
        WINDOW = 32
        INNER = HEADS * DIM_HEAD
        DIM_INNER = int(DIM * 4 * 2 / 3)
        QK_SCALE = 8.0

        def shift_tokens(t):
            a, s = jnp.split(t, 2, -1)
            s = jnp.pad(s, ((0, 0), (1, 0), (0, 0)))[:, :-1]
            return jnp.concatenate([a, s], -1)

        def l2norm(t):
            return t / jnp.maximum(jnp.linalg.norm(t, axis=-1, keepdims=True), 1e-12)

        def rotate_half(x):
            x1, x2 = jnp.split(x, 2, -1)
            return jnp.concatenate([-x2, x1], -1)

        def rotary_tables(n):
            half = jnp.arange(0, DIM_HEAD, 2, dtype=jnp.float32)
            inv_freq = 1.0 / 10000.0 ** (half / DIM_HEAD)
            t = jnp.arange(n, dtype=jnp.float32)
            freqs = t[:, None] * inv_freq[None, :]
            freqs = jnp.concatenate([freqs, freqs], -1)
            base_scale = (half + 0.4 * DIM_HEAD) / (1.4 * DIM_HEAD)
            power = (t - n // 2) / (WINDOW // 2)
            scale = base_scale[None, :] ** power[:, None]
            scale = jnp.concatenate([scale, scale], -1)
            return (freqs, scale)

        def local_attention(q, k, v):
            b, h, n, d = q.shape
            w = WINDOW
            nw = n // w
            bq = q.reshape(b, h, nw, w, d)
            bk = k.reshape(b, h, nw, w, d)
            bv = v.reshape(b, h, nw, w, d)

            def look(t):
                p = jnp.pad(t, ((0, 0), (0, 0), (1, 0), (0, 0), (0, 0)))
                return jnp.concatenate([p[:, :, :nw], p[:, :, 1:]], axis=3)
            bk2, bv2 = (look(bk), look(bv))
            seq = jnp.arange(n).reshape(nw, w)
            seq_p = jnp.pad(seq, ((1, 0), (0, 0)), constant_values=-1)
            jt = jnp.concatenate([seq_p[:nw], seq_p[1:]], axis=1)
            it = seq[:, :, None]
            jb = jt[:, None, :]
            mask = (it < jb) | (it > jb + w) | (jb == -1)
            sim = jnp.einsum('bhwie,bhwje->bhwij', bq, bk2) * QK_SCALE
            sim = jnp.where(mask, -jnp.finfo(sim.dtype).max, sim)
            attn = jax.nn.softmax(sim, -1)
            out = jnp.einsum('bhwij,bhwje->bhwie', attn, bv2)
            return out.reshape(b, h, n, d)

        def attn_layer(x, Wqkv, qs, ksc, Wo):
            b, n, _ = x.shape
            qkv = x @ Wqkv
            q, k, v = jnp.split(qkv, 3, -1)
            sh = lambda t: t.reshape(b, n, HEADS, DIM_HEAD).transpose(0, 2, 1, 3)
            q, k, v = (sh(q), sh(k), sh(v))
            q = l2norm(q) * qs
            k = l2norm(k) * ksc
            freqs, scale = rotary_tables(n)
            cos, sin = (jnp.cos(freqs), jnp.sin(freqs))
            q = q * cos * scale + rotate_half(q) * sin * scale
            inv = 1.0 / scale
            k = k * cos * inv + rotate_half(k) * sin * inv
            out = local_attention(q, k, v)
            out = out.transpose(0, 2, 1, 3).reshape(b, n, INNER)
            return out @ Wo

        def ffn_layer(x, g, bln, W1, b1, W2, b2):
            mu = x.mean(-1, keepdims=True)
            var = ((x - mu) ** 2).mean(-1, keepdims=True)
            xn = (x - mu) / jnp.sqrt(var + 1e-05) * g + bln
            hg = xn @ W1 + b1
            a, gate = jnp.split(hg, 2, -1)
            return a * jax.nn.gelu(gate, approximate=False) @ W2 + b2
        key = jax.random.key(seed)
        ks = jax.random.split(key, 8)
        B, N = (2, 256)
        init = lambda k, shape: jax.random.normal(k, shape, jnp.float32) * 0.02
        return {'x': jax.random.normal(ks[0], (B, N, DIM), jnp.float32), 'Wqkv': init(ks[1], (DEPTH, DIM, 3 * INNER)), 'q_scale': jnp.ones((DEPTH, DIM_HEAD), jnp.float32), 'k_scale': jnp.ones((DEPTH, DIM_HEAD), jnp.float32), 'Wo': init(ks[2], (DEPTH, INNER, DIM)), 'ln_g': jnp.ones((DEPTH, DIM), jnp.float32), 'ln_b': jnp.zeros((DEPTH, DIM), jnp.float32), 'W1': init(ks[3], (DEPTH, DIM, 2 * DIM_INNER)), 'b1': jnp.zeros((DEPTH, 2 * DIM_INNER), jnp.float32), 'W2': init(ks[4], (DEPTH, DIM_INNER, DIM)), 'b2': jnp.zeros((DEPTH, DIM), jnp.float32)}
    _L0_ffn_in = _L0_ffn_setup()
    _d = {'L0_attn_a_x': _L0_attn_a_in['x'], 'L0_attn_a_Wq': _L0_attn_a_in['Wq'], 'L0_attn_a_bq': _L0_attn_a_in['bq'], 'L0_attn_a_Wk': _L0_attn_a_in['Wk'], 'L0_attn_a_bk': _L0_attn_a_in['bk'], 'L0_attn_a_Wv': _L0_attn_a_in['Wv'], 'L0_attn_a_bv': _L0_attn_a_in['bv'], 'L0_attn_a_Wo': _L0_attn_a_in['Wo'], 'L0_attn_a_bo': _L0_attn_a_in['bo'], 'L0_attn_a_ln_g': _L0_attn_a_in['ln_g'], 'L0_attn_a_ln_b': _L0_attn_a_in['ln_b'], 'L0_attn_a_Wout': _L0_attn_a_in['Wout'], 'L0_attn_a_bout': _L0_attn_a_in['bout'], 'L0_attn_a_ln2_g': _L0_attn_a_in['ln2_g'], 'L0_attn_a_ln2_b': _L0_attn_a_in['ln2_b'], 'L0_attn_b_Wqkv': _L0_attn_b_in['Wqkv'], 'L0_attn_b_Wout': _L0_attn_b_in['Wout'], 'L0_ffn_Wqkv': _L0_ffn_in['Wqkv'], 'L0_ffn_q_scale': _L0_ffn_in['q_scale'], 'L0_ffn_k_scale': _L0_ffn_in['k_scale'], 'L0_ffn_Wo': _L0_ffn_in['Wo'], 'L0_ffn_ln_g': _L0_ffn_in['ln_g'], 'L0_ffn_ln_b': _L0_ffn_in['ln_b'], 'L0_ffn_W1': _L0_ffn_in['W1'], 'L0_ffn_b1': _L0_ffn_in['b1'], 'L0_ffn_W2': _L0_ffn_in['W2'], 'L0_ffn_b2': _L0_ffn_in['b2']}
    _x0 = _d['L0_attn_a_x']
    _d['L0_attn_a_x'] = jax.random.normal(jax.random.fold_in(jax.random.key(seed), 1), (2, 1024, 128), dtype=_x0.dtype)
    del _x0
    return _d

def reference(L0_attn_a_x, L0_attn_a_Wq, L0_attn_a_bq, L0_attn_a_Wk, L0_attn_a_bk, L0_attn_a_Wv, L0_attn_a_bv, L0_attn_a_Wo, L0_attn_a_bo, L0_attn_a_ln_g, L0_attn_a_ln_b, L0_attn_a_Wout, L0_attn_a_bout, L0_attn_a_ln2_g, L0_attn_a_ln2_b, L0_attn_b_Wqkv, L0_attn_b_Wout, L0_ffn_Wqkv, L0_ffn_q_scale, L0_ffn_k_scale, L0_ffn_Wo, L0_ffn_ln_g, L0_ffn_ln_b, L0_ffn_W1, L0_ffn_b1, L0_ffn_W2, L0_ffn_b2):

    def _L0_attn_a_ref(x, Wq, bq, Wk, bk, Wv, bv, Wo, bo, ln_g, ln_b, Wout, bout, ln2_g, ln2_b):
        import jax, jax.numpy as jnp
        import numpy as np
        WINDOWS = (64, 128, 256)
        NUM_HEADS = 16
        DIM = 128
        LN_EPS = 1e-05

        def _layer_norm(x, g, b):
            mu = jnp.mean(x, axis=-1, keepdims=True)
            var = jnp.mean(jnp.square(x - mu), axis=-1, keepdims=True)
            return (x - mu) * jax.lax.rsqrt(var + LN_EPS) * g + b

        def _scale_attention(x, L, ws, Wq, bq, Wk, bk, Wv, bv, Wo, bo, g, beta):
            B, _, D = x.shape
            H = NUM_HEADS
            hd = D // H
            pad = -L % ws
            xp = jnp.pad(x, ((0, 0), (0, pad), (0, 0)))
            Lp = L + pad

            def proj(W, b):
                y = xp @ W.T + b
                return y.reshape(B, Lp, H, hd).transpose(0, 2, 1, 3)
            q = proj(Wq, bq)
            k = proj(Wk, bk)
            v = proj(Wv, bv)
            scores = jnp.einsum('bhqd,bhkd->bhqk', q, k) * jnp.sqrt(jnp.float32(hd))
            causal = jnp.triu(jnp.ones((Lp, Lp), dtype=bool), k=1)
            scores = jnp.where(causal, -jnp.inf, scores)
            m = jnp.max(scores, axis=-1, keepdims=True)
            e = jnp.exp(scores - m)
            e = jnp.where(causal, 0.0, e)
            w = e / (jnp.sum(e, axis=-1, keepdims=True) + 1e-06)
            out = jnp.einsum('bhqk,bhkd->bhqd', w, v)
            out = out.transpose(0, 2, 1, 3).reshape(B, Lp, D)
            out = out @ Wo.T + bo
            out = _layer_norm(out, g, beta)
            return out[:, :L]
        B, L, D = x.shape
        outs = []
        for i, ws in enumerate(WINDOWS):
            outs.append(_scale_attention(x, L, ws, Wq[i], bq[i], Wk[i], bk[i], Wv[i], bv[i], Wo[i], bo[i], ln_g[i], ln_b[i]))
        multi = jnp.concatenate(outs, axis=-1)
        out = multi @ Wout.T + bout
        out = _layer_norm(out, ln2_g, ln2_b)
        return out

    def _L0_attn_b_ref(x, Wqkv, Wout):
        import math
        import jax, jax.numpy as jnp
        import numpy as np
        B, T, D_MODEL, N_HEADS = (2, 256, 128, 16)
        HEAD_DIM = D_MODEL // N_HEADS

        def _alibi_slopes(n_heads: int) -> np.ndarray:

            def pow2(n):
                start = 2.0 ** (-(8.0 / n))
                return [start * start ** i for i in range(n)]
            if math.log2(n_heads).is_integer():
                s = pow2(n_heads)
            else:
                cp = 2 ** math.floor(math.log2(n_heads))
                base = pow2(cp)
                extra = pow2(2 * cp)[1::2]
                s = base + extra[:n_heads - cp]
            return np.asarray(s, dtype=np.float32)
        SLOPES = jnp.asarray(_alibi_slopes(N_HEADS))
        Bc, Tc, Dc = x.shape
        qkv = x @ Wqkv
        q, k, v = jnp.split(qkv, 3, axis=-1)
        q = q.reshape(Bc, Tc, N_HEADS, HEAD_DIM)
        k = k.reshape(Bc, Tc, N_HEADS, HEAD_DIM)
        v = v.reshape(Bc, Tc, N_HEADS, HEAD_DIM)
        scale = 1.0 / math.sqrt(HEAD_DIM)
        logits = jnp.einsum('bihd,bjhd->bhij', q, k) * scale
        pos = jnp.arange(Tc, dtype=jnp.float32)
        rel = pos[None, :] - pos[:, None]
        logits = logits + SLOPES[None, :, None, None] * rel[None, None, :, :]
        causal = pos[:, None] >= pos[None, :]
        logits = jnp.where(causal[None, None, :, :], logits, -jnp.inf)
        attn = jax.nn.softmax(logits, axis=-1)
        out = jnp.einsum('bhij,bjhd->bihd', attn, v).reshape(Bc, Tc, Dc)
        return out @ Wout

    def _L0_ffn_ref(x, Wqkv, q_scale, k_scale, Wo, ln_g, ln_b, W1, b1, W2, b2):
        import jax, jax.numpy as jnp
        import numpy as np
        DIM = 128
        DEPTH = 6
        HEADS = 16
        DIM_HEAD = 64
        WINDOW = 32
        INNER = HEADS * DIM_HEAD
        DIM_INNER = int(DIM * 4 * 2 / 3)
        QK_SCALE = 8.0

        def shift_tokens(t):
            a, s = jnp.split(t, 2, -1)
            s = jnp.pad(s, ((0, 0), (1, 0), (0, 0)))[:, :-1]
            return jnp.concatenate([a, s], -1)

        def l2norm(t):
            return t / jnp.maximum(jnp.linalg.norm(t, axis=-1, keepdims=True), 1e-12)

        def rotate_half(x):
            x1, x2 = jnp.split(x, 2, -1)
            return jnp.concatenate([-x2, x1], -1)

        def rotary_tables(n):
            half = jnp.arange(0, DIM_HEAD, 2, dtype=jnp.float32)
            inv_freq = 1.0 / 10000.0 ** (half / DIM_HEAD)
            t = jnp.arange(n, dtype=jnp.float32)
            freqs = t[:, None] * inv_freq[None, :]
            freqs = jnp.concatenate([freqs, freqs], -1)
            base_scale = (half + 0.4 * DIM_HEAD) / (1.4 * DIM_HEAD)
            power = (t - n // 2) / (WINDOW // 2)
            scale = base_scale[None, :] ** power[:, None]
            scale = jnp.concatenate([scale, scale], -1)
            return (freqs, scale)

        def local_attention(q, k, v):
            b, h, n, d = q.shape
            w = WINDOW
            nw = n // w
            bq = q.reshape(b, h, nw, w, d)
            bk = k.reshape(b, h, nw, w, d)
            bv = v.reshape(b, h, nw, w, d)

            def look(t):
                p = jnp.pad(t, ((0, 0), (0, 0), (1, 0), (0, 0), (0, 0)))
                return jnp.concatenate([p[:, :, :nw], p[:, :, 1:]], axis=3)
            bk2, bv2 = (look(bk), look(bv))
            seq = jnp.arange(n).reshape(nw, w)
            seq_p = jnp.pad(seq, ((1, 0), (0, 0)), constant_values=-1)
            jt = jnp.concatenate([seq_p[:nw], seq_p[1:]], axis=1)
            it = seq[:, :, None]
            jb = jt[:, None, :]
            mask = (it < jb) | (it > jb + w) | (jb == -1)
            sim = jnp.einsum('bhwie,bhwje->bhwij', bq, bk2) * QK_SCALE
            sim = jnp.where(mask, -jnp.finfo(sim.dtype).max, sim)
            attn = jax.nn.softmax(sim, -1)
            out = jnp.einsum('bhwij,bhwje->bhwie', attn, bv2)
            return out.reshape(b, h, n, d)

        def attn_layer(x, Wqkv, qs, ksc, Wo):
            b, n, _ = x.shape
            qkv = x @ Wqkv
            q, k, v = jnp.split(qkv, 3, -1)
            sh = lambda t: t.reshape(b, n, HEADS, DIM_HEAD).transpose(0, 2, 1, 3)
            q, k, v = (sh(q), sh(k), sh(v))
            q = l2norm(q) * qs
            k = l2norm(k) * ksc
            freqs, scale = rotary_tables(n)
            cos, sin = (jnp.cos(freqs), jnp.sin(freqs))
            q = q * cos * scale + rotate_half(q) * sin * scale
            inv = 1.0 / scale
            k = k * cos * inv + rotate_half(k) * sin * inv
            out = local_attention(q, k, v)
            out = out.transpose(0, 2, 1, 3).reshape(b, n, INNER)
            return out @ Wo

        def ffn_layer(x, g, bln, W1, b1, W2, b2):
            mu = x.mean(-1, keepdims=True)
            var = ((x - mu) ** 2).mean(-1, keepdims=True)
            xn = (x - mu) / jnp.sqrt(var + 1e-05) * g + bln
            hg = xn @ W1 + b1
            a, gate = jnp.split(hg, 2, -1)
            return a * jax.nn.gelu(gate, approximate=False) @ W2 + b2
        for i in range(DEPTH):
            x = attn_layer(shift_tokens(x), Wqkv[i], q_scale[i], k_scale[i], Wo[i]) + x
            x = ffn_layer(shift_tokens(x), ln_g[i], ln_b[i], W1[i], b1[i], W2[i], b2[i]) + x
        return x
    x = L0_attn_a_x
    x = x + _L0_attn_a_ref(_layernorm(x, axis=-1), L0_attn_a_Wq, L0_attn_a_bq, L0_attn_a_Wk, L0_attn_a_bk, L0_attn_a_Wv, L0_attn_a_bv, L0_attn_a_Wo, L0_attn_a_bo, L0_attn_a_ln_g, L0_attn_a_ln_b, L0_attn_a_Wout, L0_attn_a_bout, L0_attn_a_ln2_g, L0_attn_a_ln2_b)
    x = x + _L0_ffn_ref(_layernorm(x, axis=-1), L0_ffn_Wqkv, L0_ffn_q_scale, L0_ffn_k_scale, L0_ffn_Wo, L0_ffn_ln_g, L0_ffn_ln_b, L0_ffn_W1, L0_ffn_b1, L0_ffn_W2, L0_ffn_b2)
    x = x + _L0_attn_b_ref(_layernorm(x, axis=-1), L0_attn_b_Wqkv, L0_attn_b_Wout)
    x = x + _L0_ffn_ref(_layernorm(x, axis=-1), L0_ffn_Wqkv, L0_ffn_q_scale, L0_ffn_k_scale, L0_ffn_Wo, L0_ffn_ln_g, L0_ffn_ln_b, L0_ffn_W1, L0_ffn_b1, L0_ffn_W2, L0_ffn_b2)
    return x

_drawn_inputs = setup_inputs


def setup_inputs(seed=0):
    import zlib

    import numpy as np

    out = dict(_drawn_inputs(seed))
    spreads = {'L0_attn_a_bq': (0.0, 0.8),
     'L0_attn_a_bk': (0.0, 0.8),
     'L0_attn_a_bv': (0.0, 0.1),
     'L0_attn_a_bo': (0.0, 0.1),
     'L0_attn_a_ln_g': (1.0, 0.2),
     'L0_attn_a_ln_b': (0.0, 0.1),
     'L0_attn_a_bout': (0.0, 0.1),
     'L0_attn_a_ln2_g': (1.0, 0.2),
     'L0_attn_a_ln2_b': (0.0, 0.1),
     'L0_ffn_q_scale': (1.0, 0.6),
     'L0_ffn_k_scale': (1.0, 0.6),
     'L0_ffn_ln_g': (1.0, 0.6),
     'L0_ffn_ln_b': (0.0, 0.8),
     'L0_ffn_b1': (0.0, 0.747),
     'L0_ffn_b2': (0.0, 0.1)}
    factors = {'L0_attn_a_Wq': 3.705,
     'L0_attn_a_Wk': 3.331,
     'L0_attn_b_Wqkv': 3.739,
     'L0_attn_b_Wout': 4.093,
     'L0_ffn_W2': 2.675}
    for name, (base, spread) in spreads.items():
        noise = np.random.default_rng([zlib.crc32(name.encode()), seed]).standard_normal(out[name].shape)
        drawn = base * np.exp(spread * noise) if base else spread * noise
        out[name] = jnp.asarray(drawn.astype(out[name].dtype))
    for name, factor in factors.items():
        out[name] = (out[name] * factor).astype(out[name].dtype)
    return out
```

```python
from contextlib import ExitStack

import numpy as np

import concourse.bass as bass
from concourse import mybir

F32 = mybir.dt.float32
BF16 = mybir.dt.bfloat16
ALU = mybir.AluOpType
ACT = mybir.ActivationFunctionType
AX = mybir.AxisListType

P = 128
BATCH, SEQ = 2, 1024
TOK = BATCH * SEQ
HEADS, HD = 16, 8
QT = SEQ // P
QUADS = HEADS // 4
SCALES = 3
DEPTH = 6
LH, LD = 16, 64
INNER = LH * LD
WIN = 32
HID = 341
HCH = [(0, 128), (128, 128), (256, 85)]
XW_COLS = WIN + 1 + SEQ
LN_EPS = 1e-5
CH = 512
NEG = -1e30
START = 1

COMBO_Q = [0, 0, 0, 1, 1, 2]
COMBO_K = [0, 1, 2, 0, 1, 0]
MROW = 8 * len(COMBO_Q)
AROW = MROW + 3
CROWS = 9

STEPS = [(c, kt, max(CH * c, P * kt), CH * (c + 1) - max(CH * c, P * kt))
         for c in range(2) for kt in range(4 * c + 4)]
NSTEP = len(STEPS)


def quad_order():
    first = [(j, qt) for j in range(4) for qt in range(QT)]
    cost1 = [P * (qt + 1) for _, qt in first]
    total1, total2 = sum(cost1), 4 * sum(w for *_, w in STEPS)
    out, done1, done2, at = [], 0, 0, 0
    for s, (_, _, _, w) in enumerate(STEPS):
        for j in range(4):
            while at < len(first) and done1 * total2 <= done2 * total1:
                out.append(("first", *first[at]))
                done1 += cost1[at]
                at += 1
            out.append(("second", s, j))
            done2 += w
        if s:
            out.append(("values", s - 1, 0))
    out += [("first", *f) for f in first[at:]]
    out.append(("values", NSTEP - 1, 0))
    return out


ORDER = quad_order()
PLAN = (("causal", "a"), ("layers", 0), ("causal", "b"), ("layers", 1))


def build(nc, t, out, scratch):
    with ExitStack() as ctx:
        def sb(name, shape, dt=F32, stack=ctx):
            return stack.enter_context(nc.sbuf_tensor(name, shape, dt))

        names = {}

        def sem(name):
            if name not in names:
                names[name] = ctx.enter_context(nc.semaphore(name))
            return names[name]

        ps = ctx.enter_context(nc.psum_tensor("ps", [P, 8, CH], F32))

        res = sb("res", [P, TOK])
        ident = sb("ident", [P, P])
        identb = sb("identb", [P, P], BF16)
        mean_w = sb("mean_w", [P, P])
        eps_col = sb("eps_col", [P, 1])
        lnc = sb("lnc", [P, CH])
        lnq = sb("lnq", [P, CH])
        lnr = sb("lnr", [P, CH])
        step = sem("step")
        const_in = sem("const_in")
        out_done = sem("out_done")

        def ln_pe(pe, k, src, first_bank=6):
            pe.wait_ge(step, k)
            nc.tensor.matmul(ps[:, first_bank, :], mean_w[:], src, start=True, stop=True).then_inc(step, 1)
            pe.wait_ge(step, k + 3)
            nc.tensor.matmul(ps[:, first_bank + 1, :], mean_w[:], lnq[:], start=True, stop=True).then_inc(step, 1)

        def ln_act(act, k, first_bank=6):
            act.wait_ge(step, k + 2)
            nc.scalar.activation(lnq[:], lnc[:], ACT.Square).then_inc(step, 1)
            act.wait_ge(step, k + 4)
            nc.scalar.activation(lnq[:], ps[:, first_bank + 1, :], ACT.Sqrt, bias=eps_col[:, 0:1]).then_inc(step, 1)

        def ln_dve(dve, k, src, dst, gain=None, shift=None, first_bank=6):
            dve.wait_ge(step, k + 1)
            nc.vector.tensor_tensor(lnc[:], src, ps[:, first_bank, :], ALU.subtract).then_inc(step, 1)
            dve.wait_ge(step, k + 5)
            nc.vector.reciprocal(lnr[:], lnq[:]).then_inc(step, 1)
            dve.wait_ge(step, k + 6)
            if gain is None:
                nc.vector.tensor_tensor(dst, lnc[:], lnr[:], ALU.mult).then_inc(step, 1)
                dve.wait_ge(step, k + 7)
                dve.nop().then_inc(step, 1)
            else:
                nc.vector.tensor_tensor(lnc[:], lnc[:], lnr[:], ALU.mult).then_inc(step, 1)
                dve.wait_ge(step, k + 7)
                nc.vector.tensor_scalar(dst, lnc[:], gain, shift, ALU.mult, ALU.add).then_inc(step, 1)

        LN = 8
        at = [0]

        with nc.Block() as block:
            @block.sync
            def _(sp):
                sp.dma_start(res[:], t["x"]).then_inc(const_in, 16)
                sp.dma_start(ident[:], t["ident"]).then_inc(const_in, 16)
                sp.dma_start(identb[:], t["identb"]).then_inc(const_in, 16)
                sp.wait_ge(const_in, 48)

            @block.gpsimd
            def _(pool):
                nc.gpsimd.memset(mean_w[:], 1.0 / P)
                nc.gpsimd.memset(eps_col[:], LN_EPS)

        def causal(kind):
            with ExitStack() as local:
                def lb(name, shape, dt=F32):
                    return sb(f"{kind}_{name}", shape, dt, local)

                xl = lb("xl", [P, TOK])
                qs = [lb(f"qs{i}", [P, HEADS, SEQ], BF16) for i in range(2)]
                ks = [lb(f"ks{i}", [P, HEADS, SEQ], BF16) for i in range(2)]
                vrow = lb("vrow", [P, QT, P])
                vq = lb("vq", [P, QT, 4, 32])
                pt = lb("pt", [P, 2, 4, CH])
                nm = lb("nm", [P, P])
                ot = lb("ot", [P, QUADS, SEQ])
                mask_q = lb("mask_q", [P, P], BF16)
                mask_k = lb("mask_k", [P, P], BF16)
                sel = lb("sel", [P, P])
                wts = lb("wts", [P, 3, P])
                wop = lb("wop", [P, QUADS, P])
                wout = lb("wout", [P, P])
                cols = lb("cols", [P, 5])
                cols2 = lb("cols2", [P, 3])
                bvb = lb("bvb", [P, P])
                flat = pt[:, :, :, :].rearrange("p a b c -> p (a b c)")
                qkf = [flat[:, 0:SEQ], flat[:, SEQ:2 * SEQ]]
                rest = [flat[:, 2 * SEQ:3 * SEQ], flat[:, 3 * SEQ:4 * SEQ]]
                parts = ot[:, :, :].rearrange("p q n -> p (q n)")[:, 0:3 * SEQ].bitcast(BF16).rearrange("p (a c n) -> p a c n", a=2, c=3)
                mparts = lb("mparts", [P, 3, P], BF16)
                mrest = lb("mrest", [P, P])
                rden = lnr
                on = pt[:, 0, :, :]
                yo = lb("yo", [P, CH])
                acc = lb("acc", [P, SEQ])

                scales = SCALES if kind == "a" else 1
                units = [(s, b) for b in range(BATCH) for s in range(scales)]
                qscale = float(HD) ** (0.5 if kind == "a" else -0.5)
                den_eps = 1e-6 if kind == "a" else 0.0
                k = kind
                setup_in, w_in, part_out, stack_in = sem(k + "setup_in"), sem(k + "w_in"), sem(k + "part_out"), sem(k + "stack_in")
                s1_ready, s1_free = sem(k + "s1_ready"), sem(k + "s1_free")
                s2_ready, s2_free = sem(k + "s2_ready"), sem(k + "s2_free")
                pt_free = sem(k + "pt_free")
                ot_free = sem(k + "ot_free")
                vq_ready = sem(k + "vq_ready")

                with nc.Block() as block:
                    @block.sync
                    def _(sp):
                        sp.dma_start(mask_q[:], t["mask_q"]).then_inc(setup_in, 16)
                        sp.dma_start(mask_k[:], t["mask_k"]).then_inc(setup_in, 16)
                        sp.dma_start(sel[:], t["sel"]).then_inc(setup_in, 16)
                        n = 48
                        if kind == "a":
                            for i, name in enumerate(("bout", "ln2_g", "ln2_b")):
                                sp.dma_start(cols2[:, i:i + 1], t[name].rearrange("(p a) -> p a", a=1)).then_inc(setup_in, 16)
                                n += 16
                        sp.wait_ge(setup_in, n)

                    @block.gpsimd
                    def _(pool):
                        nc.gpsimd.memset(vq[:, :, :, :], 0.0).then_inc(vq_ready, 1)
                        nc.gpsimd.memset(wop[:, :, :], 0.0)
                        pool.wait_ge(vq_ready, 1)
                        nc.gpsimd.memset(vq[:, :, :, HD:HD + 1], 1.0)
                        for one in (s1_free, s2_free, pt_free, ot_free):
                            pool.sem_inc(one, START)
                        if kind == "b":
                            nc.gpsimd.memset(cols[:], 0.0)
                            nc.gpsimd.memset(bvb[:], 0.0)

                    @block.vector
                    def _(dve):
                        for i in range(2):
                            nc.vector.memzero(qs[i][:, :, :])
                            nc.vector.memzero(ks[i][:, :, :])
                        nc.vector.memset(nm[:], 0.0).then_inc(s1_free, 1)

                    @block.scalar
                    def _(act):
                        nc.scalar.activation(lnc[:, 0:1], eps_col[:], ACT.Copy).then_inc(s2_free, 1)

                    @block.tensor
                    def _(pe):
                        nc.tensor.matmul(ps[:, 0, 0:P], ident_b(), ident_b(), start=True, stop=True).then_inc(pt_free, 1)

                k0 = at[0]
                at[0] += 4 * LN
                with nc.Block() as block:
                    @block.tensor
                    def _(pe):
                        for c in range(4):
                            ln_pe(pe, k0 + LN * c, res[:, c * CH:(c + 1) * CH])

                    @block.scalar
                    def _(act):
                        for c in range(4):
                            ln_act(act, k0 + LN * c)

                    @block.vector
                    def _(dve):
                        for c in range(4):
                            sl = slice(c * CH, (c + 1) * CH)
                            ln_dve(dve, k0 + LN * c, res[:, sl], xl[:, sl])

                for i in range(len(units) + 1):
                    now = units[i] if i < len(units) else None
                    before = units[i - 1] if i else None

                    if now:
                        s, b = now
                        k0 = at[0]
                        at[0] += 12
                        par = i % 2
                        nw = 16 * (5 if kind == "a" else 2)
                        with nc.Block() as block:
                            @block.sync
                            def _(sp):
                                if kind == "a":
                                    sp.dma_start(wts[:, 0, :], t["WqT"][s]).then_inc(w_in, 16)
                                    sp.dma_start(wts[:, 1, :], t["WkT"][s]).then_inc(w_in, 16)
                                    sp.dma_start(wts[:, 2, :], t["WvT"][s]).then_inc(w_in, 16)
                                    sp.dma_start(cols[:, 0:1], t["bq"][s].rearrange("(p a) -> p a", a=1)).then_inc(w_in, 16)
                                    sp.dma_start(cols[:, 1:2], t["bk"][s].rearrange("(p a) -> p a", a=1)).then_inc(w_in, 16)
                                else:
                                    sp.dma_start(wts[:, :, :], t["bWqkv"].rearrange("p (a n) -> p a n", a=3)).then_inc(w_in, 16)
                                    sp.dma_start(bvb[:], t["zero_row"][0:1, 0:P].to_broadcast([P, P])).then_inc(w_in, 16)
                                sp.dma_start(qs[par][MROW:MROW + CROWS, :, :], t["crow_q" + kind]).then_inc(stack_in, 16)
                                sp.dma_start(ks[par][MROW:MROW + CROWS, :, :], t["crow_k" + kind]).then_inc(stack_in, 16)
                                for a in range(2):
                                    sp.wait_ge(step, k0 + 6 + 5 * a + 1)
                                    sp.dma_start(scratch[a].rearrange("c p n -> p c n"), parts[:, a, :, :]).then_inc(part_out, 16)
                                sp.wait_ge(part_out, 32 * (i + 1))
                                for a, (combo, stack) in enumerate(((COMBO_Q, qs[par]), (COMBO_K, ks[par]))):
                                    for g, c in enumerate(combo):
                                        sp.dma_start(stack[8 * g:8 * g + 8, :, :],
                                                     scratch[a, c].rearrange("(h d) n -> d h n", d=HD)).then_inc(stack_in, 16)
                                sp.wait_ge(stack_in, 16 * 14 * (i + 1))

                            @block.tensor
                            def _(pe):
                                pe.wait_ge(w_in, nw * (i + 1))
                                for a in range(2):
                                    for c in range(2):
                                        last = nc.tensor.matmul(ps[:, 2 * a + c, :], wts[:, a, :],
                                                                xl[:, b * SEQ + c * CH:b * SEQ + (c + 1) * CH],
                                                                start=True, stop=True)
                                last.then_inc(step, 1)

                            @block.vector
                            def _(dve):
                                dve.wait_ge(step, k0 + 1)
                                for a in range(2):
                                    nc.vector.tensor_scalar(qkf[a].rearrange("p (c n) -> p c n", c=2), ps[:, 2 * a:2 * a + 2, :],
                                                            cols[:, a:a + 1], qscale if a == 0 else 1.0,
                                                            ALU.add, ALU.mult)
                                    k1 = k0 + 1 + 5 * a
                                    dve.drain().then_inc(step, 1)
                                    dve.wait_ge(step, k1 + 1)
                                    nc.vector.tensor_copy(parts[:, a, 0, :], qkf[a]).then_inc(step, 1)
                                    dve.wait_ge(step, k1 + 2)
                                    nc.vector.tensor_tensor(rest[a], qkf[a], parts[:, a, 0, :], ALU.subtract).then_inc(step, 1)
                                    dve.wait_ge(step, k1 + 3)
                                    nc.vector.tensor_copy(parts[:, a, 1, :], rest[a]).then_inc(step, 1)
                                    dve.wait_ge(step, k1 + 4)
                                    nc.vector.tensor_tensor(parts[:, a, 2, :], rest[a], parts[:, a, 1, :], ALU.subtract).then_inc(step, 1)
                                    dve.wait_ge(step, k1 + 5)
                                dve.nop().then_inc(step, 1)
                    par1, par2 = i % 2, (i + 1) % 2
                    b2 = before[1] if before else 0
                    with nc.Block() as block:
                        @block.sync
                        def _(sp):
                            pass

                        @block.gpsimd
                        def _(pool):
                            if not before:
                                return
                            u = i - 1
                            with pool.Fori(0, QUADS) as quad:
                                pool.wait_ge(pt_free, NSTEP * (4 * u + quad) + 1 + START)
                                nc.gpsimd.tensor_copy(vq[:, :, :, 0:HD],
                                                      vrow[:, :, bass.ds(quad * 4 * HD, 4 * HD)].rearrange("p t (j d) -> p t j d", d=HD)
                                                      ).then_inc(vq_ready, 1)

                        @block.tensor
                        def _(pe):
                            with pe.Fori(0, QUADS) as quad:
                                n1 = (4 * i + quad) * 4 * QT
                                u = i - 1
                                n2 = (4 * u + quad) * 4 * NSTEP
                                nst = (4 * u + quad) * NSTEP
                                seen1 = seen2 = 0
                                for what, x, y in ORDER:
                                    if what == "first":
                                        if not now:
                                            continue
                                        j, qt = x, y
                                        bank = 2 * (seen1 % 2)
                                        lhs = qs[par1][:, bass.ds(quad * 4 + j, 1), qt * P:(qt + 1) * P]
                                        pe.wait_ge(s1_free, n1 + seen1 + START)
                                        cols_n = P * (qt + 1)
                                        last = None
                                        for h in range(0, cols_n, CH):
                                            w = min(CH, cols_n - h)
                                            diag = h + w == cols_n
                                            last = nc.tensor.matmul(ps[:, bank + h // CH, 0:w], lhs,
                                                                    ks[par1][:, bass.ds(quad * 4 + j, 1), h:h + w],
                                                                    start=True, stop=not diag)
                                        e = cols_n - P
                                        last = nc.tensor.matmul(ps[:, bank + e // CH, e % CH:e % CH + P], identb[:], mask_q[:],
                                                                start=False, stop=True)
                                        last.then_inc(s1_ready, 1)
                                        seen1 += 1
                                    elif not before:
                                        continue
                                    elif what == "second":
                                        c, kt, q0, w = STEPS[x]
                                        j = y
                                        bank = 4 + seen2 % 2
                                        pe.wait_ge(s2_free, n2 + seen2 + START)
                                        diag = q0 == kt * P
                                        last = nc.tensor.matmul(ps[:, bank, 0:w], ks[par2][:, bass.ds(quad * 4 + j, 1), kt * P:(kt + 1) * P],
                                                                qs[par2][:, bass.ds(quad * 4 + j, 1), q0:q0 + w],
                                                                start=True, stop=not diag)
                                        if diag:
                                            last = nc.tensor.matmul(ps[:, bank, 0:P], identb[:], mask_k[:], start=False, stop=True)
                                        last.then_inc(s2_ready, 1)
                                        seen2 += 1
                                    else:
                                        c, kt, q0, w = STEPS[x]
                                        if x == 0:
                                            pe.wait_ge(vq_ready, 4 * u + quad + 2)
                                        if kt == 0:
                                            pe.wait_ge(ot_free, 2 * (4 * u + quad) + c + START)
                                        pe.wait_ge(s2_free, n2 + 4 * x + 5 + START)
                                        for j in range(4):
                                            last = nc.tensor.matmul(ps[32 * j:32 * j + 32, 6 + c, q0 - c * CH:q0 - c * CH + w],
                                                                    vq[:, kt, j, :], pt[:, x % 2, j, 0:w],
                                                                    start=kt == 0, stop=kt == 4 * c + 3)
                                        last.then_inc(pt_free, 1)

                        @block.vector
                        def _(dve):
                            with dve.Fori(0, QUADS) as quad:
                                n1 = (4 * i + quad) * 4 * QT
                                u = i - 1
                                if now:
                                    seen1 = 0
                                    for what, x, y in ORDER:
                                        if what != "first":
                                            continue
                                        j, qt = x, y
                                        bank = 2 * (seen1 % 2)
                                        dve.wait_ge(s1_ready, n1 + seen1 + 1)
                                        flat1 = ps[:, bank:bank + 2, :].rearrange("p a n -> p (a n)")
                                        nc.vector.tensor_reduce(nm[:, bass.ds(quad * 32 + j * QT + qt, 1)], flat1[:, 0:P * (qt + 1)],
                                                                AX.X, ALU.max, negate=True).then_inc(s1_free, 1)
                                        seen1 += 1
                                if before:
                                    dve.wait_ge(pt_free, NSTEP * (4 * u + quad + 1) + 1 + START)
                                    nc.vector.tensor_copy(ot[:, bass.ds(quad, 1), CH:2 * CH], ps[:, 7, :]).then_inc(ot_free, 1)

                        @block.scalar
                        def _(act):
                            if not before:
                                return
                            with act.Fori(0, QUADS) as quad:
                                u = i - 1
                                n2 = (4 * u + quad) * 4 * NSTEP
                                nst = (4 * u + quad) * NSTEP
                                seen2 = 0
                                for x, (c, kt, q0, w) in enumerate(STEPS):
                                    act.wait_ge(pt_free, nst + x + START)
                                    for j in range(4):
                                        act.wait_ge(s2_ready, n2 + seen2 + 1)
                                        nc.scalar.activation(pt[:, x % 2, j, 0:w], ps[:, 4 + seen2 % 2, 0:w], ACT.Exp).then_inc(s2_free, 1)
                                        seen2 += 1
                                    if x == 4:
                                        act.wait_ge(pt_free, nst + 4 + 1 + START)
                                        nc.scalar.activation(ot[:, bass.ds(quad, 1), 0:CH], ps[:, 6, :], ACT.Copy).then_inc(ot_free, 1)

                    if now:
                        k0 = at[0]
                        at[0] += 6
                        s, b = now
                        with nc.Block() as block:
                            @block.tensor
                            def _(pe):
                                nc.tensor.transpose(ps[:, 0, 0:P], nm[:], ident[:]).then_inc(step, 1)

                            @block.vector
                            def _(dve):
                                dve.wait_ge(step, k0 + 1)
                                nc.vector.tensor_copy(mparts[:, 0, :], ps[:, 0, 0:P]).then_inc(step, 1)
                                dve.wait_ge(step, k0 + 2)
                                nc.vector.tensor_tensor(mrest[:], ps[:, 0, 0:P], mparts[:, 0, :], ALU.subtract).then_inc(step, 1)
                                dve.wait_ge(step, k0 + 3)
                                nc.vector.tensor_copy(mparts[:, 1, :], mrest[:]).then_inc(step, 1)
                                dve.wait_ge(step, k0 + 4)
                                nc.vector.tensor_tensor(mparts[:, 2, :], mrest[:], mparts[:, 1, :], ALU.subtract).then_inc(step, 1)
                                dve.wait_ge(step, k0 + 5)
                                dve.nop().then_inc(step, 1)

                            @block.sync
                            def _(sp):
                                sp.wait_ge(step, k0 + 6)
                                for c in range(3):
                                    sp.dma_start(qs[par1][MROW + c:MROW + c + 1, :, :].rearrange("p h (q n) -> p (h q) n", n=P),
                                                 mparts[:, c, :]).then_inc(sem(k + "m_in"), 16)
                                sp.wait_ge(sem(k + "m_in"), 48 * (i + 1))

                    if now:
                        k0 = at[0]
                        at[0] += 2
                        with nc.Block() as block:
                            @block.sync
                            def _(sp):
                                if kind == "a":
                                    sp.dma_start(bvb[:], t["bv"][s:s + 1, :].to_broadcast([P, P])).then_inc(sem(k + "bv_in"), 16)
                                    sp.wait_ge(sem(k + "bv_in"), 16 * (i + 1))

                            @block.tensor
                            def _(pe):
                                for kt in range(QT):
                                    last = nc.tensor.matmul(ps[:, 4 + kt // 4, (kt % 4) * P:(kt % 4 + 1) * P],
                                                            xl[:, b * SEQ + kt * P:b * SEQ + (kt + 1) * P], wts[:, 2, :],
                                                            start=True, stop=True)
                                last.then_inc(step, 1)

                            @block.vector
                            def _(dve):
                                if kind == "a":
                                    dve.wait_ge(sem(k + "bv_in"), 16 * (i + 1))
                                dve.wait_ge(step, k0 + 1)
                                nc.vector.tensor_tensor(vrow[:, :, :].rearrange("p t n -> p t n"),
                                                        ps[:, 4:6, :].rearrange("p a (t n) -> p (a t) n", n=P),
                                                        bvb[:].unsqueeze(1).to_broadcast([P, QT, P]), ALU.add).then_inc(step, 1)

                    if before:
                        s, b = before
                        nwo = 16 * (4 + (4 if kind == "a" else 0))
                        with nc.Block() as block:
                            @block.sync
                            def _(sp):
                                wo = t["WoT"][s] if kind == "a" else t["bWout"]
                                for j in range(4):
                                    sp.dma_start(wop[32 * j:32 * j + HD, :, :],
                                                 wo.rearrange("(q j d) o -> j d q o", j=4, d=HD)[j]).then_inc(sem(k + "wo_in"), 16)
                                if kind == "a":
                                    for n, name in enumerate(("bo", "ln_g", "ln_b")):
                                        sp.dma_start(cols[:, 2 + n:3 + n], t[name][s].rearrange("(p a) -> p a", a=1)).then_inc(sem(k + "wo_in"), 16)
                                    sp.dma_start(wout[:], t["WoutT"][s * P:(s + 1) * P, :]).then_inc(sem(k + "wo_in"), 16)
                                sp.wait_ge(sem(k + "wo_in"), nwo * i)

                        for c in range(2):
                            k0 = at[0]
                            sl = slice(b * SEQ + c * CH, b * SEQ + (c + 1) * CH)
                            ac = acc[:, c * CH:(c + 1) * CH]
                            last_scale = kind == "a" and s == scales - 1
                            kln = k0 + 15
                            with nc.Block() as block:
                                @block.tensor
                                def _(pe):
                                    for q in range(QUADS):
                                        last = nc.tensor.matmul(ps[:, q, :], sel[:], ot[:, q, c * CH:(c + 1) * CH], start=True, stop=True)
                                    last.then_inc(step, 1)
                                    pe.wait_ge(step, k0 + 13)
                                    for q in range(QUADS):
                                        last = nc.tensor.matmul(ps[:, 4, :], wop[:, q, :], on[:, q, :], start=q == 0, stop=q == QUADS - 1)
                                    last.then_inc(step, 1)
                                    if kind == "a":
                                        ln_pe(pe, kln, yo[:])
                                        pe.wait_ge(step, kln + LN)
                                        nc.tensor.matmul(ps[:, 5, :], wout[:], yo[:], start=True, stop=True).then_inc(step, 1)
                                    if last_scale:
                                        ln_pe(pe, kln + LN + 3, yo[:])

                                @block.scalar
                                def _(act):
                                    if kind == "a":
                                        ln_act(act, kln)
                                    if last_scale:
                                        ln_act(act, kln + LN + 3)

                                @block.vector
                                def _(dve):
                                    dve.wait_ge(step, k0 + 1)
                                    for q in range(QUADS):
                                        nc.vector.tensor_scalar(lnq[:], ps[:, q, :], den_eps, None, ALU.add).then_inc(step, 1)
                                        dve.wait_ge(step, k0 + 3 * q + 2)
                                        nc.vector.reciprocal(rden[:], lnq[:]).then_inc(step, 1)
                                        dve.wait_ge(step, k0 + 3 * q + 3)
                                        nc.vector.tensor_tensor(on[:, q, :], ot[:, q, c * CH:(c + 1) * CH], rden[:], ALU.mult).then_inc(step, 1)
                                        dve.wait_ge(step, k0 + 3 * q + 4)
                                    dve.wait_ge(step, k0 + 14)
                                    if kind == "b":
                                        nc.vector.tensor_tensor(res[:, sl], res[:, sl], ps[:, 4, :], ALU.add).then_inc(step, 1)
                                        return
                                    nc.vector.tensor_scalar(yo[:], ps[:, 4, :], cols[:, 2:3], None, ALU.add).then_inc(step, 1)
                                    ln_dve(dve, kln, yo[:], yo[:], cols[:, 3:4], cols[:, 4:5])
                                    dve.wait_ge(step, kln + LN + 1)
                                    if s == 0:
                                        nc.vector.tensor_copy(ac, ps[:, 5, :]).then_inc(step, 1)
                                    else:
                                        nc.vector.tensor_tensor(ac, ps[:, 5, :], ac, ALU.add).then_inc(step, 1)
                                    if last_scale:
                                        dve.wait_ge(step, kln + LN + 2)
                                        nc.vector.tensor_scalar(yo[:], ac, cols2[:, 0:1], None, ALU.add).then_inc(step, 1)
                                        ln_dve(dve, kln + LN + 3, yo[:], yo[:], cols2[:, 1:2], cols2[:, 2:3])
                                        dve.wait_ge(step, kln + 2 * LN + 3)
                                        nc.vector.tensor_tensor(res[:, sl], res[:, sl], yo[:], ALU.add).then_inc(step, 1)
                            at[0] += 15
                            if kind == "a":
                                at[0] += LN + 2
                            if last_scale:
                                at[0] += LN + 2

        def ident_b():
            return identb[:]

        def layers(call):
            with ExitStack() as local:
                def lb(name, shape, dt=F32):
                    return sb(f"l{call}_{name}", shape, dt, local)

                xa = lb("xa", [P, BATCH, XW_COLS])
                xb = lb("xb", [P, BATCH, XW_COLS])
                xs = lb("xs", [P, XW_COLS])
                wqk = lb("wqk", [P, 2 * INNER])
                wvt = lb("wvt", [P, LH // 2, P])
                wo = lb("wo", [P, LH // 2, P])
                mh = lb("mh", [P, LH, P])
                w1 = lb("w1", [P, 2 * HID])
                w2 = lb("w2", [P, 3, P])
                b1 = lb("b1", [P, 2, 3])
                gcols = lb("gcols", [P, 3])
                base = lb("base", [P, 4, QT, LD])
                tab = lb("tab", [P, 4, QT, LD])
                sc = lb("sc", [P, 2, LD])
                lmask = lb("lmask", [P, QT, 2 * WIN], BF16)
                sq = lb("sq", [P, 2, INNER])
                rc = lb("rc", [P, 2, INNER])
                rs = lb("rs", [P, 2, INNER])
                qkn = rs
                ss = lb("ss", [P, 2, LH])
                rn = lb("rn", [P, 2, LH])
                qt_ = lb("qt", [P, LH // 2, P])
                kt_ = lb("kt", [P, LH // 2, WIN + SEQ])
                mx = lb("mx", [P, LH])
                pd = lb("pd", [P, LH, 2 * WIN])
                pe_ = lb("pe", [P, LH, 2 * WIN])
                pn = pd
                rl = lb("rl", [P, LH])
                lsum = lb("lsum", [P, LH])
                ptl = lb("ptl", [P, LH // 2, P])
                xw = lb("xw", [P, 4, 2, P])
                yb = lb("yb", [P, LH, CH])
                xn = lb("xn", [P, CH])
                gl = lb("gl", [P, 3, CH])
                hh = gl

                c = f"l{call}"
                lin = sem(c + "in")
                a_in, m_in = sem(c + "attn_w_in"), sem(c + "mlp_w_in")
                k0 = at[0]
                at[0] += 4 * LN

                def load_attn(sp, L):
                    sp.dma_start(wqk[:], t["lWqkv"][bass.ds(L, 1), :, 0:2 * INNER]).then_inc(a_in, 16)
                    sp.dma_start(wvt[:, :, :], t["lWvT"][bass.ds(L, 1)]).then_inc(a_in, 16)
                    sp.dma_start(wo[:, :, :], t["lWo"][bass.ds(L, 1)].rearrange("a (g p) o -> p (a g) o", p=P)).then_inc(a_in, 16)
                    sp.dma_start(sc[:, 0, :], t["q_scale"][bass.ds(L, 1), :].to_broadcast([P, LD])).then_inc(a_in, 16)
                    sp.dma_start(sc[:, 1, :], t["k_scale"][bass.ds(L, 1), :].to_broadcast([P, LD])).then_inc(a_in, 16)

                A_IN = 80

                def load_mlp(sp, L):
                    sp.dma_start(w1[:], t["lW1"][bass.ds(L, 1)]).then_inc(m_in, 16)
                    sp.dma_start(w2[:, 0:2, :], t["lW2"][bass.ds(L, 1), 0:2 * P, :].rearrange("a (g p) o -> p (a g) o", p=P)).then_inc(m_in, 16)
                    sp.dma_start(w2[0:85, 2, :], t["lW2"][bass.ds(L, 1), 2 * P:HID, :].rearrange("a p o -> p (a o)")).then_inc(m_in, 16)
                    for half in range(2):
                        for n, (h0, w) in enumerate(HCH):
                            sp.dma_start(b1[0:w, half, n:n + 1], t["lb1"][bass.ds(L, 1), half * HID + h0:half * HID + h0 + w].rearrange("a (p n) -> p (a n)", n=1)).then_inc(m_in, 16)
                    for n, name in enumerate(("lg", "lb", "lb2")):
                        sp.dma_start(gcols[:, n:n + 1], t[name][bass.ds(L, 1)].rearrange("a (p n) -> p (a n)", n=1)).then_inc(m_in, 16)

                M_IN = 12 * 16

                with nc.Block() as block:
                    @block.sync
                    def _(sp):
                        sp.dma_start(base[:, :, :, :], t["rot"]).then_inc(lin, 16)
                        sp.dma_start(lmask[:, :, :], t["lmask"]).then_inc(lin, 16)
                        load_attn(sp, 0)
                        sp.wait_ge(lin, 32)
                        sp.wait_ge(a_in, A_IN)

                    @block.vector
                    def _(dve):
                        nc.vector.memset(xa[:, :, :], 0.0)
                        nc.vector.memset(xb[:, :, :], 0.0)
                        nc.vector.memset(kt_[:, :, 0:WIN], 0.0)
                        nc.vector.memset(xw[:, :, :, :], 0.0)

                with nc.Block() as block:
                    @block.tensor
                    def _(pe):
                        for n in range(4):
                            ln_pe(pe, k0 + LN * n, res[:, n * CH:(n + 1) * CH])

                    @block.scalar
                    def _(act):
                        for n in range(4):
                            ln_act(act, k0 + LN * n)

                    @block.vector
                    def _(dve):
                        for n in range(4):
                            ln_dve(dve, k0 + LN * n, res[:, n * CH:(n + 1) * CH], xn[:])
                            o = WIN + (n % 2) * CH
                            nc.vector.tensor_copy(xa[0:64, n // 2, o:o + CH], xn[0:64, :])
                            nc.vector.tensor_copy(xa[64:P, n // 2, o + 1:o + 1 + CH], xn[64:P, :])
                            dve.drain()

                w_done = sem(c + "w_done")
                chain = sem(c + "mlp_step")
                S = {n: sem(c + n) for n in (
                    "qk_ready", "sq_done", "qk_read", "ss_done", "sd_done", "rn_done", "cos_sin_done", "rot_done", "unit_done",
                    "tr_ready", "tr_read", "s_ready", "mx_done", "s_read", "exp_done", "sum_done", "rl_done", "p_done",
                    "xw_ready", "xw_done", "y_ready", "y_read_a", "y_read_v", "g_ready", "g_read", "rmax_done", "xs_done")}

                with nc.Block() as block:
                    @block.gpsimd
                    def _(pool):
                        for one in (*S.values(), chain):
                            pool.sem_inc(one, START)

                with nc.Fori(0, DEPTH) as L:
                    with nc.Block() as block:
                        @block.sync
                        def _(sp):
                            load_mlp(sp, L)

                        @block.tensor
                        def _(pe):
                            pe.wait_ge(a_in, A_IN * (L + 1))
                            for h in range(LH):
                                e = 64 * (h % 2)
                                last = nc.tensor.matmul(ps[:, h // 4 * 2 + h % 2, (h % 4) // 2 * P:(h % 4) // 2 * P + P],
                                                        wvt[e:e + 64, h // 2, :], wo[e:e + 64, h // 2, :], start=True, stop=True)
                            last.then_inc(w_done, 1)

                        @block.scalar
                        def _(act):
                            act.wait_ge(w_done, L + 1)
                            for g in range(4):
                                nc.scalar.activation(mh[:, 4 * g:4 * g + 4, :].rearrange("p (r e) n -> p e r n", e=2),
                                                     ps[:, 2 * g:2 * g + 2, 0:2 * P].rearrange("p e (r n) -> p e r n", n=P), ACT.Copy)

                        @block.vector
                        def _(dve):
                            dve.wait_ge(a_in, A_IN * (L + 1))
                            for a in range(2):
                                full = sc[:, a, :].unsqueeze(1).to_broadcast([P, QT, LD])
                                nc.vector.tensor_tensor(tab[:, 2 * a, :, :], base[:, 2 * a, :, :], full, ALU.mult)
                                for lo, hi in ((0, 32), (32, 0)):
                                    part = sc[:, a, hi:hi + 32].unsqueeze(1).to_broadcast([P, QT, 32])
                                    nc.vector.tensor_tensor(tab[:, 2 * a + 1, :, lo:lo + 32], base[:, 2 * a + 1, :, lo:lo + 32], part, ALU.mult)

                    with nc.Fori(0, BATCH) as b:
                        with nc.Block() as block:
                            @block.vector
                            def _(dve):
                                nc.vector.tensor_copy(xs[:], xa[:, bass.ds(b, 1), :])
                        with nc.Block() as block:
                            n0 = (L * BATCH + b) * QT

                            @block.sync
                            def _(sp):
                                pass

                            @block.tensor
                            def _(pe):
                                def product(i, a):
                                    pe.wait_ge(S["qk_read"], 2 * (n0 + i) + a + START)
                                    for x in range(2):
                                        last = nc.tensor.matmul(ps[:, x, :], xs[:, WIN + i * P:WIN + (i + 1) * P],
                                                                wqk[:, a * INNER + x * CH:a * INNER + (x + 1) * CH], start=True, stop=True)
                                    last.then_inc(S["qk_ready"], 1)

                                def transposes(src, waits):
                                    for x in range(8):
                                        last = nc.tensor.transpose(ps[:, 2 + x // 4, (x % 4) * P:(x % 4 + 1) * P],
                                                                   src[:, x * P:(x + 1) * P], ident[:])
                                    last.then_inc(S["tr_ready"], 1)

                                product(0, 0)
                                product(0, 1)
                                for i in range(QT):
                                    n = n0 + i
                                    pe.wait_ge(S["unit_done"], 2 * n + 1 + START)
                                    pe.wait_ge(S["tr_read"], 3 * n + START)
                                    pe.wait_ge(S["g_read"], L * 4 + b * 2 + i // 4 + START)
                                    transposes(qkn[:, 0, :], None)
                                    if i + 1 < QT:
                                        product(i + 1, 0)
                                    pe.wait_ge(S["unit_done"], 2 * n + 2 + START)
                                    pe.wait_ge(S["tr_read"], 3 * n + 1 + START)
                                    transposes(qkn[:, 1, :], None)
                                    if i + 1 < QT:
                                        product(i + 1, 1)
                                    pe.wait_ge(S["s_read"], n + START)
                                    pe.wait_ge(S["tr_read"], 3 * n + 2 + START)
                                    for x in range(2):
                                        nc.tensor.matmul(ps[:, 4 + x, :], identb[:],
                                                         lmask[:, i, :].unsqueeze(1).to_broadcast([P, 8, 2 * WIN]),
                                                         start=True, stop=False, skip_group_check=True)
                                    for h in range(LH):
                                        e = 64 * (h % 2)
                                        for w in range(4):
                                            last = nc.tensor.matmul(
                                                ps[32 * w:32 * w + 32, 4 + h % 2, (h // 2) * 64:(h // 2 + 1) * 64],
                                                qt_[e:e + 64, h // 2, 32 * w:32 * w + 32],
                                                kt_[e:e + 64, h // 2, i * P + 32 * w:i * P + 32 * w + 64],
                                                start=False, stop=True, skip_group_check=True)
                                    last.then_inc(S["s_ready"], 1)
                                    pe.wait_ge(S["y_read_a"], 2 * n + START)
                                    for w in range(2):
                                        o = i * P + 32 * w
                                        last = nc.tensor.transpose(ps[:, 6, w * P:(w + 1) * P], xs[:, o:o + P], ident[:])
                                    last.then_inc(S["xw_ready"], 1)
                                    pe.wait_ge(S["p_done"], n + 1 + START)
                                    transposes(pn[:, :, :].rearrange("p h j -> p (h j)"), None)
                                    pe.wait_ge(S["xw_done"], n + 1 + START)
                                    pe.wait_ge(S["tr_read"], 3 * n + 3 + START)
                                    for half in range(2):
                                        pe.wait_ge(S["y_read_v"], 2 * n + half + START)
                                        pe.wait_ge(S["y_read_a"], 2 * n + half + START)
                                        for w in range(2):
                                            for e in range(2):
                                                ww = 2 * half + w
                                                last = nc.tensor.matmul(ps[:, 6 + e, w * 256:(w + 1) * 256], xw[:, ww, e, :],
                                                                        ptl[:, :, 32 * ww:32 * ww + 32], start=True, stop=True)
                                        last.then_inc(S["y_ready"], 1)
                                    if i % 4 == 3:
                                        pe.wait_ge(S["y_read_v"], 2 * n + 2 + START)
                                        pe.wait_ge(S["y_read_a"], 2 * n + 2 + START)
                                        for h in range(LH):
                                            last = nc.tensor.matmul(ps[:, 2, :], mh[:, h, :], yb[:, h, :], start=h == 0, stop=h == LH - 1)
                                        last.then_inc(S["g_ready"], 1)

                            @block.scalar
                            def _(act):
                                def squares(i, a):
                                    act.wait_ge(S["qk_ready"], 2 * (n0 + i) + a + 1 + START)
                                    act.wait_ge(S["ss_done"], 2 * (n0 + i) + START)
                                    nc.scalar.activation(sq[:, a, :].rearrange("p (x n) -> p x n", x=2), ps[:, 0:2, :], ACT.Square).then_inc(S["sq_done"], 1)

                                def norms(i):
                                    act.wait_ge(S["ss_done"], 2 * (n0 + i) + 2 + START)
                                    act.wait_ge(S["rn_done"], n0 + i + START)
                                    nc.scalar.activation(ss[:, :, :], ss[:, :, :], ACT.Sqrt).then_inc(S["sd_done"], 1)

                                squares(0, 0)
                                squares(0, 1)
                                norms(0)
                                for i in range(QT):
                                    n = n0 + i
                                    act.wait_ge(S["tr_ready"], 3 * n + 1 + START)
                                    act.wait_ge(S["s_ready"], n + START)
                                    nc.scalar.activation(qt_[:, :, :].rearrange("p (x g) n -> p x (g n)", x=2), ps[:, 2:4, :], ACT.Copy).then_inc(S["tr_read"], 1)
                                    if i + 1 < QT:
                                        squares(i + 1, 0)
                                    act.wait_ge(S["tr_ready"], 3 * n + 2 + START)
                                    for x in range(2):
                                        ins = nc.scalar.activation(kt_[:, 4 * x:4 * x + 4, WIN + i * P:WIN + (i + 1) * P],
                                                                   ps[:, 2 + x, :].rearrange("p (g n) -> p g n", n=P), ACT.Copy)
                                    ins.then_inc(S["tr_read"], 1)
                                    if i + 1 < QT:
                                        squares(i + 1, 1)
                                        norms(i + 1)
                                    act.wait_ge(S["xw_ready"], n + 1 + START)
                                    act.wait_ge(S["y_ready"], 2 * n + START)
                                    for r in range(2):
                                        src = ps[64 * r:64 * r + 64, 6, 0:2 * P].rearrange("p (w n) -> p w n", n=P)
                                        for e in range(2):
                                            ins = nc.scalar.activation(xw[64 * e:64 * e + 64, 2 * r:2 * r + 2, e, :], src, ACT.Copy)
                                    ins.then_inc(S["xw_done"], 1)
                                    act.wait_ge(S["s_read"], n + 1 + START)
                                    nc.scalar.activation(pe_[:, :, :], pd[:, :, :], ACT.Exp, scale=8.0).then_inc(S["exp_done"], 1)
                                    act.wait_ge(S["tr_ready"], 3 * n + 3 + START)
                                    nc.scalar.activation(ptl[:, :, :].rearrange("p (x g) n -> p x (g n)", x=2), ps[:, 2:4, :], ACT.Copy).then_inc(S["tr_read"], 1)
                                    for half in range(2):
                                        act.wait_ge(S["y_ready"], 2 * n + half + 1 + START)
                                        act.wait_ge(S["g_ready"], L * 4 + b * 2 + i // 4 + START)
                                        o = (i % 4) * P + half * 64
                                        for w in range(2):
                                            ins = nc.scalar.activation(
                                                yb[:, :, o + 32 * w:o + 32 * w + 32].rearrange("p (g e) n -> p e g n", e=2)[:, 0],
                                                ps[:, 6, w * 256:(w + 1) * 256].rearrange("p (g n) -> p g n", n=WIN), ACT.Copy)
                                        ins.then_inc(S["y_read_a"], 1)

                            @block.gpsimd
                            def _(pool):
                                for i in range(QT):
                                    for a in range(2):
                                        m = 2 * (n0 + i) + a
                                        pool.wait_ge(S["cos_sin_done"], m + 1 + START)
                                        nc.gpsimd.tensor_tensor(rc[:, a, :], rc[:, a, :], rs[:, a, :], ALU.add).then_inc(S["rot_done"], 1)
                                        pool.wait_ge(S["rot_done"], m + 1 + START)
                                        pool.wait_ge(S["rn_done"], n0 + i + 1 + START)
                                        nc.gpsimd.tensor_tensor(qkn[:, a, :].rearrange("p (h d) -> p h d", d=LD),
                                                                rc[:, a, :].rearrange("p (h d) -> p h d", d=LD),
                                                                rn[:, a, :].unsqueeze(2).to_broadcast([P, LH, LD]), ALU.mult).then_inc(S["unit_done"], 1)

                            @block.vector
                            def _(dve):
                                def rotate(i, a):
                                    m = 2 * (n0 + i) + a
                                    dve.wait_ge(S["sq_done"], m + 1 + START)
                                    dve.wait_ge(S["tr_ready"], (3 * (n0 + i) - (2 - a) if i else 3 * n0) + START)
                                    src = ps[:, 0:2, :].rearrange("p x (h d) -> p (x h) d", d=LD)
                                    dst = rc[:, a, :].rearrange("p (h d) -> p h d", d=LD)
                                    dsin = rs[:, a, :].rearrange("p (h d) -> p h d", d=LD)
                                    nc.vector.tensor_tensor(dst, src, tab[:, 2 * a, i, :].unsqueeze(1).to_broadcast([P, LH, LD]), ALU.mult)
                                    for lo, hi in ((0, 32), (32, 0)):
                                        ins = nc.vector.tensor_tensor(dsin[:, :, lo:lo + 32], src[:, :, hi:hi + 32],
                                                                      tab[:, 2 * a + 1, i, lo:lo + 32].unsqueeze(1).to_broadcast([P, LH, 32]), ALU.mult)
                                    ins.then_inc(S["qk_read"], 1)
                                    dve.wait_ge(S["qk_read"], m + 1 + START)
                                    nc.vector.tensor_reduce(ss[:, a, :], sq[:, a, :].rearrange("p (h d) -> p h d", d=LD), AX.X, ALU.add).then_inc(S["ss_done"], 1)
                                    dve.sem_inc(S["cos_sin_done"], 1)

                                def norms(i):
                                    dve.wait_ge(S["sd_done"], n0 + i + 1 + START)
                                    dve.wait_ge(S["unit_done"], 2 * (n0 + i) + START)
                                    nc.vector.tensor_scalar(rn[:, :, :], ss[:, :, :], 1e-12, None, ALU.max).then_inc(S["rmax_done"], 1)
                                    dve.wait_ge(S["rmax_done"], n0 + i + 1 + START)
                                    nc.vector.reciprocal(rn[:, :, :], rn[:, :, :]).then_inc(S["rn_done"], 1)

                                rotate(0, 0)
                                rotate(0, 1)
                                norms(0)
                                for i in range(QT):
                                    n = n0 + i
                                    if i + 1 < QT:
                                        rotate(i + 1, 0)
                                        rotate(i + 1, 1)
                                        norms(i + 1)
                                    dve.wait_ge(S["s_ready"], n + 1 + START)
                                    sc_ps = ps[:, 4:6, :].rearrange("p e (g j) -> p e g j", j=2 * WIN)
                                    mxv = mx[:].rearrange("p (e g) -> p e g", e=2)
                                    nc.vector.tensor_reduce(mxv, sc_ps, AX.X, ALU.max).then_inc(S["mx_done"], 1)
                                    dve.wait_ge(S["mx_done"], n + 1 + START)
                                    dve.wait_ge(S["tr_ready"], 3 * n + START)
                                    nc.vector.tensor_tensor(pd[:, :, :].rearrange("p (g e) j -> p e g j", e=2), sc_ps,
                                                            mxv.unsqueeze(3).to_broadcast([P, 2, LH // 2, 2 * WIN]), ALU.subtract).then_inc(S["s_read"], 1)
                                    dve.wait_ge(S["exp_done"], n + 1 + START)
                                    nc.vector.tensor_reduce(lsum[:], pe_[:, :, :], AX.X, ALU.add).then_inc(S["sum_done"], 1)
                                    dve.wait_ge(S["sum_done"], n + 1 + START)
                                    nc.vector.reciprocal(rl[:], lsum[:]).then_inc(S["rl_done"], 1)
                                    dve.wait_ge(S["rl_done"], n + 1 + START)
                                    nc.vector.tensor_tensor(pn[:, :, :], pe_[:, :, :], rl[:].unsqueeze(2).to_broadcast([P, LH, 2 * WIN]), ALU.mult).then_inc(S["p_done"], 1)
                                    for half in range(2):
                                        dve.wait_ge(S["y_ready"], 2 * n + half + 1 + START)
                                        dve.wait_ge(S["g_ready"], L * 4 + b * 2 + i // 4 + START)
                                        o = (i % 4) * P + half * 64
                                        for w in range(2):
                                            ins = nc.vector.tensor_copy(
                                                yb[:, :, o + 32 * w:o + 32 * w + 32].rearrange("p (g e) n -> p e g n", e=2)[:, 1],
                                                ps[:, 7, w * 256:(w + 1) * 256].rearrange("p (g n) -> p g n", n=WIN))
                                        ins.then_inc(S["y_read_v"], 1)
                                    if i % 4 == 3:
                                        dve.wait_ge(S["g_ready"], L * 4 + b * 2 + i // 4 + 1 + START)
                                        o = WIN + (i // 4) * CH
                                        nc.vector.tensor_tensor(xb[0:64, bass.ds(b, 1), o:o + CH], ps[0:64, 2, :], xs[0:64, o:o + CH], ALU.add)
                                        nc.vector.tensor_tensor(xb[64:P, bass.ds(b, 1), o + 1:o + 1 + CH], ps[64:P, 2, :], xs[64:P, o + 1:o + 1 + CH], ALU.add).then_inc(S["g_read"], 1)

                    with nc.Block() as block:
                        @block.sync
                        def _(sp):
                            load_attn(sp, L + 1)

                    MS = 16
                    with nc.Fori(0, BATCH) as b:
                        with nc.Block() as block:
                            def places(cc):
                                o = WIN + cc * CH
                                return xb[:, bass.ds(b, 1), o:o + CH], o

                            @block.tensor
                            def _(pe):
                                pe.wait_ge(m_in, M_IN * (L + 1))
                                for cc in range(2):
                                    m = (L * 4 + b * 2 + cc) * MS
                                    view, o = places(cc)
                                    pe.wait_ge(chain, m + START)
                                    nc.tensor.matmul(ps[:, 0, :], mean_w[:], view, start=True, stop=True).then_inc(chain, 1)
                                    pe.wait_ge(chain, m + 3 + START)
                                    nc.tensor.matmul(ps[:, 1, :], mean_w[:], lnq[:], start=True, stop=True).then_inc(chain, 1)
                                    pe.wait_ge(chain, m + 8 + START)
                                    for half in (1, 0):
                                        for g, (h0, w) in enumerate(HCH):
                                            last = nc.tensor.matmul(ps[0:w, 2 + 3 * half + g, :], w1[:, half * HID + h0:half * HID + h0 + w], xn[:], start=True, stop=True)
                                    last.then_inc(chain, 1)
                                    pe.wait_ge(chain, m + 15 + START)
                                    for g, (h0, w) in enumerate(HCH):
                                        last = nc.tensor.matmul(ps[:, 0, :], w2[0:w, g, :], hh[0:w, g, :], start=g == 0, stop=g == 2)
                                    last.then_inc(sem(c + "w2_done"), 1)

                            @block.scalar
                            def _(act):
                                act.wait_ge(m_in, M_IN * (L + 1))
                                for cc in range(2):
                                    m = (L * 4 + b * 2 + cc) * MS
                                    act.wait_ge(chain, m + 2 + START)
                                    nc.scalar.activation(lnq[:], lnc[:], ACT.Square).then_inc(chain, 1)
                                    act.wait_ge(chain, m + 4 + START)
                                    nc.scalar.activation(lnq[:], ps[:, 1, :], ACT.Sqrt, bias=eps_col[:, 0:1]).then_inc(chain, 1)
                                    act.wait_ge(chain, m + 9 + START)
                                    for g, (h0, w) in enumerate(HCH):
                                        nc.scalar.activation(gl[0:w, g, :], ps[0:w, 5 + g, :], ACT.Gelu, bias=b1[0:w, 1, g:g + 1]).then_inc(chain, 1)

                            @block.vector
                            def _(dve):
                                dve.wait_ge(m_in, M_IN * (L + 1))
                                for cc in range(2):
                                    m = (L * 4 + b * 2 + cc) * MS
                                    view, o = places(cc)
                                    dve.wait_ge(chain, m + 1 + START)
                                    nc.vector.tensor_tensor(lnc[:], view, ps[:, 0, :], ALU.subtract).then_inc(chain, 1)
                                    dve.wait_ge(chain, m + 5 + START)
                                    nc.vector.reciprocal(lnr[:], lnq[:]).then_inc(chain, 1)
                                    dve.wait_ge(chain, m + 6 + START)
                                    nc.vector.tensor_tensor(lnc[:], lnc[:], lnr[:], ALU.mult).then_inc(chain, 1)
                                    dve.wait_ge(chain, m + 7 + START)
                                    nc.vector.tensor_scalar(xn[:], lnc[:], gcols[:, 0:1], gcols[:, 1:2], ALU.mult, ALU.add).then_inc(chain, 1)
                                    dve.wait_ge(chain, m + 12 + START)
                                    for g, (h0, w) in enumerate(HCH):
                                        nc.vector.scalar_tensor_tensor(hh[0:w, g, :], ps[0:w, 2 + g, :], b1[0:w, 0, g:g + 1], gl[0:w, g, :], ALU.add, ALU.mult).then_inc(chain, 1)
                                    dve.wait_ge(sem(c + "w2_done"), L * 4 + b * 2 + cc + 1)
                                    nc.vector.scalar_tensor_tensor(xa[0:64, bass.ds(b, 1), o:o + CH], ps[0:64, 0, :], gcols[0:64, 2:3], xb[0:64, bass.ds(b, 1), o:o + CH], ALU.add, ALU.add)
                                    nc.vector.scalar_tensor_tensor(xa[64:P, bass.ds(b, 1), o + 1:o + 1 + CH], ps[64:P, 0, :], gcols[64:P, 2:3], xb[64:P, bass.ds(b, 1), o + 1:o + 1 + CH], ALU.add, ALU.add).then_inc(chain, 1)

                with nc.Block() as block:
                    @block.sync
                    def _(sp):
                        sp.wait_ge(a_in, A_IN * (DEPTH + 1))

                    @block.vector
                    def _(dve):
                        r = res[:, :].rearrange("p (b n) -> p b n", b=BATCH)
                        nc.vector.tensor_tensor(r[0:64], r[0:64], xa[0:64, :, WIN:WIN + SEQ], ALU.add)
                        nc.vector.tensor_tensor(r[64:P], r[64:P], xa[64:P, :, WIN + 1:WIN + 1 + SEQ], ALU.add)

        for stage, which in PLAN:
            (causal if stage == "causal" else layers)(which)

        with nc.Block() as block:
            @block.sync
            def _(sp):
                sp.dma_start(out, res[:]).then_inc(out_done, 16)
                sp.wait_ge(out_done, 16)


def constants():
    f = np.float32

    def bf(a):
        u = np.asarray(a, f).view(np.uint32)
        return ((u + 0x7FFF + ((u >> 16) & 1)) >> 16).astype(np.uint16)

    def parts(a):
        a = np.asarray(a, f)
        out = []
        for _ in range(3):
            out.append((bf(a).astype(np.uint32) << 16).view(f))
            a = a - out[-1]
        return out

    n = np.arange(P)
    mask_q = bf(np.where(n[None, :] > n[:, None], NEG, 0.0))
    sel = np.zeros((P, P), f)
    for j in range(4):
        sel[32 * j + HD, 32 * j:32 * j + 32] = 1.0
    crow = {}
    pos = np.arange(SEQ)
    hi = pos // 32 * 32
    for kind in "ab":
        q = np.zeros((CROWS, HEADS, SEQ), f)
        k = np.zeros((CROWS, HEADS, SEQ), f)
        k[0:3] = 1.0
        if kind == "b":
            start = 2.0 ** (-(8.0 / HEADS))
            slopes = np.asarray([start * start ** i for i in range(HEADS)], f)
            for i, part in enumerate(parts(slopes)):
                q[3 + 2 * i] = q[4 + 2 * i] = part[:, None]
                k[3 + 2 * i] = hi
                k[4 + 2 * i] = pos - hi
        crow["crow_q" + kind], crow["crow_k" + kind] = bf(q), bf(k)
    half = np.arange(0, LD, 2, dtype=f)
    freqs = np.arange(SEQ, dtype=f)[:, None] * (f(1.0) / f(10000.0) ** (half / f(LD)))[None, :]
    freqs = np.concatenate([freqs, freqs], -1)
    base_scale = (half + f(0.4 * LD)) / f(1.4 * LD)
    power = (np.arange(SEQ, dtype=f) - SEQ // 2) / f(WIN // 2)
    scale = base_scale[None, :] ** power[:, None]
    scale = np.concatenate([scale, scale], -1)
    sign = np.concatenate([-np.ones(LD // 2, f), np.ones(LD // 2, f)])
    cos, sin = np.cos(freqs), np.sin(freqs) * sign
    rot = np.stack([cos * scale, sin * scale, cos / scale, sin / scale]).astype(f)
    rot = np.ascontiguousarray(rot.reshape(4, QT, P, LD).transpose(2, 0, 1, 3))
    i = n % WIN
    j = np.arange(2 * WIN)
    ok = (j[None, :] >= i[:, None]) & (j[None, :] <= i[:, None] + WIN)
    lmask = np.repeat(np.where(ok, 0.0, NEG)[:, None, :], QT, 1)
    lmask[:WIN, 0, :WIN] = NEG
    return {"ident": np.eye(P, dtype=f), "identb": bf(np.eye(P)), "mask_q": mask_q,
            "mask_k": np.ascontiguousarray(mask_q.T), "sel": sel, "rot": rot, "lmask": bf(lmask),
            "zero_row": np.zeros((1, P), f), **crow}


BF16_CONSTANTS = ("identb", "mask_q", "mask_k", "lmask", "crow_qa", "crow_ka", "crow_qb", "crow_kb")


def arrays(inputs):
    g = {k.replace("L0_", ""): np.asarray(v) for k, v in inputs.items()}

    def tr(a):
        return np.ascontiguousarray(np.swapaxes(a, -1, -2))

    def wrap(a):
        return np.concatenate([a, a[:1]])

    wv = g["ffn_Wqkv"][:, :, 2 * INNER:]
    wvt = np.ascontiguousarray(wv.reshape(DEPTH, P, LH // 2, P).transpose(0, 3, 2, 1))
    d = {"x": tr(g["attn_a_x"].reshape(TOK, P)),
         "WqT": tr(g["attn_a_Wq"]), "WkT": tr(g["attn_a_Wk"]), "WvT": tr(g["attn_a_Wv"]), "WoT": tr(g["attn_a_Wo"]),
         "bq": g["attn_a_bq"], "bk": g["attn_a_bk"], "bv": g["attn_a_bv"], "bo": g["attn_a_bo"],
         "ln_g": g["attn_a_ln_g"], "ln_b": g["attn_a_ln_b"], "WoutT": tr(g["attn_a_Wout"]),
         "bout": g["attn_a_bout"], "ln2_g": g["attn_a_ln2_g"], "ln2_b": g["attn_a_ln2_b"],
         "bWqkv": g["attn_b_Wqkv"], "bWout": g["attn_b_Wout"],
         "lWqkv": wrap(g["ffn_Wqkv"]), "lWvT": wrap(wvt), "lWo": wrap(g["ffn_Wo"]),
         "q_scale": wrap(g["ffn_q_scale"]), "k_scale": wrap(g["ffn_k_scale"]),
         "lg": g["ffn_ln_g"], "lb": g["ffn_ln_b"], "lW1": g["ffn_W1"], "lb1": g["ffn_b1"],
         "lW2": g["ffn_W2"], "lb2": g["ffn_b2"]}
    return {**d, **constants()}


def kernel(**inputs):
    import concourse.bacc as bacc
    from concourse.bass_utils import run_bass_kernel_spmd

    nc = bacc.Bacc("TRN2", target_bir_lowering=False, num_devices=1)
    data = {"in_" + k: np.ascontiguousarray(v) for k, v in arrays(inputs).items()}
    t = {k[3:]: nc.dram_tensor(k, v.shape, mybir.dt.from_np(v.dtype), kind="ExternalInput").ap() for k, v in data.items()}
    out = nc.dram_tensor("out", (P, TOK), F32, kind="ExternalOutput").ap()
    scratch = nc.dram_tensor("scratch", (2, 3, P, SEQ), BF16, kind="Internal").ap()
    t = {k: ap.bitcast(BF16) if k in BF16_CONSTANTS else ap for k, ap in t.items()}
    build(nc, t, out, scratch)
    r = run_bass_kernel_spmd(nc, [data], core_ids=[0])
    y = r.results[0]["out"]
    return np.ascontiguousarray(y.T).reshape(BATCH, SEQ, P)
```

```python
from contextlib import ExitStack

import numpy as np

import concourse.bass as bass
from concourse import mybir

F32 = mybir.dt.float32
BF16 = mybir.dt.bfloat16
ALU = mybir.AluOpType
ACT = mybir.ActivationFunctionType
AX = mybir.AxisListType

P = 128
BATCH, SEQ = 2, 1024
TOK = BATCH * SEQ
HEADS, HD = 16, 8
QT = SEQ // P
QUADS = HEADS // 4
SCALES = 3
DEPTH = 6
TILES = BATCH * QT
LH, LD = 16, 64
INNER = LH * LD
WIN = 32
HID = 341
HCH = [(0, 128), (128, 128), (256, 85)]
XW_COLS = WIN + 1 + SEQ
LN_EPS = 1e-5
CH = 512
NEG = -1e30
START = 1

COMBO_Q = [0, 0, 0, 1, 1, 2]
COMBO_K = [0, 1, 2, 0, 1, 0]
MROW = 8 * len(COMBO_Q)
AROW = MROW + 3
CROWS = 9

STEPS = [(c, kt, max(CH * c, P * kt), CH * (c + 1) - max(CH * c, P * kt))
         for c in range(2) for kt in range(4 * c + 4)]
NSTEP = len(STEPS)
S2_BANKS = (4, 5, 7)


def quad_order():
    first = [(j, qt) for j in range(4) for qt in range(QT)]
    cost1 = [P * (qt + 1) for _, qt in first]
    total1, total2 = sum(cost1), 4 * sum(w for *_, w in STEPS)
    out, done1, done2, at = [], 0, 0, 0
    for s, (_, _, _, w) in enumerate(STEPS):
        for j in range(4):
            while at < len(first) and done1 * total2 <= done2 * total1:
                out.append(("first", *first[at]))
                done1 += cost1[at]
                at += 1
            out.append(("second", s, j))
            done2 += w
        if s:
            out.append(("values", s - 1, 0))
    out += [("first", *f) for f in first[at:]]
    out.append(("values", NSTEP - 1, 0))
    return out


ORDER = quad_order()
PLAN = (("causal", "a"), ("layers", 0), ("causal", "b"), ("layers", 1))


def build(nc, t, out, scratch):
    with ExitStack() as ctx:
        def sb(name, shape, dt=F32, stack=ctx):
            return stack.enter_context(nc.sbuf_tensor(name, shape, dt))

        names = {}

        def sem(name):
            if name not in names:
                names[name] = ctx.enter_context(nc.semaphore(name))
            return names[name]

        ps = ctx.enter_context(nc.psum_tensor("ps", [P, 8, CH], F32))

        res = sb("res", [P, TOK])
        ident = sb("ident", [P, P])
        identb = sb("identb", [P, P], BF16)
        mean_w = sb("mean_w", [P, P])
        ones_w = sb("ones_w", [P, P])
        eps_col = sb("eps_col", [P, 1])
        lnc = sb("lnc", [P, SEQ])
        lnq = sb("lnq", [P, SEQ])
        dev8 = sb("dev8", [P, 2, QT])
        rdev8 = sb("rdev8", [P, 2, QT])
        step = sem("step")
        const_in = sem("const_in")
        out_done = sem("out_done")

        PLACE = (step, 6, 2, lnc[:], lnq[:])
        wide = ps[:, 6:8, :].rearrange("p x n -> p (x n)")

        def pair(bank):
            return ps[:, bank:bank + 2, :].rearrange("p x n -> p (x n)")

        def ln_mean(pe, k, src, place):
            chain, bank, v, centred, squares = place
            pe.wait_ge(chain, k)
            for x in range(2):
                last = nc.tensor.matmul(ps[:, bank + x, :], mean_w[:], src[:, x * CH:(x + 1) * CH], start=True, stop=True)
            last.then_inc(chain, 1)

        def ln_variance(pe, k, place):
            chain, bank, v, centred, squares = place
            pe.wait_ge(chain, k + 3)
            for x in range(QT):
                last = nc.tensor.matmul(ps[:, v, x:x + 1], squares[:, x * P:(x + 1) * P], mean_w[:, 0:1], start=True, stop=True)
            last.then_inc(chain, 1)

        def ln_spread(pe, k, place):
            chain, bank, v, centred, squares = place
            pe.wait_ge(chain, k + 7)
            for x in range(2):
                last = nc.tensor.matmul(ps[:, bank + x, :], ones_w[:], squares[:, x * CH:(x + 1) * CH], start=True, stop=True)
            last.then_inc(chain, 1)

        def ln_square(act, k, place):
            chain, bank, v, centred, squares = place
            act.wait_ge(chain, k + 2)
            nc.scalar.activation(squares, centred, ACT.Square).then_inc(chain, 1)

        def ln_deviation(act, k, place):
            chain, bank, v, centred, squares = place
            act.wait_ge(chain, k + 4)
            nc.scalar.activation(dev8[:, v - 2, :], ps[:, v, 0:QT], ACT.Sqrt, bias=eps_col[:, 0:1]).then_inc(chain, 1)

        def ln_centre(dve, k, src, place):
            chain, bank, v, centred, squares = place
            dve.wait_ge(chain, k + 1)
            nc.vector.tensor_tensor(centred, src, pair(bank), ALU.subtract).then_inc(chain, 1)

        def ln_factors(dve, k, place):
            chain, bank, v, centred, squares = place
            dve.wait_ge(chain, k + 5)
            nc.vector.reciprocal(rdev8[:, v - 2, :], dev8[:, v - 2, :]).then_inc(chain, 1)
            dve.wait_ge(chain, k + 6)
            nc.vector.tensor_tensor(squares.rearrange("p (x n) -> p x n", n=P), ident[:].unsqueeze(1).to_broadcast([P, QT, P]),
                                    rdev8[:, v - 2, :].unsqueeze(2).to_broadcast([P, QT, P]), ALU.mult).then_inc(chain, 1)

        def ln_scale(dve, k, dst, place, gain=None, shift=None):
            chain, bank, v, centred, squares = place
            dve.wait_ge(chain, k + 8)
            if gain is None:
                nc.vector.tensor_tensor(dst, centred, pair(bank), ALU.mult).then_inc(chain, 2)
            else:
                nc.vector.tensor_tensor(centred, centred, pair(bank), ALU.mult).then_inc(chain, 1)
                dve.wait_ge(chain, k + 9)
                nc.vector.tensor_scalar(dst, centred, gain, shift, ALU.mult, ALU.add).then_inc(chain, 1)

        def ln_pe(pe, k, src):
            ln_mean(pe, k, src, PLACE)
            ln_variance(pe, k, PLACE)
            ln_spread(pe, k, PLACE)

        def ln_act(act, k):
            ln_square(act, k, PLACE)
            ln_deviation(act, k, PLACE)

        def ln_dve(dve, k, src, dst, gain, shift):
            ln_centre(dve, k, src, PLACE)
            ln_factors(dve, k, PLACE)
            ln_scale(dve, k, dst, PLACE, gain, shift)

        LN = 10

        def stream_norm(block, second, dsts):
            other = sem("other_step")
            places = [PLACE, (other, 4, 3, *second)]
            ks = [at[0], other_at[0]]
            at[0] += LN
            other_at[0] += LN
            both = list(zip(ks, places))
            srcs = [res[:, u * SEQ:(u + 1) * SEQ] for u in range(BATCH)]

            @block.tensor
            def _(pe):
                for (k, place), src in zip(both, srcs):
                    ln_mean(pe, k, src, place)
                for k, place in both:
                    ln_variance(pe, k, place)
                for k, place in both:
                    ln_spread(pe, k, place)

            @block.scalar
            def _(act):
                for k, place in both:
                    ln_square(act, k, place)
                for k, place in both:
                    ln_deviation(act, k, place)

            @block.vector
            def _(dve):
                for (k, place), src in zip(both, srcs):
                    ln_centre(dve, k, src, place)
                for k, place in both:
                    ln_factors(dve, k, place)
                for (k, place), dst in zip(both, dsts):
                    if len(dst) == 1:
                        ln_scale(dve, k, dst[0], place)
                    else:
                        dve.wait_ge(place[0], k + 8)
                        for half, to in enumerate(dst):
                            rows = slice(64 * half, 64 * half + 64)
                            ins = nc.vector.tensor_tensor(to, place[3][rows], pair(place[1])[rows], ALU.mult)
                        ins.then_inc(place[0], 2)

        at = [0]
        other_at = [0]

        with nc.Block() as block:
            @block.sync
            def _(sp):
                sp.dma_start(res[:], t["x"]).then_inc(const_in, 16)
                sp.dma_start(ident[:], t["ident"]).then_inc(const_in, 16)
                sp.dma_start(identb[:], t["identb"]).then_inc(const_in, 16)
                sp.wait_ge(const_in, 48)

            @block.gpsimd
            def _(pool):
                nc.gpsimd.memset(mean_w[:], 1.0 / P)
                nc.gpsimd.memset(ones_w[:], 1.0)
                nc.gpsimd.memset(eps_col[:], LN_EPS)

        def causal(kind):
            with ExitStack() as local:
                def lb(name, shape, dt=F32):
                    return sb(f"{kind}_{name}", shape, dt, local)

                xl = lb("xl", [P, TOK])
                qs = [lb(f"qs{i}", [P, HEADS, SEQ], BF16) for i in range(2)]
                ks = [lb(f"ks{i}", [P, HEADS, SEQ], BF16) for i in range(2)]
                vrow = lb("vrow", [P, QT, P])
                vq = lb("vq", [P, QT, 4, 32])
                pt = lb("pt", [P, 2, 4, CH])
                nm = lb("nm", [P, P])
                ot = lb("ot", [P, QUADS, SEQ])
                mask_q = lb("mask_q", [P, P], BF16)
                mask_k = lb("mask_k", [P, P], BF16)
                wts = lb("wts", [P, 2, 3, P])
                wo = lb("wo", [P, P])
                wout = lb("wout", [P, P])
                cols = lb("cols", [P, 5])
                cols2 = lb("cols2", [P, 3])
                bvb = lb("bvb", [P, P])
                flat = pt[:, :, :, :].rearrange("p a b c -> p (a b c)")
                qkf = [flat[:, 0:SEQ], flat[:, SEQ:2 * SEQ]]
                rest = [flat[:, 2 * SEQ:3 * SEQ], flat[:, 3 * SEQ:4 * SEQ]]
                parts = ot[:, :, :].rearrange("p q n -> p (q n)")[:, 0:3 * SEQ].bitcast(BF16).rearrange("p (a c n) -> p a c n", a=2, c=3)
                onm = ot[:, 3, :].rearrange("p (x n) -> p x n", n=P)
                mparts = lb("mparts", [P, 3, P], BF16)
                mrest = lb("mrest", [P, P])
                den = lb("den", [P, QT, HEADS])
                rden = lb("rden", [P, QT, HEADS])
                acc = lb("acc", [P, SEQ])

                scales = SCALES if kind == "a" else 1
                units = [(s, b) for b in range(BATCH) for s in range(scales)]
                qscale = float(HD) ** (0.5 if kind == "a" else -0.5)
                den_eps = 1e-6 if kind == "a" else 0.0
                k = kind
                setup_in, w_in, stack_in = sem(k + "setup_in"), sem(k + "w_in"), sem(k + "stack_in")
                part_out = [sem(k + "q_part_out"), sem(k + "k_part_out")]
                s1_ready, s1_free = sem(k + "s1_ready"), sem(k + "s1_free")
                s2_ready, s2_free = sem(k + "s2_ready"), sem(k + "s2_free")
                pt_free = sem(k + "pt_free")
                ot_free = sem(k + "ot_free")
                vq_ready = sem(k + "vq_ready")

                with nc.Block() as block:
                    @block.sync
                    def _(sp):
                        sp.dma_start(mask_q[:], t["mask_q"]).then_inc(setup_in, 16)
                        sp.dma_start(mask_k[:], t["mask_k"]).then_inc(setup_in, 16)
                        n = 32
                        if kind == "a":
                            for i, name in enumerate(("bout", "ln2_g", "ln2_b")):
                                sp.dma_start(cols2[:, i:i + 1], t[name].rearrange("(p a) -> p a", a=1)).then_inc(setup_in, 16)
                                n += 16
                        sp.wait_ge(setup_in, n)

                    @block.gpsimd
                    def _(pool):
                        nc.gpsimd.memset(vq[:, :, :, :], 0.0).then_inc(vq_ready, 1)
                        pool.wait_ge(vq_ready, 1)
                        nc.gpsimd.memset(vq[:, :, :, HD:HD + 1], 1.0)
                        for one in (s1_free, s2_free, pt_free, ot_free):
                            pool.sem_inc(one, START)
                        if kind == "b":
                            nc.gpsimd.memset(cols[:], 0.0)
                            nc.gpsimd.memset(bvb[:], 0.0)

                    @block.vector
                    def _(dve):
                        nc.vector.memset(nm[:], 0.0).then_inc(s1_free, 1)

                    @block.scalar
                    def _(act):
                        nc.scalar.activation(lnc[:, 0:1], eps_col[:], ACT.Copy).then_inc(s2_free, 2)

                    @block.tensor
                    def _(pe):
                        nc.tensor.matmul(ps[:, 0, 0:P], ident_b(), ident_b(), start=True, stop=True).then_inc(pt_free, 1)

                loaded, stacked, parted = [0], [0], [0, 0]

                def load(sp, dst, src):
                    loaded[0] += 16
                    sp.dma_start(dst, src).then_inc(w_in, 16)

                def load_ahead(sp, i):
                    if i + 1 < len(units) and kind == "a":
                        s, w = units[i + 1][0], (i + 1) % 2
                        for a, name in enumerate(("WqT", "WkT", "WvT")):
                            load(sp, wts[:, w, a, :], t[name][s])
                        for a, name in enumerate(("bq", "bk")):
                            load(sp, cols[:, a:a + 1], t[name][s].rearrange("(p a) -> p a", a=1))
                    if 0 <= i < len(units) and kind == "a":
                        load(sp, bvb[:], t["bv"][units[i][0]:units[i][0] + 1, :].to_broadcast([P, P]))
                    if i >= 1 and kind == "a":
                        s = units[i - 1][0]
                        load(sp, wo[:], t["WoT"][s])
                        load(sp, wout[:], t["WoutT"][s * P:(s + 1) * P, :])
                        for n, name in enumerate(("bo", "ln_g", "ln_b")):
                            load(sp, cols[:, 2 + n:3 + n], t[name][s].rearrange("(p a) -> p a", a=1))
                    if i < 0 and kind == "b":
                        load(sp, wts[:, 0, :, :], t["bWqkv"].rearrange("p (a n) -> p a n", a=3))
                        load(sp, wo[:], t["bWout"])

                def stack(sp, dst, src):
                    stacked[0] += 16
                    sp.dma_start(dst, src).then_inc(stack_in, 16)

                zeroed = sem(k + "zeroed")
                with nc.Block() as block:
                    @block.gpsimd
                    def _(pool):
                        for i in range(2):
                            nc.gpsimd.memset(qs[i][:, :, :].bitcast(F32), 0.0).then_inc(zeroed, 1)
                            nc.gpsimd.memset(ks[i][:, :, :].bitcast(F32), 0.0).then_inc(zeroed, 1)

                    @block.sync
                    def _(sp):
                        load_ahead(sp, -1)
                        for i in range(2):
                            for a, (to, name) in enumerate(((qs[i], "crow_q"), (ks[i], "crow_k"))):
                                sp.wait_ge(zeroed, 2 * i + a + 1)
                                stack(sp, to[MROW:MROW + CROWS, :, :], t[name + kind])

                    stream_norm(block, (flat[:, 0:SEQ], flat[:, SEQ:2 * SEQ]), [(xl[:, u * SEQ:(u + 1) * SEQ],) for u in range(BATCH)])

                chains = {n: sem(k + n + "_step") for n in ("q", "k", "m", "v")}
                stood = dict.fromkeys(chains, 0)

                def between(i):
                    now = units[i] if 0 <= i < len(units) else None
                    after = units[i + 1] if i + 1 < len(units) else None
                    before = units[i - 1] if i >= 1 else None
                    w_now, w_after = (i % 2, (i + 1) % 2) if kind == "a" else (0, 0)
                    par, par_after = i % 2, (i + 1) % 2
                    z, e0 = dict(stood), at[0]
                    if now:
                        stood["m"] += 5
                        stood["v"] += 2
                    if after:
                        stood["q"] += 6
                        stood["k"] += 6
                    last_scale = bool(before) and kind == "a" and before[0] == scales - 1
                    kln = e0 + 8
                    if before:
                        at[0] += 8 + (LN + 2 if kind == "a" else 0) + (LN + 2 if last_scale else 0)
                    with nc.Block() as block:
                        @block.sync
                        def _(sp):
                            if now:
                                sp.wait_ge(chains["m"], z["m"] + 5)
                                for c in range(3):
                                    stack(sp, qs[par][MROW + c:MROW + c + 1, :, :].rearrange("p h (q n) -> p (h q) n", n=P), mparts[:, c, :])
                            if after:
                                if i + 1 >= 2:
                                    stack(sp, qs[par_after][MROW:MROW + 3, :, :], t["crow_q" + kind][0:3])
                                for a in range(2):
                                    sp.wait_ge(chains["qk"[a]], z["qk"[a]] + 6)
                                    sp.dma_start(scratch[a].rearrange("c p n -> p c n"), parts[:, a, :, :]).then_inc(part_out[a], 16)
                                for a, (combo, to) in enumerate(((COMBO_Q, qs[par_after]), (COMBO_K, ks[par_after]))):
                                    parted[a] += 16
                                    sp.wait_ge(part_out[a], parted[a])
                                    for g, c in enumerate(combo):
                                        stack(sp, to[8 * g:8 * g + 8, :, :], scratch[a, c].rearrange("(h d) n -> d h n", d=HD))

                        @block.tensor
                        def _(pe):
                            if now:
                                nc.tensor.transpose(ps[:, 0, 0:P], nm[:], ident[:]).then_inc(chains["m"], 1)
                            if before:
                                for x in (*range(1, QT), 0):
                                    if x == 0 and now:
                                        pe.wait_ge(chains["m"], z["m"] + 3)
                                    for q in range(QUADS):
                                        last = nc.tensor.transpose(ps[:, x, q * P:(q + 1) * P], ot[:, q, x * P:(x + 1) * P], ident[:])
                                last.then_inc(step, 1)
                                pe.wait_ge(step, e0 + 4)
                            if now or after:
                                pe.wait_ge(w_in, loaded[0])
                            if after:
                                if now and not before:
                                    pe.wait_ge(chains["m"], z["m"] + 3)
                                for a in range(2):
                                    for c in range(2):
                                        last = nc.tensor.matmul(ps[:, 2 * a + c, :], wts[:, w_after, a, :],
                                                                xl[:, after[1] * SEQ + c * CH:after[1] * SEQ + (c + 1) * CH],
                                                                start=True, stop=True)
                                    last.then_inc(chains["qk"[a]], 1)
                            if before:
                                for x in range(QT):
                                    last = nc.tensor.transpose(ps[:, 6 + x // 4, x % 4 * P:(x % 4 + 1) * P], onm[:, x, :], ident[:])
                                last.then_inc(step, 1)
                            if now:
                                for kt in range(QT):
                                    last = nc.tensor.matmul(ps[:, 4 + kt // 4, (kt % 4) * P:(kt % 4 + 1) * P],
                                                            xl[:, now[1] * SEQ + kt * P:now[1] * SEQ + (kt + 1) * P], wts[:, w_now, 2, :],
                                                            start=True, stop=True)
                                last.then_inc(chains["v"], 1)
                            if before:
                                pe.wait_ge(w_in, loaded[0])
                                pe.wait_ge(step, e0 + 6)
                                for x in range(2):
                                    last = nc.tensor.matmul(ps[:, 6 + x, :], wo[:], lnq[:, x * CH:(x + 1) * CH], start=True, stop=True)
                                last.then_inc(step, 1)
                                if kind == "a":
                                    if after:
                                        pe.wait_ge(chains["k"], z["k"] + 2)
                                    ln_pe(pe, kln, lnc)
                                    pe.wait_ge(step, kln + LN)
                                    for x in range(2):
                                        last = nc.tensor.matmul(ps[:, 6 + x, :], wout[:], lnc[:, x * CH:(x + 1) * CH], start=True, stop=True)
                                    last.then_inc(step, 1)
                                if last_scale:
                                    ln_pe(pe, kln + LN + 3, lnc)

                        @block.scalar
                        def _(act):
                            def part(a, n):
                                act.wait_ge(chains["qk"[a]], z["qk"[a]] + 2 + 2 * n)
                                nc.scalar.activation(parts[:, a, n, :], (rest if n else qkf)[a], ACT.Copy).then_inc(chains["qk"[a]], 1)

                            if after:
                                part(0, 0)
                                part(1, 0)
                            if before:
                                act.wait_ge(step, e0 + 5)
                                nc.scalar.activation(lnq[:], wide, ACT.Copy).then_inc(step, 1)
                            if after:
                                part(0, 1)
                                part(1, 1)
                            if before and kind == "a":
                                ln_act(act, kln)
                            if last_scale:
                                ln_act(act, kln + LN + 3)

                        @block.vector
                        def _(dve):
                            if now:
                                mz = z["m"]
                                dve.wait_ge(chains["m"], mz + 1)
                                nc.vector.tensor_copy(mparts[:, 0, :], ps[:, 0, 0:P]).then_inc(chains["m"], 1)
                                dve.wait_ge(chains["m"], mz + 2)
                                nc.vector.tensor_tensor(mrest[:], ps[:, 0, 0:P], mparts[:, 0, :], ALU.subtract).then_inc(chains["m"], 1)
                                dve.wait_ge(chains["m"], mz + 3)
                                nc.vector.tensor_copy(mparts[:, 1, :], mrest[:]).then_inc(chains["m"], 1)
                                dve.wait_ge(chains["m"], mz + 4)
                                nc.vector.tensor_tensor(mparts[:, 2, :], mrest[:], mparts[:, 1, :], ALU.subtract).then_inc(chains["m"], 1)
                            if before:
                                turned = ps[:, :, :].rearrange("p x (h d) -> p x h d", d=32)
                                dve.wait_ge(step, e0 + 1)
                                nc.vector.tensor_scalar(den[:, :, :], turned[:, :, :, HD], den_eps, None, ALU.add).then_inc(step, 1)
                                dve.wait_ge(step, e0 + 2)
                                nc.vector.reciprocal(rden[:, :, :], den[:, :, :]).then_inc(step, 1)
                                dve.wait_ge(step, e0 + 3)
                                nc.vector.tensor_tensor(onm[:, :, :].rearrange("p x (h d) -> p x h d", d=HD), turned[:, :, :, 0:HD],
                                                        rden[:, :, :].unsqueeze(3).to_broadcast([P, QT, HEADS, HD]), ALU.mult).then_inc(step, 1)
                            if now or after:
                                dve.wait_ge(w_in, loaded[0])

                            def scale(a):
                                dve.wait_ge(chains["qk"[a]], z["qk"[a]] + 1)
                                nc.vector.tensor_scalar(qkf[a].rearrange("p (c n) -> p c n", c=2), ps[:, 2 * a:2 * a + 2, :],
                                                        cols[:, a:a + 1], qscale if a == 0 else 1.0,
                                                        ALU.add, ALU.mult).then_inc(chains["qk"[a]], 1)

                            def subtract(a, n):
                                dve.wait_ge(chains["qk"[a]], z["qk"[a]] + 3 + 2 * n)
                                nc.vector.tensor_tensor(parts[:, a, 2, :] if n else rest[a], (rest if n else qkf)[a],
                                                        parts[:, a, n, :], ALU.subtract).then_inc(chains["qk"[a]], 1)

                            if after:
                                scale(0)
                                scale(1)
                                subtract(0, 0)
                                subtract(1, 0)
                            if now:
                                dve.wait_ge(chains["v"], z["v"] + 1)
                                nc.vector.tensor_tensor(vrow[:, :, :], ps[:, 4:6, :].rearrange("p a (t n) -> p (a t) n", n=P),
                                                        bvb[:].unsqueeze(1).to_broadcast([P, QT, P]), ALU.add).then_inc(chains["v"], 1)
                            if after:
                                subtract(0, 1)
                                subtract(1, 1)
                            if not before:
                                return
                            sl = slice(before[1] * SEQ, (before[1] + 1) * SEQ)
                            dve.wait_ge(step, e0 + 7)
                            if kind == "b":
                                nc.vector.tensor_tensor(res[:, sl], res[:, sl], wide, ALU.add).then_inc(step, 1)
                                return
                            nc.vector.tensor_scalar(lnc[:], wide, cols[:, 2:3], None, ALU.add).then_inc(step, 1)
                            ln_dve(dve, kln, lnc[:], lnc[:], cols[:, 3:4], cols[:, 4:5])
                            dve.wait_ge(step, kln + LN + 1)
                            if before[0] == 0:
                                nc.vector.tensor_copy(acc[:], wide).then_inc(step, 1)
                            else:
                                nc.vector.tensor_tensor(acc[:], wide, acc[:], ALU.add).then_inc(step, 1)
                            if last_scale:
                                dve.wait_ge(step, kln + LN + 2)
                                nc.vector.tensor_scalar(lnc[:], acc[:], cols2[:, 0:1], None, ALU.add).then_inc(step, 1)
                                ln_dve(dve, kln + LN + 3, lnc[:], lnc[:], cols2[:, 1:2], cols2[:, 2:3])
                                dve.wait_ge(step, kln + 2 * LN + 3)
                                nc.vector.tensor_tensor(res[:, sl], res[:, sl], lnc[:], ALU.add).then_inc(step, 1)

                between(-1)
                for i in range(len(units) + 1):
                    now = units[i] if i < len(units) else None
                    before = units[i - 1] if i else None

                    par1, par2 = i % 2, (i + 1) % 2
                    b2 = before[1] if before else 0
                    with nc.Block() as block:
                        @block.sync
                        def _(sp):
                            load_ahead(sp, i)

                        @block.gpsimd
                        def _(pool):
                            if not before:
                                return
                            u = i - 1
                            with pool.Fori(0, QUADS) as quad:
                                pool.wait_ge(pt_free, NSTEP * (4 * u + quad) + 1 + START)
                                nc.gpsimd.tensor_copy(vq[:, :, :, 0:HD],
                                                      vrow[:, :, bass.ds(quad * 4 * HD, 4 * HD)].rearrange("p t (j d) -> p t j d", d=HD)
                                                      ).then_inc(vq_ready, 1)

                        @block.tensor
                        def _(pe):
                            pe.wait_ge(stack_in, stacked[0])
                            with pe.Fori(0, QUADS) as quad:
                                n1 = (4 * i + quad) * 4 * QT
                                u = i - 1
                                n2 = (4 * u + quad) * 4 * NSTEP
                                nst = (4 * u + quad) * NSTEP
                                seen1 = seen2 = 0
                                for what, x, y in ORDER:
                                    if what == "first":
                                        if not now:
                                            continue
                                        j, qt = x, y
                                        bank = 2 * (seen1 % 2)
                                        lhs = qs[par1][:, bass.ds(quad * 4 + j, 1), qt * P:(qt + 1) * P]
                                        pe.wait_ge(s1_free, n1 + seen1 + START)
                                        cols_n = P * (qt + 1)
                                        last = None
                                        for h in range(0, cols_n, CH):
                                            w = min(CH, cols_n - h)
                                            diag = h + w == cols_n
                                            last = nc.tensor.matmul(ps[:, bank + h // CH, 0:w], lhs,
                                                                    ks[par1][:, bass.ds(quad * 4 + j, 1), h:h + w],
                                                                    start=True, stop=not diag)
                                        e = cols_n - P
                                        last = nc.tensor.matmul(ps[:, bank + e // CH, e % CH:e % CH + P], identb[:], mask_q[:],
                                                                start=False, stop=True)
                                        last.then_inc(s1_ready, 1)
                                        seen1 += 1
                                    elif not before:
                                        continue
                                    elif what == "second":
                                        c, kt, q0, w = STEPS[x]
                                        j = y
                                        bank = S2_BANKS[seen2 % 3]
                                        pe.wait_ge(s2_free, n2 + seen2 + START)
                                        diag = q0 == kt * P
                                        last = nc.tensor.matmul(ps[:, bank, 0:w], ks[par2][:, bass.ds(quad * 4 + j, 1), kt * P:(kt + 1) * P],
                                                                qs[par2][:, bass.ds(quad * 4 + j, 1), q0:q0 + w],
                                                                start=True, stop=not diag)
                                        if diag:
                                            last = nc.tensor.matmul(ps[:, bank, 0:P], identb[:], mask_k[:], start=False, stop=True)
                                        last.then_inc(s2_ready, 1)
                                        seen2 += 1
                                    else:
                                        c, kt, q0, w = STEPS[x]
                                        if x == 0:
                                            pe.wait_ge(vq_ready, 4 * u + quad + 2)
                                        if kt == 0:
                                            pe.wait_ge(ot_free, 2 * (4 * u + quad) + c + START)
                                        pe.wait_ge(s2_free, n2 + 4 * x + 6 + START)
                                        for j in range(4):
                                            last = nc.tensor.matmul(ps[32 * j:32 * j + 32, 6, q0 - c * CH:q0 - c * CH + w],
                                                                    vq[:, kt, j, :], pt[:, x % 2, j, 0:w],
                                                                    start=kt == 0, stop=kt == 4 * c + 3)
                                        last.then_inc(pt_free, 1)

                        @block.vector
                        def _(dve):
                            with dve.Fori(0, QUADS) as quad:
                                n1 = (4 * i + quad) * 4 * QT
                                u = i - 1
                                if now:
                                    seen1 = 0
                                    for what, x, y in ORDER:
                                        if what != "first":
                                            continue
                                        j, qt = x, y
                                        bank = 2 * (seen1 % 2)
                                        dve.wait_ge(s1_ready, n1 + seen1 + 1)
                                        flat1 = ps[:, bank:bank + 2, :].rearrange("p a n -> p (a n)")
                                        nc.vector.tensor_reduce(nm[:, bass.ds(quad * 32 + j * QT + qt, 1)], flat1[:, 0:P * (qt + 1)],
                                                                AX.X, ALU.max, negate=True).then_inc(s1_free, 1)
                                        seen1 += 1
                                if before:
                                    dve.wait_ge(pt_free, NSTEP * (4 * u + quad + 1) + 1 + START)
                                    nc.vector.tensor_copy(ot[:, bass.ds(quad, 1), CH:2 * CH], ps[:, 6, :]).then_inc(ot_free, 1)

                        @block.scalar
                        def _(act):
                            if not before:
                                return
                            with act.Fori(0, QUADS) as quad:
                                u = i - 1
                                n2 = (4 * u + quad) * 4 * NSTEP
                                nst = (4 * u + quad) * NSTEP
                                seen2 = 0
                                for x, (c, kt, q0, w) in enumerate(STEPS):
                                    act.wait_ge(pt_free, nst + x + START)
                                    for j in range(4):
                                        act.wait_ge(s2_ready, n2 + seen2 + 1)
                                        nc.scalar.activation(pt[:, x % 2, j, 0:w], ps[:, S2_BANKS[seen2 % 3], 0:w], ACT.Exp).then_inc(s2_free, 1)
                                        seen2 += 1
                                    if x == 4:
                                        act.wait_ge(pt_free, nst + 4 + 1 + START)
                                        nc.scalar.activation(ot[:, bass.ds(quad, 1), 0:CH], ps[:, 6, :], ACT.Copy).then_inc(ot_free, 1)

                    between(i)

        def ident_b():
            return identb[:]

        def layers(call):
            with ExitStack() as local:
                def lb(name, shape, dt=F32):
                    return sb(f"l{call}_{name}", shape, dt, local)

                xa = lb("xa", [P, BATCH, XW_COLS])
                xb = lb("xb", [P, BATCH, XW_COLS])
                wqk = lb("wqk", [P, 2 * INNER])
                wvt = lb("wvt", [P, LH // 2, P])
                wo = lb("wo", [P, LH // 2, P])
                mh = lb("mh", [P, LH, P])
                w1 = lb("w1", [P, 2 * HID])
                w2 = lb("w2", [P, 3, P])
                b1 = lb("b1", [P, 2, 3])
                gcols = lb("gcols", [P, 3])
                base = lb("base", [P, 4, QT, LD])
                tab = lb("tab", [P, 4, QT, LD])
                sc = lb("sc", [P, 2, LD])
                lmask = lb("lmask", [P, QT, 2 * WIN], BF16)
                sq = lb("sq", [P, 2, INNER])
                rc = lb("rc", [P, 2, INNER])
                rs = lb("rs", [P, 2, INNER])
                turns = [[rc[:, 0, :], rc[:, 1, :]], [lnc[:], lnq[:]]]
                qkn = lb("qkn", [P, 2, INNER])
                ss = lb("ss", [P, 2, LH])
                rn = lb("rn", [P, 2, LH])
                qt_ = lb("qt", [P, 2, LH // 2, P])
                kt_ = lb("kt", [P, LH // 2, WIN + SEQ])
                mx = lb("mx", [P, LH])
                pe_ = lb("pe", [P, LH, 2 * WIN])
                pn = lb("pn", [P, LH, 2 * WIN])
                rl = lb("rl", [P, LH])
                lsum = lb("lsum", [P, LH])
                ptl = lb("ptl", [P, LH // 2, P])
                xw = lb("xw", [P, 4, 2, P])
                yb = lb("yb", [P, LH, CH])
                dev = lb("dev", [P, BATCH, QT])
                rdev = lb("rdev", [P, BATCH, QT])
                ybf = yb[:, :, :].rearrange("p h n -> p (h n)")
                dg = ybf[:, 0:BATCH * SEQ].rearrange("p (u n) -> p u n", u=BATCH)
                gl, hh = (ybf[:, BATCH * SEQ + x * 6 * CH:BATCH * SEQ + (x + 1) * 6 * CH].rearrange("p (c g n) -> p c g n", c=2, g=3) for x in range(2))

                c = f"l{call}"
                lin = sem(c + "in")
                a_in, m_in = sem(c + "attn_w_in"), sem(c + "mlp_w_in")
                def load_attn(sp, L):
                    sp.dma_start(wqk[:], t["lWqkv"][bass.ds(L, 1), :, 0:2 * INNER]).then_inc(a_in, 16)
                    sp.dma_start(wvt[:, :, :], t["lWvT"][bass.ds(L, 1)]).then_inc(a_in, 16)
                    sp.dma_start(wo[:, :, :], t["lWo"][bass.ds(L, 1)].rearrange("a (g p) o -> p (a g) o", p=P)).then_inc(a_in, 16)
                    sp.dma_start(sc[:, 0, :], t["q_scale"][bass.ds(L, 1), :].to_broadcast([P, LD])).then_inc(a_in, 16)
                    sp.dma_start(sc[:, 1, :], t["k_scale"][bass.ds(L, 1), :].to_broadcast([P, LD])).then_inc(a_in, 16)

                A_IN = 80

                def load_mlp(sp, L):
                    sp.dma_start(w1[:], t["lW1"][bass.ds(L, 1)]).then_inc(m_in, 16)
                    sp.dma_start(w2[:, 0:2, :], t["lW2"][bass.ds(L, 1), 0:2 * P, :].rearrange("a (g p) o -> p (a g) o", p=P)).then_inc(m_in, 16)
                    sp.dma_start(w2[0:85, 2, :], t["lW2"][bass.ds(L, 1), 2 * P:HID, :].rearrange("a p o -> p (a o)")).then_inc(m_in, 16)
                    for half in range(2):
                        for n, (h0, w) in enumerate(HCH):
                            sp.dma_start(b1[0:w, half, n:n + 1], t["lb1"][bass.ds(L, 1), half * HID + h0:half * HID + h0 + w].rearrange("a (p n) -> p (a n)", n=1)).then_inc(m_in, 16)
                    for n, name in enumerate(("lg", "lb", "lb2")):
                        sp.dma_start(gcols[:, n:n + 1], t[name][bass.ds(L, 1)].rearrange("a (p n) -> p (a n)", n=1)).then_inc(m_in, 16)

                M_IN = 12 * 16

                with nc.Block() as block:
                    @block.sync
                    def _(sp):
                        sp.dma_start(base[:, :, :, :], t["rot"]).then_inc(lin, 16)
                        sp.dma_start(lmask[:, :, :], t["lmask"]).then_inc(lin, 16)
                        load_attn(sp, 0)

                    @block.vector
                    def _(dve):
                        nc.vector.memset(xa[:, :, :], 0.0)
                        nc.vector.memset(xb[:, :, :], 0.0)
                        nc.vector.memset(kt_[:, :, 0:WIN], 0.0)
                        nc.vector.memset(xw[:, :, :, :], 0.0)

                def scale_tables(pool):
                    for a in range(2):
                        full = sc[:, a, :].unsqueeze(1).to_broadcast([P, QT, LD])
                        nc.gpsimd.tensor_tensor(tab[:, 2 * a, :, :], base[:, 2 * a, :, :], full, ALU.mult)
                        for lo, hi in ((0, 32), (32, 0)):
                            part = sc[:, a, hi:hi + 32].unsqueeze(1).to_broadcast([P, QT, 32])
                            nc.gpsimd.tensor_tensor(tab[:, 2 * a + 1, :, lo:lo + 32], base[:, 2 * a + 1, :, lo:lo + 32], part, ALU.mult)

                with nc.Block() as block:
                    stream_norm(block, (rc[:, 0, :], rc[:, 1, :]),
                                [(xa[0:64, u, WIN:WIN + SEQ], xa[64:P, u, WIN + 1:WIN + 1 + SEQ]) for u in range(BATCH)])

                    @block.gpsimd
                    def _(pool):
                        pool.wait_ge(lin, 32)
                        pool.wait_ge(a_in, A_IN)
                        scale_tables(pool)

                    @block.sync
                    def _(sp):
                        pass

                M = {n: sem(c + n) for n in (
                    "mean_ready", "centred", "squared", "var_ready", "dev_done", "rdev_done", "diag_done", "spread_ready", "scaled",
                    "xn_done", "gate_ready", "a_ready", "gelu_done", "h_done", "w2_ready", "out_done")}
                S = {n: sem(c + n) for n in (
                    *(what + of for what in "qk" for of in ("_ready", "_squared", "_summed", "_read", "_rotated", "_unit", "_turned", "_placed")),
                    "sd_done", "rmax_done", "rn_done", "s_ready", "mx_done", "s_read", "exp_done", "sum_done", "rl_done", "p_done",
                    "p_turned", "p_placed", "xw_ready", "xw_done", "y_ready", "y_read_a", "y_read_v", "g_ready", "g_read", "mh_ready", "mh_read")}

                with nc.Block() as block:
                    @block.gpsimd
                    def _(pool):
                        for one in (*S.values(), *M.values()):
                            pool.sem_inc(one, START)

                with nc.Fori(0, DEPTH) as L:
                    with nc.Block() as block:
                        n0 = L * TILES

                        def done(name, n, per_tile=1):
                            return S[name], per_tile * n0 + n + START

                        def tile(t, stage, *args):
                            if 0 <= t < TILES:
                                stage(t, *args)

                        TURNS = range(-3, TILES + 1)

                        @block.sync
                        def _(sp):
                            load_mlp(sp, L)

                        @block.tensor
                        def _(pe):
                            shared = []

                            def product(t, a):
                                pe.wait_ge(*(done("q_read", t + 1) if a else done("k_read", t)))
                                for x in range(2):
                                    last = nc.tensor.matmul(ps[:, x, :], xa[:, t // QT, WIN + t % QT * P:WIN + (t % QT + 1) * P],
                                                            wqk[:, a * INNER + x * CH:a * INNER + (x + 1) * CH], start=True, stop=True)
                                last.then_inc(S["qk"[a] + "_ready"], 1)

                            def transposes(what, t, src):
                                if shared:
                                    pe.wait_ge(*done(*shared[-1]))
                                for x in range(8):
                                    last = nc.tensor.transpose(ps[:, 2 + x // 4, (x % 4) * P:(x % 4 + 1) * P],
                                                               src[:, x * P:(x + 1) * P], ident[:])
                                last.then_inc(S[what + "_turned"], 1)
                                shared.append((what + "_placed", t + 1))

                            def transpose_qk(t, a):
                                pe.wait_ge(*done("qk"[a] + "_unit", t + 1))
                                transposes("qk"[a], t, qkn[:, a, :])

                            def transpose_p(t):
                                pe.wait_ge(*done("p_done", t + 1))
                                transposes("p", t, pn[:, :, :].rearrange("p h j -> p (h j)"))

                            def score(t, part):
                                if part == 0:
                                    pe.wait_ge(S["mh_read"], L + 1 + START)
                                    pe.wait_ge(*done("s_read", t))
                                    pe.wait_ge(*done("q_placed", t + 1))
                                    pe.wait_ge(*done("k_placed", t + 1))
                                    for x in range(2):
                                        nc.tensor.matmul(ps[:, 4 + x, :], identb[:],
                                                         lmask[:, t % QT, :].unsqueeze(1).to_broadcast([P, 8, 2 * WIN]),
                                                         start=True, stop=False, skip_group_check=True)
                                for h in range(8 * part, 8 * part + 8):
                                    e = 64 * (h % 2)
                                    for w in range(4):
                                        last = nc.tensor.matmul(
                                            ps[32 * w:32 * w + 32, 4 + h % 2, (h // 2) * 64:(h // 2 + 1) * 64],
                                            qt_[e:e + 64, t % 2, h // 2, 32 * w:32 * w + 32],
                                            kt_[e:e + 64, h // 2, t % QT * P + 32 * w:t % QT * P + 32 * w + 64],
                                            start=False, stop=True, skip_group_check=True)
                                if part == 1:
                                    last.then_inc(S["s_ready"], 1)

                            def windows(t):
                                pe.wait_ge(S["mh_read"], L + 1 + START)
                                pe.wait_ge(*done("y_read_a", 2 * t, 2))
                                for w in range(2):
                                    o = t % QT * P + 32 * w
                                    last = nc.tensor.transpose(ps[:, 6, w * P:(w + 1) * P], xa[:, t // QT, o:o + P], ident[:])
                                last.then_inc(S["xw_ready"], 1)

                            def mix(t, half):
                                if half == 0:
                                    pe.wait_ge(*done("xw_done", t + 1))
                                    pe.wait_ge(*done("p_placed", t + 1))
                                pe.wait_ge(*done("y_read_v", 2 * t + half, 2))
                                pe.wait_ge(*done("y_read_a", 2 * t + half, 2))
                                for w in range(2):
                                    for e in range(2):
                                        ww = 2 * half + w
                                        last = nc.tensor.matmul(ps[:, 6 + e, w * 256:(w + 1) * 256], xw[:, ww, e, :],
                                                                ptl[:, :, 32 * ww:32 * ww + 32], start=True, stop=True)
                                last.then_inc(S["y_ready"], 1)

                            def project(t):
                                if t % 4 != 3:
                                    return
                                pe.wait_ge(*done("y_read_v", 2 * t + 2, 2))
                                pe.wait_ge(*done("y_read_a", 2 * t + 2, 2))
                                pe.wait_ge(*done(*shared[-1]))
                                for h in range(LH):
                                    last = nc.tensor.matmul(ps[:, 2, :], mh[:, h, :], yb[:, h, :], start=h == 0, stop=h == LH - 1)
                                last.then_inc(S["g_ready"], 1)
                                shared.append(("g_read", t + 1))

                            def head_weights():
                                for h in range(LH):
                                    e = 64 * (h % 2)
                                    last = nc.tensor.matmul(ps[:, 4 + h // 8 * 2 + h % 2, h % 8 // 2 * P:(h % 8 // 2 + 1) * P],
                                                            wvt[e:e + 64, h // 2, :], wo[e:e + 64, h // 2, :], start=True, stop=True)
                                last.then_inc(S["mh_ready"], 1)

                            pe.wait_ge(a_in, A_IN * (L + 1))
                            for i in TURNS:
                                if i == -2:
                                    head_weights()
                                tile(i - 1, mix, 1)
                                tile(i + 1, score, 0)
                                tile(i, windows)
                                tile(i + 1, score, 1)
                                tile(i, transpose_p)
                                tile(i + 3, product, 0)
                                tile(i - 1, project)
                                tile(i, mix, 0)
                                tile(i + 2, transpose_qk, 0)
                                tile(i + 3, product, 1)
                                tile(i + 2, transpose_qk, 1)

                        @block.scalar
                        def _(act):
                            def squares(t, a):
                                act.wait_ge(*done("qk"[a] + "_ready", t + 1))
                                act.wait_ge(*done("qk"[a] + "_summed", t))
                                nc.scalar.activation(sq[:, a, :].rearrange("p (x n) -> p x n", x=2), ps[:, 0:2, :], ACT.Square).then_inc(S["qk"[a] + "_squared"], 1)

                            def norms(t):
                                act.wait_ge(*done("q_summed", t + 1))
                                act.wait_ge(*done("k_summed", t + 1))
                                nc.scalar.activation(ss[:, :, :], ss[:, :, :], ACT.Sqrt).then_inc(S["sd_done"], 1)

                            def place_q(t):
                                act.wait_ge(*done("q_turned", t + 1))
                                act.wait_ge(*done("s_ready", max(t - 1, 0)))
                                nc.scalar.activation(qt_[:, t % 2, :, :].rearrange("p (x g) n -> p x (g n)", x=2), ps[:, 2:4, :], ACT.Copy).then_inc(S["q_placed"], 1)

                            def place_k(t):
                                act.wait_ge(*done("k_turned", t + 1))
                                if t >= QT:
                                    act.wait_ge(*done("s_ready", t - QT + 2))
                                for x in range(2):
                                    ins = nc.scalar.activation(kt_[:, 4 * x:4 * x + 4, WIN + t % QT * P:WIN + (t % QT + 1) * P],
                                                               ps[:, 2 + x, :].rearrange("p (g n) -> p g n", n=P), ACT.Copy)
                                ins.then_inc(S["k_placed"], 1)

                            def place_p(t):
                                act.wait_ge(*done("p_turned", t + 1))
                                act.wait_ge(*done("y_ready", 2 * t, 2))
                                nc.scalar.activation(ptl[:, :, :].rearrange("p (x g) n -> p x (g n)", x=2), ps[:, 2:4, :], ACT.Copy).then_inc(S["p_placed"], 1)

                            def place_windows(t):
                                act.wait_ge(*done("xw_ready", t + 1))
                                act.wait_ge(*done("y_ready", 2 * t, 2))
                                for r in range(2):
                                    src = ps[64 * r:64 * r + 64, 6, 0:2 * P].rearrange("p (w n) -> p w n", n=P)
                                    for e in range(2):
                                        ins = nc.scalar.activation(xw[64 * e:64 * e + 64, 2 * r:2 * r + 2, e, :], src, ACT.Copy)
                                ins.then_inc(S["xw_done"], 1)

                            def exponentials(t):
                                act.wait_ge(*done("s_read", t + 1))
                                nc.scalar.activation(pe_[:, :, :], pe_[:, :, :], ACT.Exp, scale=8.0).then_inc(S["exp_done"], 1)

                            def take_mixed(t, half):
                                act.wait_ge(*done("y_ready", 2 * t + half + 1, 2))
                                act.wait_ge(S["g_ready"], L * (TILES // 4) + t // 4 + START)
                                o = (t % 4) * P + half * 64
                                for w in range(2):
                                    ins = nc.scalar.activation(
                                        yb[:, :, o + 32 * w:o + 32 * w + 32].rearrange("p (g e) n -> p e g n", e=2)[:, 0],
                                        ps[:, 6, w * 256:(w + 1) * 256].rearrange("p (g n) -> p g n", n=WIN), ACT.Copy)
                                ins.then_inc(S["y_read_a"], 1)

                            def take_head_weights():
                                act.wait_ge(S["mh_ready"], L + 1 + START)
                                for g in range(2):
                                    ins = nc.scalar.activation(mh[:, 8 * g:8 * g + 8, :].rearrange("p (r e) n -> p e r n", e=2),
                                                               ps[:, 4 + 2 * g:6 + 2 * g, :].rearrange("p e (r n) -> p e r n", n=P), ACT.Copy)
                                ins.then_inc(S["mh_read"], 1)

                            for i in TURNS:
                                if i == -2:
                                    take_head_weights()
                                tile(i - 1, take_mixed, 0)
                                tile(i + 2, squares, 1)
                                tile(i + 1, place_k)
                                tile(i - 1, take_mixed, 1)
                                tile(i + 2, norms)
                                tile(i, place_windows)
                                tile(i, place_p)
                                tile(i + 3, squares, 0)
                                tile(i + 1, exponentials)
                                tile(i + 2, place_q)

                        @block.gpsimd
                        def _(pool):
                            def add(t, a):
                                pool.wait_ge(*done("qk"[a] + "_read", t + 1))
                                nc.gpsimd.tensor_tensor(turns[t % 2][a], turns[t % 2][a], rs[:, a, :], ALU.add).then_inc(S["qk"[a] + "_rotated"], 1)

                            def unit(t, a):
                                pool.wait_ge(*done("qk"[a] + "_rotated", t + 1))
                                pool.wait_ge(*done("rn_done", t + 1))
                                pool.wait_ge(*done("qk"[a] + "_turned", t))
                                nc.gpsimd.tensor_tensor(qkn[:, a, :].rearrange("p (h d) -> p h d", d=LD),
                                                        turns[t % 2][a].rearrange("p (h d) -> p h d", d=LD),
                                                        rn[:, a, :].unsqueeze(2).to_broadcast([P, LH, LD]), ALU.mult).then_inc(S["qk"[a] + "_unit"], 1)

                            for i in TURNS:
                                tile(i + 3, add, 0)
                                tile(i + 3, unit, 0)
                                tile(i + 3, add, 1)
                                tile(i + 3, unit, 1)

                        @block.vector
                        def _(dve):
                            def rotate(t, a):
                                dve.wait_ge(*done("qk"[a] + "_squared", t + 1))
                                dve.wait_ge(*done("qk"[a] + "_rotated", t))
                                if t >= 2:
                                    dve.wait_ge(*done("qk"[a] + "_unit", t - 1))
                                src = ps[:, 0:2, :].rearrange("p x (h d) -> p (x h) d", d=LD)
                                dst = turns[t % 2][a].rearrange("p (h d) -> p h d", d=LD)
                                dsin = rs[:, a, :].rearrange("p (h d) -> p h d", d=LD)
                                nc.vector.tensor_tensor(dst, src, tab[:, 2 * a, t % QT, :].unsqueeze(1).to_broadcast([P, LH, LD]), ALU.mult)
                                for lo, hi in ((0, 32), (32, 0)):
                                    ins = nc.vector.tensor_tensor(dsin[:, :, lo:lo + 32], src[:, :, hi:hi + 32],
                                                                  tab[:, 2 * a + 1, t % QT, lo:lo + 32].unsqueeze(1).to_broadcast([P, LH, 32]), ALU.mult)
                                ins.then_inc(S["qk"[a] + "_read"], 1)

                            def sum_squares(t, a):
                                dve.wait_ge(*done("qk"[a] + "_squared", t + 1))
                                nc.vector.tensor_reduce(ss[:, a, :], sq[:, a, :].rearrange("p (h d) -> p h d", d=LD), AX.X, ALU.add).then_inc(S["qk"[a] + "_summed"], 1)

                            def norms(t):
                                dve.wait_ge(*done("sd_done", t + 1))
                                dve.wait_ge(*done("k_unit", t))
                                dve.wait_ge(*done("q_unit", t))
                                nc.vector.tensor_scalar(rn[:, :, :], ss[:, :, :], 1e-12, None, ALU.max).then_inc(S["rmax_done"], 1)
                                dve.wait_ge(*done("rmax_done", t + 1))
                                nc.vector.reciprocal(rn[:, :, :], rn[:, :, :]).then_inc(S["rn_done"], 1)

                            def subtract_maxima(t):
                                dve.wait_ge(*done("s_ready", t + 1))
                                sc_ps = ps[:, 4:6, :].rearrange("p e (g j) -> p e g j", j=2 * WIN)
                                mxv = mx[:].rearrange("p (e g) -> p e g", e=2)
                                nc.vector.tensor_reduce(mxv, sc_ps, AX.X, ALU.max).then_inc(S["mx_done"], 1)
                                dve.wait_ge(*done("mx_done", t + 1))
                                nc.vector.tensor_tensor(pe_[:, :, :].rearrange("p (g e) j -> p e g j", e=2), sc_ps,
                                                        mxv.unsqueeze(3).to_broadcast([P, 2, LH // 2, 2 * WIN]), ALU.subtract).then_inc(S["s_read"], 1)

                            def sums(t):
                                dve.wait_ge(*done("exp_done", t + 1))
                                nc.vector.tensor_reduce(lsum[:], pe_[:, :, :], AX.X, ALU.add).then_inc(S["sum_done"], 1)
                                dve.wait_ge(*done("sum_done", t + 1))
                                nc.vector.reciprocal(rl[:], lsum[:]).then_inc(S["rl_done"], 1)

                            def normalise(t):
                                dve.wait_ge(*done("rl_done", t + 1))
                                dve.wait_ge(*done("p_turned", t))
                                nc.vector.tensor_tensor(pn[:, :, :], pe_[:, :, :], rl[:].unsqueeze(2).to_broadcast([P, LH, 2 * WIN]), ALU.mult).then_inc(S["p_done"], 1)

                            def take_mixed(t, half):
                                dve.wait_ge(*done("y_ready", 2 * t + half + 1, 2))
                                dve.wait_ge(S["g_ready"], L * (TILES // 4) + t // 4 + START)
                                o = (t % 4) * P + half * 64
                                for w in range(2):
                                    ins = nc.vector.tensor_copy(
                                        yb[:, :, o + 32 * w:o + 32 * w + 32].rearrange("p (g e) n -> p e g n", e=2)[:, 1],
                                        ps[:, 7, w * 256:(w + 1) * 256].rearrange("p (g n) -> p g n", n=WIN))
                                ins.then_inc(S["y_read_v"], 1)

                            def take_projected(t):
                                if t % 4 != 3:
                                    return
                                dve.wait_ge(S["g_ready"], L * (TILES // 4) + t // 4 + 1 + START)
                                o = WIN + (t % QT // 4) * CH
                                nc.vector.tensor_tensor(xb[0:64, t // QT, o:o + CH], ps[0:64, 2, :], xa[0:64, t // QT, o:o + CH], ALU.add)
                                nc.vector.tensor_tensor(xb[64:P, t // QT, o + 1:o + 1 + CH], ps[64:P, 2, :], xa[64:P, t // QT, o + 1:o + 1 + CH], ALU.add).then_inc(S["g_read"], 4)

                            for i in TURNS:
                                tile(i + 3, rotate, 0)
                                tile(i + 3, sum_squares, 0)
                                tile(i - 1, take_projected)
                                tile(i, take_mixed, 0)
                                tile(i + 1, sums)
                                tile(i + 1, normalise)
                                tile(i + 3, sum_squares, 1)
                                tile(i + 3, rotate, 1)
                                tile(i, take_mixed, 1)
                                tile(i + 3, norms)
                                tile(i + 2, subtract_maxima)

                    with nc.Block() as block:
                        def count(name, per_layer, n):
                            return M[name], L * per_layer + n + START

                        @block.sync
                        def _(sp):
                            load_attn(sp, L + 1)

                        @block.gpsimd
                        def _(pool):
                            pool.wait_ge(a_in, A_IN * (L + 2))
                            scale_tables(pool)

                        @block.tensor
                        def _(pe):
                            def mean(u):
                                if u:
                                    pe.wait_ge(*count("scaled", BATCH, u))
                                for cc in range(2):
                                    last = nc.tensor.matmul(ps[:, cc, :], mean_w[:], xb[:, u, WIN + cc * CH:WIN + (cc + 1) * CH], start=True, stop=True)
                                last.then_inc(M["mean_ready"], 1)

                            def variance(u):
                                pe.wait_ge(*count("squared", BATCH, u + 1))
                                for x in range(QT):
                                    last = nc.tensor.matmul(ps[:, 2, u * QT + x:u * QT + x + 1], sq[:, u, x * P:(x + 1) * P], mean_w[:, 0:1], start=True, stop=True)
                                last.then_inc(M["var_ready"], 1)

                            def spread(u):
                                pe.wait_ge(*count("diag_done", BATCH, u + 1))
                                for cc in range(2):
                                    last = nc.tensor.matmul(ps[:, cc, :], ones_w[:], dg[:, u, cc * CH:(cc + 1) * CH], start=True, stop=True)
                                last.then_inc(M["spread_ready"], 1)

                            def hidden(c, g):
                                n = 3 * c + g
                                h0, w = HCH[g]
                                if g == 0:
                                    pe.wait_ge(*count("xn_done", BATCH, c // 2 + 1))
                                if n >= 2:
                                    pe.wait_ge(*count("h_done", 12, n - 1))
                                for half in (1, 0):
                                    last = nc.tensor.matmul(ps[0:w, 3 + 2 * (n % 2) + half, :], w1[:, half * HID + h0:half * HID + h0 + w],
                                                            rs[:, c // 2, (c % 2) * CH:(c % 2 + 1) * CH], start=True, stop=True)
                                    last.then_inc(M["gate_ready" if half else "a_ready"], 1)

                            def output(c):
                                pe.wait_ge(*count("h_done", 12, 3 * c + 3))
                                if c:
                                    pe.wait_ge(*count("out_done", 4, c))
                                for g, (h0, w) in enumerate(HCH):
                                    last = nc.tensor.matmul(ps[:, 7, :], w2[0:w, g, :], hh[0:w, c % 2, g, :], start=g == 0, stop=g == 2)
                                last.then_inc(M["w2_ready"], 1)

                            pe.wait_ge(m_in, M_IN * (L + 1))
                            mean(0)
                            variance(0)
                            spread(0)
                            for g in range(3):
                                hidden(0, g)
                            mean(1)
                            hidden(1, 0)
                            output(0)
                            hidden(1, 1)
                            hidden(1, 2)
                            variance(1)
                            output(1)
                            spread(1)
                            for g in range(3):
                                hidden(2, g)
                            hidden(3, 0)
                            output(2)
                            hidden(3, 1)
                            hidden(3, 2)
                            output(3)

                        @block.scalar
                        def _(act):
                            def squares(u):
                                act.wait_ge(*count("centred", BATCH, u + 1))
                                nc.scalar.activation(sq[:, u, :], rc[:, u, :], ACT.Square).then_inc(M["squared"], 1)

                            def deviation(u):
                                act.wait_ge(*count("var_ready", BATCH, u + 1))
                                nc.scalar.activation(dev[:, u, :], ps[:, 2, u * QT:(u + 1) * QT], ACT.Sqrt, bias=eps_col[:, 0:1]).then_inc(M["dev_done"], 1)

                            def gates(c):
                                for g, (h0, w) in enumerate(HCH):
                                    act.wait_ge(*count("gate_ready", 12, 3 * c + g + 1))
                                    nc.scalar.activation(gl[0:w, c % 2, g, :], ps[0:w, 4 + 2 * ((3 * c + g) % 2), :], ACT.Gelu, bias=b1[0:w, 1, g:g + 1]).then_inc(M["gelu_done"], 1)

                            act.wait_ge(m_in, M_IN * (L + 1))
                            squares(0)
                            deviation(0)
                            gates(0)
                            squares(1)
                            gates(1)
                            deviation(1)
                            gates(2)
                            gates(3)

                        @block.vector
                        def _(dve):
                            def centre(u):
                                dve.wait_ge(*count("mean_ready", BATCH, u + 1))
                                nc.vector.tensor_tensor(rc[:, u, :], xb[:, u, WIN:WIN + SEQ], ps[:, 0:2, :].rearrange("p x n -> p (x n)"), ALU.subtract).then_inc(M["centred"], 1)

                            def diagonal(u):
                                dve.wait_ge(*count("dev_done", BATCH, u + 1))
                                nc.vector.reciprocal(rdev[:, u, :], dev[:, u, :]).then_inc(M["rdev_done"], 1)
                                dve.wait_ge(*count("rdev_done", BATCH, u + 1))
                                nc.vector.tensor_tensor(dg[:, u, :].rearrange("p (x n) -> p x n", n=P), ident[:].unsqueeze(1).to_broadcast([P, QT, P]),
                                                        rdev[:, u, :].unsqueeze(2).to_broadcast([P, QT, P]), ALU.mult).then_inc(M["diag_done"], 1)

                            def normalise(u):
                                dve.wait_ge(*count("spread_ready", BATCH, u + 1))
                                dve.wait_ge(*count("squared", BATCH, u + 1))
                                nc.vector.tensor_tensor(rc[:, u, :], rc[:, u, :], ps[:, 0:2, :].rearrange("p x n -> p (x n)"), ALU.mult).then_inc(M["scaled"], 1)
                                dve.wait_ge(*count("scaled", BATCH, u + 1))
                                nc.vector.tensor_scalar(rs[:, u, :], rc[:, u, :], gcols[:, 0:1], gcols[:, 1:2], ALU.mult, ALU.add).then_inc(M["xn_done"], 1)

                            def products(c, first, end):
                                for g in range(first, end):
                                    n, w = 3 * c + g, HCH[g][1]
                                    dve.wait_ge(*count("gelu_done", 12, n + 1))
                                    dve.wait_ge(*count("a_ready", 12, n + 1))
                                    nc.vector.scalar_tensor_tensor(hh[0:w, c % 2, g, :], ps[0:w, 3 + 2 * (n % 2), :], b1[0:w, 0, g:g + 1], gl[0:w, c % 2, g, :], ALU.add, ALU.mult).then_inc(M["h_done"], 1)

                            def stream(c):
                                u, o = c // 2, WIN + (c % 2) * CH
                                dve.wait_ge(*count("w2_ready", 4, c + 1))
                                nc.vector.scalar_tensor_tensor(xa[0:64, u, o:o + CH], ps[0:64, 7, :], gcols[0:64, 2:3], xb[0:64, u, o:o + CH], ALU.add, ALU.add)
                                nc.vector.scalar_tensor_tensor(xa[64:P, u, o + 1:o + 1 + CH], ps[64:P, 7, :], gcols[64:P, 2:3], xb[64:P, u, o + 1:o + 1 + CH], ALU.add, ALU.add).then_inc(M["out_done"], 1)

                            dve.wait_ge(m_in, M_IN * (L + 1))
                            centre(0)
                            diagonal(0)
                            normalise(0)
                            products(0, 0, 2)
                            centre(1)
                            products(0, 2, 3)
                            products(1, 0, 1)
                            stream(0)
                            products(1, 1, 3)
                            diagonal(1)
                            normalise(1)
                            stream(1)
                            products(2, 0, 3)
                            products(3, 0, 1)
                            stream(2)
                            products(3, 1, 3)
                            stream(3)

                with nc.Block() as block:
                    @block.sync
                    def _(sp):
                        sp.wait_ge(a_in, A_IN * (DEPTH + 1))

                    @block.vector
                    def _(dve):
                        r = res[:, :].rearrange("p (b n) -> p b n", b=BATCH)
                        nc.vector.tensor_tensor(r[0:64], r[0:64], xa[0:64, :, WIN:WIN + SEQ], ALU.add)
                        nc.vector.tensor_tensor(r[64:P], r[64:P], xa[64:P, :, WIN + 1:WIN + 1 + SEQ], ALU.add)

        for stage, which in PLAN:
            (causal if stage == "causal" else layers)(which)

        with nc.Block() as block:
            @block.sync
            def _(sp):
                sp.dma_start(out, res[:]).then_inc(out_done, 16)
                sp.wait_ge(out_done, 16)


def constants():
    f = np.float32

    def bf(a):
        u = np.asarray(a, f).view(np.uint32)
        return ((u + 0x7FFF + ((u >> 16) & 1)) >> 16).astype(np.uint16)

    def parts(a):
        a = np.asarray(a, f)
        out = []
        for _ in range(3):
            out.append((bf(a).astype(np.uint32) << 16).view(f))
            a = a - out[-1]
        return out

    n = np.arange(P)
    mask_q = bf(np.where(n[None, :] > n[:, None], NEG, 0.0))
    crow = {}
    pos = np.arange(SEQ)
    hi = pos // 32 * 32
    for kind in "ab":
        q = np.zeros((CROWS, HEADS, SEQ), f)
        k = np.zeros((CROWS, HEADS, SEQ), f)
        k[0:3] = 1.0
        if kind == "b":
            start = 2.0 ** (-(8.0 / HEADS))
            slopes = np.asarray([start * start ** i for i in range(HEADS)], f)
            for i, part in enumerate(parts(slopes)):
                q[3 + 2 * i] = q[4 + 2 * i] = part[:, None]
                k[3 + 2 * i] = hi
                k[4 + 2 * i] = pos - hi
        crow["crow_q" + kind], crow["crow_k" + kind] = bf(q), bf(k)
    half = np.arange(0, LD, 2, dtype=f)
    freqs = np.arange(SEQ, dtype=f)[:, None] * (f(1.0) / f(10000.0) ** (half / f(LD)))[None, :]
    freqs = np.concatenate([freqs, freqs], -1)
    base_scale = (half + f(0.4 * LD)) / f(1.4 * LD)
    power = (np.arange(SEQ, dtype=f) - SEQ // 2) / f(WIN // 2)
    scale = base_scale[None, :] ** power[:, None]
    scale = np.concatenate([scale, scale], -1)
    sign = np.concatenate([-np.ones(LD // 2, f), np.ones(LD // 2, f)])
    cos, sin = np.cos(freqs), np.sin(freqs) * sign
    rot = np.stack([cos * scale, sin * scale, cos / scale, sin / scale]).astype(f)
    rot = np.ascontiguousarray(rot.reshape(4, QT, P, LD).transpose(2, 0, 1, 3))
    i = n % WIN
    j = np.arange(2 * WIN)
    ok = (j[None, :] >= i[:, None]) & (j[None, :] <= i[:, None] + WIN)
    lmask = np.repeat(np.where(ok, 0.0, NEG)[:, None, :], QT, 1)
    lmask[:WIN, 0, :WIN] = NEG
    return {"ident": np.eye(P, dtype=f), "identb": bf(np.eye(P)), "mask_q": mask_q,
            "mask_k": np.ascontiguousarray(mask_q.T), "rot": rot, "lmask": bf(lmask),
            "zero_row": np.zeros((1, P), f), **crow}


BF16_CONSTANTS = ("identb", "mask_q", "mask_k", "lmask", "crow_qa", "crow_ka", "crow_qb", "crow_kb")


def arrays(inputs):
    g = {k.replace("L0_", ""): np.asarray(v) for k, v in inputs.items()}

    def tr(a):
        return np.ascontiguousarray(np.swapaxes(a, -1, -2))

    def wrap(a):
        return np.concatenate([a, a[:1]])

    wv = g["ffn_Wqkv"][:, :, 2 * INNER:]
    wvt = np.ascontiguousarray(wv.reshape(DEPTH, P, LH // 2, P).transpose(0, 3, 2, 1))
    d = {"x": tr(g["attn_a_x"].reshape(TOK, P)),
         "WqT": tr(g["attn_a_Wq"]), "WkT": tr(g["attn_a_Wk"]), "WvT": tr(g["attn_a_Wv"]), "WoT": tr(g["attn_a_Wo"]),
         "bq": g["attn_a_bq"], "bk": g["attn_a_bk"], "bv": g["attn_a_bv"], "bo": g["attn_a_bo"],
         "ln_g": g["attn_a_ln_g"], "ln_b": g["attn_a_ln_b"], "WoutT": tr(g["attn_a_Wout"]),
         "bout": g["attn_a_bout"], "ln2_g": g["attn_a_ln2_g"], "ln2_b": g["attn_a_ln2_b"],
         "bWqkv": g["attn_b_Wqkv"], "bWout": g["attn_b_Wout"],
         "lWqkv": wrap(g["ffn_Wqkv"]), "lWvT": wrap(wvt), "lWo": wrap(g["ffn_Wo"]),
         "q_scale": wrap(g["ffn_q_scale"]), "k_scale": wrap(g["ffn_k_scale"]),
         "lg": g["ffn_ln_g"], "lb": g["ffn_ln_b"], "lW1": g["ffn_W1"], "lb1": g["ffn_b1"],
         "lW2": g["ffn_W2"], "lb2": g["ffn_b2"]}
    return {**d, **constants()}


def kernel(**inputs):
    import concourse.bacc as bacc
    from concourse.bass_utils import run_bass_kernel_spmd

    nc = bacc.Bacc("TRN2", target_bir_lowering=False, num_devices=1)
    data = {"in_" + k: np.ascontiguousarray(v) for k, v in arrays(inputs).items()}
    t = {k[3:]: nc.dram_tensor(k, v.shape, mybir.dt.from_np(v.dtype), kind="ExternalInput").ap() for k, v in data.items()}
    out = nc.dram_tensor("out", (P, TOK), F32, kind="ExternalOutput").ap()
    scratch = nc.dram_tensor("scratch", (2, 3, P, SEQ), BF16, kind="Internal").ap()
    t = {k: ap.bitcast(BF16) if k in BF16_CONSTANTS else ap for k, ap in t.items()}
    build(nc, t, out, scratch)
    r = run_bass_kernel_spmd(nc, [data], core_ids=[0])
    y = r.results[0]["out"]
    return np.ascontiguousarray(y.T).reshape(BATCH, SEQ, P)
```

```python
from contextlib import ExitStack

import numpy as np

import concourse.bass as bass
from concourse import mybir

F32 = mybir.dt.float32
BF16 = mybir.dt.bfloat16
ALU = mybir.AluOpType
ACT = mybir.ActivationFunctionType
AX = mybir.AxisListType

P = 128
BATCH, SEQ = 2, 1024
TOK = BATCH * SEQ
HEADS, HD = 16, 8
QT = SEQ // P
QUADS = HEADS // 4
SCALES = 3
DEPTH = 6
TILES = BATCH * QT
LH, LD = 16, 64
INNER = LH * LD
WIN = 32
HID = 341
HCH = [(0, 128), (128, 128), (256, 85)]
XW_COLS = WIN + 1 + SEQ
LN_EPS = 1e-5
CH = 512
NEG = -1e30
START = 1

COMBO_Q = [0, 0, 0, 1, 1, 2]
COMBO_K = [0, 1, 2, 0, 1, 0]
MROW = 8 * len(COMBO_Q)
AROW = MROW + 3
CROWS = 9

STEPS = [(c, kt, max(CH * c, P * kt), CH * (c + 1) - max(CH * c, P * kt))
         for c in range(2) for kt in range(4 * c + 4)]
NSTEP = len(STEPS)
S2_BANKS = (4, 5, 7, 0, 1, 2)


def quad_order():
    first = [(j, qt) for j in range(4) for qt in range(QT)]
    cost1 = [P * (qt + 1) for _, qt in first]
    total1, total2 = sum(cost1), 4 * sum(w for *_, w in STEPS)
    out, done1, done2, at = [], 0, 0, 0
    for s, (_, _, _, w) in enumerate(STEPS):
        for j in range(4):
            while at < len(first) and done1 * total2 <= done2 * total1:
                out.append(("first", *first[at]))
                done1 += cost1[at]
                at += 1
            out.append(("second", s, j))
            done2 += w
        if s:
            out.append(("values", s - 1, 0))
    out += [("first", *f) for f in first[at:]]
    out.append(("values", NSTEP - 1, 0))
    return out


ORDER = quad_order()
PLAN = (("causal", "a"), ("layers", 0), ("causal", "b"), ("layers", 1))


def build(nc, t, out, scratch):
    with ExitStack() as ctx:
        def sb(name, shape, dt=F32, stack=ctx):
            return stack.enter_context(nc.sbuf_tensor(name, shape, dt))

        names = {}

        def sem(name):
            if name not in names:
                names[name] = ctx.enter_context(nc.semaphore(name))
            return names[name]

        ps = ctx.enter_context(nc.psum_tensor("ps", [P, 8, CH], F32))

        res = sb("res", [P, TOK])
        ident = sb("ident", [P, P])
        identb = sb("identb", [P, P], BF16)
        mean_w = sb("mean_w", [P, P])
        ones_w = sb("ones_w", [P, P])
        eps_col = sb("eps_col", [P, 1])
        lnc = sb("lnc", [P, SEQ])
        lnq = sb("lnq", [P, SEQ])
        dev8 = sb("dev8", [P, 2, QT])
        rdev8 = sb("rdev8", [P, 2, QT])
        step = sem("step")
        const_in = sem("const_in")
        out_done = sem("out_done")

        PLACE = (step, 6, 2, lnc[:], lnq[:])
        wide = ps[:, 6:8, :].rearrange("p x n -> p (x n)")

        def pair(bank):
            return ps[:, bank:bank + 2, :].rearrange("p x n -> p (x n)")

        def ln_mean(pe, k, src, place):
            chain, bank, v, centred, squares = place
            pe.wait_ge(chain, k)
            for x in range(2):
                last = nc.tensor.matmul(ps[:, bank + x, :], mean_w[:], src[:, x * CH:(x + 1) * CH], start=True, stop=True)
            last.then_inc(chain, 1)

        def ln_variance(pe, k, place):
            chain, bank, v, centred, squares = place
            pe.wait_ge(chain, k + 3)
            for x in range(QT):
                last = nc.tensor.matmul(ps[:, v, x:x + 1], squares[:, x * P:(x + 1) * P], mean_w[:, 0:1], start=True, stop=True)
            last.then_inc(chain, 1)

        def ln_spread(pe, k, place):
            chain, bank, v, centred, squares = place
            pe.wait_ge(chain, k + 7)
            for x in range(2):
                last = nc.tensor.matmul(ps[:, bank + x, :], ones_w[:], squares[:, x * CH:(x + 1) * CH], start=True, stop=True)
            last.then_inc(chain, 1)

        def ln_square(act, k, place):
            chain, bank, v, centred, squares = place
            act.wait_ge(chain, k + 2)
            nc.scalar.activation(squares, centred, ACT.Square).then_inc(chain, 1)

        def ln_deviation(act, k, place):
            chain, bank, v, centred, squares = place
            act.wait_ge(chain, k + 4)
            nc.scalar.activation(dev8[:, v - 2, :], ps[:, v, 0:QT], ACT.Sqrt, bias=eps_col[:, 0:1]).then_inc(chain, 1)

        def ln_centre(dve, k, src, place):
            chain, bank, v, centred, squares = place
            dve.wait_ge(chain, k + 1)
            nc.vector.tensor_tensor(centred, src, pair(bank), ALU.subtract).then_inc(chain, 1)

        def ln_factors(dve, k, place):
            chain, bank, v, centred, squares = place
            dve.wait_ge(chain, k + 5)
            nc.vector.reciprocal(rdev8[:, v - 2, :], dev8[:, v - 2, :]).then_inc(chain, 1)
            dve.wait_ge(chain, k + 6)
            nc.vector.tensor_tensor(squares.rearrange("p (x n) -> p x n", n=P), ident[:].unsqueeze(1).to_broadcast([P, QT, P]),
                                    rdev8[:, v - 2, :].unsqueeze(2).to_broadcast([P, QT, P]), ALU.mult).then_inc(chain, 1)

        def ln_scale(dve, k, dst, place, gain=None, shift=None):
            chain, bank, v, centred, squares = place
            dve.wait_ge(chain, k + 8)
            if gain is None:
                nc.vector.tensor_tensor(dst, centred, pair(bank), ALU.mult).then_inc(chain, 2)
            else:
                nc.vector.tensor_tensor(centred, centred, pair(bank), ALU.mult).then_inc(chain, 1)
                dve.wait_ge(chain, k + 9)
                nc.vector.tensor_scalar(dst, centred, gain, shift, ALU.mult, ALU.add).then_inc(chain, 1)

        def ln_pe(pe, k, src):
            ln_mean(pe, k, src, PLACE)
            ln_variance(pe, k, PLACE)
            ln_spread(pe, k, PLACE)

        def ln_act(act, k):
            ln_square(act, k, PLACE)
            ln_deviation(act, k, PLACE)

        def ln_dve(dve, k, src, dst, gain, shift):
            ln_centre(dve, k, src, PLACE)
            ln_factors(dve, k, PLACE)
            ln_scale(dve, k, dst, PLACE, gain, shift)

        LN = 10

        def stream_norm(block, second, dsts):
            other = sem("other_step")
            places = [PLACE, (other, 4, 3, *second)]
            ks = [at[0], other_at[0]]
            at[0] += LN
            other_at[0] += LN
            both = list(zip(ks, places))
            srcs = [res[:, u * SEQ:(u + 1) * SEQ] for u in range(BATCH)]

            @block.tensor
            def _(pe):
                for (k, place), src in zip(both, srcs):
                    ln_mean(pe, k, src, place)
                for k, place in both:
                    ln_variance(pe, k, place)
                for k, place in both:
                    ln_spread(pe, k, place)

            @block.scalar
            def _(act):
                for k, place in both:
                    ln_square(act, k, place)
                for k, place in both:
                    ln_deviation(act, k, place)

            @block.vector
            def _(dve):
                for (k, place), src in zip(both, srcs):
                    ln_centre(dve, k, src, place)
                for k, place in both:
                    ln_factors(dve, k, place)
                for (k, place), dst in zip(both, dsts):
                    if len(dst) == 1:
                        ln_scale(dve, k, dst[0], place)
                    else:
                        dve.wait_ge(place[0], k + 8)
                        for half, to in enumerate(dst):
                            rows = slice(64 * half, 64 * half + 64)
                            ins = nc.vector.tensor_tensor(to, place[3][rows], pair(place[1])[rows], ALU.mult)
                        ins.then_inc(place[0], 2)

        at = [0]
        other_at = [0]

        with nc.Block() as block:
            @block.sync
            def _(sp):
                sp.dma_start(res[:], t["x"]).then_inc(const_in, 16)
                sp.dma_start(ident[:], t["ident"]).then_inc(const_in, 16)
                sp.dma_start(identb[:], t["identb"]).then_inc(const_in, 16)
                sp.wait_ge(const_in, 48)

            @block.gpsimd
            def _(pool):
                nc.gpsimd.memset(mean_w[:], 1.0 / P)
                nc.gpsimd.memset(ones_w[:], 1.0)
                nc.gpsimd.memset(eps_col[:], LN_EPS)

        def causal(kind):
            with ExitStack() as local:
                def lb(name, shape, dt=F32):
                    return sb(f"{kind}_{name}", shape, dt, local)

                xl = lb("xl", [P, TOK])
                qs = [lb(f"qs{i}", [P, HEADS, SEQ], BF16) for i in range(2)]
                ks = [lb(f"ks{i}", [P, HEADS, SEQ], BF16) for i in range(2)]
                vrow = lb("vrow", [P, QT, P])
                vq = lb("vq", [P, QT, 4, 32])
                pt = lb("pt", [P, 2, 4, CH])
                nm = lb("nm", [P, P])
                ot = lb("ot", [P, QUADS, SEQ])
                mask_q = lb("mask_q", [P, P], BF16)
                mask_k = lb("mask_k", [P, P], BF16)
                wts = lb("wts", [P, 2, 3, P])
                wo = lb("wo", [P, P])
                wout = lb("wout", [P, P])
                bqk = lb("bqk", [P, 2, 2])
                cols = lb("cols", [P, 3])
                cols2 = lb("cols2", [P, 3])
                bvb = lb("bvb", [P, P])
                flat = pt[:, :, :, :].rearrange("p a b c -> p (a b c)")
                qkf = [flat[:, 0:SEQ], flat[:, SEQ:2 * SEQ]]
                rest = [flat[:, 2 * SEQ:3 * SEQ], flat[:, 3 * SEQ:4 * SEQ]]
                parts = ot[:, :, :].rearrange("p q n -> p (q n)")[:, 0:3 * SEQ].bitcast(BF16).rearrange("p (a c n) -> p a c n", a=2, c=3)
                onm = ot[:, 3, :].rearrange("p (x n) -> p x n", n=P)
                mparts = lb("mparts", [P, 3, P], BF16)
                mrest = lb("mrest", [P, P])
                den = lb("den", [P, QT, HEADS])
                rden = lb("rden", [P, QT, HEADS])
                acc = lb("acc", [P, SEQ])

                scales = SCALES if kind == "a" else 1
                units = [(s, b) for b in range(BATCH) for s in range(scales)]
                qscale = float(HD) ** (0.5 if kind == "a" else -0.5)
                den_eps = 1e-6 if kind == "a" else 0.0
                k = kind
                setup_in, w_in, stack_in = sem(k + "setup_in"), sem(k + "w_in"), sem(k + "stack_in")
                part_out = [sem(k + "q_part_out"), sem(k + "k_part_out")]
                s1_ready, s1_free = sem(k + "s1_ready"), sem(k + "s1_free")
                s2_ready, s2_free = sem(k + "s2_ready"), sem(k + "s2_free")
                pt_free = sem(k + "pt_free")
                ot_free = sem(k + "ot_free")
                vq_ready = sem(k + "vq_ready")

                with nc.Block() as block:
                    @block.sync
                    def _(sp):
                        sp.dma_start(mask_q[:], t["mask_q"]).then_inc(setup_in, 16)
                        sp.dma_start(mask_k[:], t["mask_k"]).then_inc(setup_in, 16)
                        n = 32
                        if kind == "a":
                            for i, name in enumerate(("bout", "ln2_g", "ln2_b")):
                                sp.dma_start(cols2[:, i:i + 1], t[name].rearrange("(p a) -> p a", a=1)).then_inc(setup_in, 16)
                                n += 16
                        sp.wait_ge(setup_in, n)

                    @block.gpsimd
                    def _(pool):
                        nc.gpsimd.memset(vq[:, :, :, :], 0.0).then_inc(vq_ready, 1)
                        pool.wait_ge(vq_ready, 1)
                        nc.gpsimd.memset(vq[:, :, :, HD:HD + 1], 1.0)
                        for one in (s1_free, s2_free, pt_free, ot_free):
                            pool.sem_inc(one, START)
                        if kind == "b":
                            nc.gpsimd.memset(bqk[:, :, :], 0.0)
                            nc.gpsimd.memset(bvb[:], 0.0)

                    @block.vector
                    def _(dve):
                        nc.vector.memset(nm[:], 0.0).then_inc(s1_free, 3)

                    @block.scalar
                    def _(act):
                        nc.scalar.activation(lnc[:, 0:1], eps_col[:], ACT.Copy).then_inc(s2_free, 2)

                    @block.tensor
                    def _(pe):
                        nc.tensor.matmul(ps[:, 0, 0:P], ident_b(), ident_b(), start=True, stop=True).then_inc(pt_free, 1)

                loaded, stacked, parted = [0], [0], [0, 0]

                def load(sp, dst, src):
                    loaded[0] += 16
                    sp.dma_start(dst, src).then_inc(w_in, 16)

                def load_ahead(sp, i):
                    for n in (0, 1) if i < 0 else (i + 1,) if 0 < i < len(units) - 1 else ():
                        if kind == "a":
                            s = units[n][0]
                            for a, name in enumerate(("WqT", "WkT", "WvT")):
                                load(sp, wts[:, n % 2, a, :], t[name][s])
                            for a, name in enumerate(("bq", "bk")):
                                load(sp, bqk[:, n % 2, a:a + 1], t[name][s].rearrange("(p a) -> p a", a=1))
                    if 0 <= i < len(units) and kind == "a":
                        load(sp, bvb[:], t["bv"][units[i][0]:units[i][0] + 1, :].to_broadcast([P, P]))
                    if i >= 1 and kind == "a":
                        s = units[i - 1][0]
                        load(sp, wo[:], t["WoT"][s])
                        load(sp, wout[:], t["WoutT"][s * P:(s + 1) * P, :])
                        for n, name in enumerate(("bo", "ln_g", "ln_b")):
                            load(sp, cols[:, n:n + 1], t[name][s].rearrange("(p a) -> p a", a=1))
                    if i < 0 and kind == "b":
                        load(sp, wts[:, 0, :, :], t["bWqkv"].rearrange("p (a n) -> p a n", a=3))
                        load(sp, wo[:], t["bWout"])

                def stack(sp, dst, src):
                    stacked[0] += 16
                    sp.dma_start(dst, src).then_inc(stack_in, 16)

                zeroed = sem(k + "zeroed")
                with nc.Block() as block:
                    @block.gpsimd
                    def _(pool):
                        for i in range(2):
                            nc.gpsimd.memset(qs[i][:, :, :].bitcast(F32), 0.0).then_inc(zeroed, 1)
                            nc.gpsimd.memset(ks[i][:, :, :].bitcast(F32), 0.0).then_inc(zeroed, 1)

                    @block.sync
                    def _(sp):
                        load_ahead(sp, -1)
                        for i in range(2):
                            for a, (to, name) in enumerate(((qs[i], "crow_q"), (ks[i], "crow_k"))):
                                sp.wait_ge(zeroed, 2 * i + a + 1)
                                stack(sp, to[MROW:MROW + CROWS, :, :], t[name + kind])

                    stream_norm(block, (flat[:, 0:SEQ], flat[:, SEQ:2 * SEQ]), [(xl[:, u * SEQ:(u + 1) * SEQ],) for u in range(BATCH)])

                chains = {n: sem(k + n + "_step") for n in ("q", "k", "m", "v")}
                stood = dict.fromkeys(chains, 0)

                def between(i, prepares):
                    now = units[i] if 0 <= i < len(units) else None
                    after = units[prepares] if prepares is not None and prepares < len(units) else None
                    before = units[i - 1] if i >= 1 else None
                    par, par_after = i % 2, (prepares or 0) % 2
                    w_now, w_after = (par, par_after) if kind == "a" else (0, 0)
                    z, e0 = dict(stood), at[0]
                    if now:
                        stood["m"] += 5
                        stood["v"] += 2
                    if after:
                        stood["q"] += 6
                        stood["k"] += 6
                    last_scale = bool(before) and kind == "a" and before[0] == scales - 1
                    kln = e0 + 8
                    if before:
                        at[0] += 8 + (LN + 2 if kind == "a" else 0) + (LN + 2 if last_scale else 0)
                    with nc.Block() as block:
                        @block.sync
                        def _(sp):
                            if now:
                                sp.wait_ge(chains["m"], z["m"] + 5)
                                for c in range(3):
                                    stack(sp, qs[par][MROW + c:MROW + c + 1, :, :].rearrange("p h (q n) -> p (h q) n", n=P), mparts[:, c, :])
                            if after:
                                if prepares >= 2:
                                    stack(sp, qs[par_after][MROW:MROW + 3, :, :], t["crow_q" + kind][0:3])
                                for a in range(2):
                                    sp.wait_ge(chains["qk"[a]], z["qk"[a]] + 6)
                                    sp.dma_start(scratch[par_after, a].rearrange("c p n -> p c n"), parts[:, a, :, :]).then_inc(part_out[a], 16)
                                for a, (combo, to) in enumerate(((COMBO_Q, qs[par_after]), (COMBO_K, ks[par_after]))):
                                    parted[a] += 16
                                    sp.wait_ge(part_out[a], parted[a])
                                    for g, c in enumerate(combo):
                                        stack(sp, to[8 * g:8 * g + 8, :, :], scratch[par_after, a, c].rearrange("(h d) n -> d h n", d=HD))

                        @block.tensor
                        def _(pe):
                            if now:
                                nc.tensor.transpose(ps[:, 0, 0:P], nm[:], ident[:]).then_inc(chains["m"], 1)
                            if before:
                                for x in (*range(1, QT), 0):
                                    if x == 0 and now:
                                        pe.wait_ge(chains["m"], z["m"] + 3)
                                    for q in range(QUADS):
                                        last = nc.tensor.transpose(ps[:, x, q * P:(q + 1) * P], ot[:, q, x * P:(x + 1) * P], ident[:])
                                last.then_inc(step, 1)
                                pe.wait_ge(step, e0 + 4)
                            if now or after:
                                pe.wait_ge(w_in, loaded[0])
                            if after:
                                if now and not before:
                                    pe.wait_ge(chains["m"], z["m"] + 3)
                                for a in range(2):
                                    for c in range(2):
                                        last = nc.tensor.matmul(ps[:, 2 * a + c, :], wts[:, w_after, a, :],
                                                                xl[:, after[1] * SEQ + c * CH:after[1] * SEQ + (c + 1) * CH],
                                                                start=True, stop=True)
                                    last.then_inc(chains["qk"[a]], 1)
                            if before:
                                for x in range(QT):
                                    last = nc.tensor.transpose(ps[:, 6 + x // 4, x % 4 * P:(x % 4 + 1) * P], onm[:, x, :], ident[:])
                                last.then_inc(step, 1)
                            if now:
                                for kt in range(QT):
                                    last = nc.tensor.matmul(ps[:, 4 + kt // 4, (kt % 4) * P:(kt % 4 + 1) * P],
                                                            xl[:, now[1] * SEQ + kt * P:now[1] * SEQ + (kt + 1) * P], wts[:, w_now, 2, :],
                                                            start=True, stop=True)
                                last.then_inc(chains["v"], 1)
                            if before:
                                pe.wait_ge(w_in, loaded[0])
                                pe.wait_ge(step, e0 + 6)
                                for x in range(2):
                                    last = nc.tensor.matmul(ps[:, 6 + x, :], wo[:], lnq[:, x * CH:(x + 1) * CH], start=True, stop=True)
                                last.then_inc(step, 1)
                                if kind == "a":
                                    if after:
                                        pe.wait_ge(chains["k"], z["k"] + 2)
                                    ln_pe(pe, kln, lnc)
                                    pe.wait_ge(step, kln + LN)
                                    for x in range(2):
                                        last = nc.tensor.matmul(ps[:, 6 + x, :], wout[:], lnc[:, x * CH:(x + 1) * CH], start=True, stop=True)
                                    last.then_inc(step, 1)
                                if last_scale:
                                    ln_pe(pe, kln + LN + 3, lnc)

                        @block.scalar
                        def _(act):
                            def part(a, n):
                                act.wait_ge(chains["qk"[a]], z["qk"[a]] + 2 + 2 * n)
                                nc.scalar.activation(parts[:, a, n, :], (rest if n else qkf)[a], ACT.Copy).then_inc(chains["qk"[a]], 1)

                            if after:
                                part(0, 0)
                                part(1, 0)
                            if before:
                                act.wait_ge(step, e0 + 5)
                                nc.scalar.activation(lnq[:], wide, ACT.Copy).then_inc(step, 1)
                            if after:
                                part(0, 1)
                                part(1, 1)
                            if before and kind == "a":
                                ln_act(act, kln)
                            if last_scale:
                                ln_act(act, kln + LN + 3)

                        @block.vector
                        def _(dve):
                            if now:
                                mz = z["m"]
                                dve.wait_ge(chains["m"], mz + 1)
                                nc.vector.tensor_copy(mparts[:, 0, :], ps[:, 0, 0:P]).then_inc(chains["m"], 1)
                                dve.wait_ge(chains["m"], mz + 2)
                                nc.vector.tensor_tensor(mrest[:], ps[:, 0, 0:P], mparts[:, 0, :], ALU.subtract).then_inc(chains["m"], 1)
                                dve.wait_ge(chains["m"], mz + 3)
                                nc.vector.tensor_copy(mparts[:, 1, :], mrest[:]).then_inc(chains["m"], 1)
                                dve.wait_ge(chains["m"], mz + 4)
                                nc.vector.tensor_tensor(mparts[:, 2, :], mrest[:], mparts[:, 1, :], ALU.subtract).then_inc(chains["m"], 1)
                            if before:
                                turned = ps[:, :, :].rearrange("p x (h d) -> p x h d", d=32)
                                dve.wait_ge(step, e0 + 1)
                                nc.vector.tensor_scalar(den[:, :, :], turned[:, :, :, HD], den_eps, None, ALU.add).then_inc(step, 1)
                                dve.wait_ge(step, e0 + 2)
                                nc.vector.reciprocal(rden[:, :, :], den[:, :, :]).then_inc(step, 1)
                                dve.wait_ge(step, e0 + 3)
                                nc.vector.tensor_tensor(onm[:, :, :].rearrange("p x (h d) -> p x h d", d=HD), turned[:, :, :, 0:HD],
                                                        rden[:, :, :].unsqueeze(3).to_broadcast([P, QT, HEADS, HD]), ALU.mult).then_inc(step, 1)
                            if now or after:
                                dve.wait_ge(w_in, loaded[0])

                            def scale(a):
                                dve.wait_ge(chains["qk"[a]], z["qk"[a]] + 1)
                                nc.vector.tensor_scalar(qkf[a].rearrange("p (c n) -> p c n", c=2), ps[:, 2 * a:2 * a + 2, :],
                                                        bqk[:, w_after, a:a + 1], qscale if a == 0 else 1.0,
                                                        ALU.add, ALU.mult).then_inc(chains["qk"[a]], 1)

                            def subtract(a, n):
                                dve.wait_ge(chains["qk"[a]], z["qk"[a]] + 3 + 2 * n)
                                nc.vector.tensor_tensor(parts[:, a, 2, :] if n else rest[a], (rest if n else qkf)[a],
                                                        parts[:, a, n, :], ALU.subtract).then_inc(chains["qk"[a]], 1)

                            if after:
                                scale(0)
                                scale(1)
                                subtract(0, 0)
                                subtract(1, 0)
                            if now:
                                dve.wait_ge(chains["v"], z["v"] + 1)
                                nc.vector.tensor_tensor(vrow[:, :, :], ps[:, 4:6, :].rearrange("p a (t n) -> p (a t) n", n=P),
                                                        bvb[:].unsqueeze(1).to_broadcast([P, QT, P]), ALU.add).then_inc(chains["v"], 1)
                            if after:
                                subtract(0, 1)
                                subtract(1, 1)
                            if not before:
                                return
                            sl = slice(before[1] * SEQ, (before[1] + 1) * SEQ)
                            dve.wait_ge(step, e0 + 7)
                            if kind == "b":
                                nc.vector.tensor_tensor(res[:, sl], res[:, sl], wide, ALU.add).then_inc(step, 1)
                                return
                            nc.vector.tensor_scalar(lnc[:], wide, cols[:, 0:1], None, ALU.add).then_inc(step, 1)
                            ln_dve(dve, kln, lnc[:], lnc[:], cols[:, 1:2], cols[:, 2:3])
                            dve.wait_ge(step, kln + LN + 1)
                            if before[0] == 0:
                                nc.vector.tensor_copy(acc[:], wide).then_inc(step, 1)
                            else:
                                nc.vector.tensor_tensor(acc[:], wide, acc[:], ALU.add).then_inc(step, 1)
                            if last_scale:
                                dve.wait_ge(step, kln + LN + 2)
                                nc.vector.tensor_scalar(lnc[:], acc[:], cols2[:, 0:1], None, ALU.add).then_inc(step, 1)
                                ln_dve(dve, kln + LN + 3, lnc[:], lnc[:], cols2[:, 1:2], cols2[:, 2:3])
                                dve.wait_ge(step, kln + 2 * LN + 3)
                                nc.vector.tensor_tensor(res[:, sl], res[:, sl], lnc[:], ALU.add).then_inc(step, 1)

                between(-1, 0)
                between(-1, 1)
                for i in range(len(units) + 1):
                    now = units[i] if i < len(units) else None
                    before = units[i - 1] if i else None

                    par1, par2 = i % 2, (i + 1) % 2
                    b2 = before[1] if before else 0
                    with nc.Block() as block:
                        @block.sync
                        def _(sp):
                            load_ahead(sp, i)

                        @block.gpsimd
                        def _(pool):
                            if not before:
                                return
                            u = i - 1
                            with pool.Fori(0, QUADS) as quad:
                                pool.wait_ge(pt_free, NSTEP * (4 * u + quad) + 1 + START)
                                nc.gpsimd.tensor_copy(vq[:, :, :, 0:HD],
                                                      vrow[:, :, bass.ds(quad * 4 * HD, 4 * HD)].rearrange("p t (j d) -> p t j d", d=HD)
                                                      ).then_inc(vq_ready, 1)

                        @block.tensor
                        def _(pe):
                            pe.wait_ge(stack_in, stacked[0])
                            with pe.Fori(0, QUADS) as quad:
                                n1 = (4 * i + quad) * 4 * QT
                                u = i - 1
                                n2 = (4 * u + quad) * 4 * NSTEP
                                nst = (4 * u + quad) * NSTEP
                                seen1 = seen2 = 0
                                for what, x, y in ORDER:
                                    if what == "first":
                                        if not now:
                                            continue
                                        j, qt = x, y
                                        bank = 2 * (seen1 % (2 if before else 4))
                                        lhs = qs[par1][:, bass.ds(quad * 4 + j, 1), qt * P:(qt + 1) * P]
                                        pe.wait_ge(s1_free, n1 + seen1 + (2 if before else 0) + START)
                                        cols_n = P * (qt + 1)
                                        last = None
                                        for h in range(0, cols_n, CH):
                                            w = min(CH, cols_n - h)
                                            diag = h + w == cols_n
                                            last = nc.tensor.matmul(ps[:, bank + h // CH, 0:w], lhs,
                                                                    ks[par1][:, bass.ds(quad * 4 + j, 1), h:h + w],
                                                                    start=True, stop=not diag)
                                        e = cols_n - P
                                        last = nc.tensor.matmul(ps[:, bank + e // CH, e % CH:e % CH + P], identb[:], mask_q[:],
                                                                start=False, stop=True)
                                        last.then_inc(s1_ready, 1)
                                        seen1 += 1
                                    elif not before:
                                        continue
                                    elif what == "second":
                                        c, kt, q0, w = STEPS[x]
                                        j = y
                                        bank = S2_BANKS[seen2 % (3 if now else 6)]
                                        pe.wait_ge(s2_free, n2 + seen2 - (0 if now else 3) + START)
                                        diag = q0 == kt * P
                                        last = nc.tensor.matmul(ps[:, bank, 0:w], ks[par2][:, bass.ds(quad * 4 + j, 1), kt * P:(kt + 1) * P],
                                                                qs[par2][:, bass.ds(quad * 4 + j, 1), q0:q0 + w],
                                                                start=True, stop=not diag)
                                        if diag:
                                            last = nc.tensor.matmul(ps[:, bank, 0:P], identb[:], mask_k[:], start=False, stop=True)
                                        last.then_inc(s2_ready, 1)
                                        seen2 += 1
                                    else:
                                        c, kt, q0, w = STEPS[x]
                                        if x == 0:
                                            pe.wait_ge(vq_ready, 4 * u + quad + 2)
                                        if kt == 0:
                                            pe.wait_ge(ot_free, 2 * (4 * u + quad) + c + START)
                                        pe.wait_ge(s2_free, n2 + 4 * x + 6 + START)
                                        for j in range(4):
                                            last = nc.tensor.matmul(ps[32 * j:32 * j + 32, 6, q0 - c * CH:q0 - c * CH + w],
                                                                    vq[:, kt, j, :], pt[:, x % 2, j, 0:w],
                                                                    start=kt == 0, stop=kt == 4 * c + 3)
                                        last.then_inc(pt_free, 1)

                        @block.vector
                        def _(dve):
                            with dve.Fori(0, QUADS) as quad:
                                n1 = (4 * i + quad) * 4 * QT
                                u = i - 1
                                if now:
                                    seen1 = 0
                                    for what, x, y in ORDER:
                                        if what != "first":
                                            continue
                                        j, qt = x, y
                                        bank = 2 * (seen1 % (2 if before else 4))
                                        dve.wait_ge(s1_ready, n1 + seen1 + 1)
                                        flat1 = ps[:, bank:bank + 2, :].rearrange("p a n -> p (a n)")
                                        nc.vector.tensor_reduce(nm[:, bass.ds(quad * 32 + j * QT + qt, 1)], flat1[:, 0:P * (qt + 1)],
                                                                AX.X, ALU.max, negate=True).then_inc(s1_free, 1)
                                        seen1 += 1
                                if before:
                                    dve.wait_ge(pt_free, NSTEP * (4 * u + quad + 1) + 1 + START)
                                    nc.vector.tensor_copy(ot[:, bass.ds(quad, 1), CH:2 * CH], ps[:, 6, :]).then_inc(ot_free, 1)

                        @block.scalar
                        def _(act):
                            if not before:
                                return
                            with act.Fori(0, QUADS) as quad:
                                u = i - 1
                                n2 = (4 * u + quad) * 4 * NSTEP
                                nst = (4 * u + quad) * NSTEP
                                seen2 = 0
                                for x, (c, kt, q0, w) in enumerate(STEPS):
                                    act.wait_ge(pt_free, nst + x + START)
                                    for j in range(4):
                                        act.wait_ge(s2_ready, n2 + seen2 + 1)
                                        nc.scalar.activation(pt[:, x % 2, j, 0:w], ps[:, S2_BANKS[seen2 % (3 if now else 6)], 0:w], ACT.Exp).then_inc(s2_free, 1)
                                        seen2 += 1
                                    if x == 4:
                                        act.wait_ge(pt_free, nst + 4 + 1 + START)
                                        nc.scalar.activation(ot[:, bass.ds(quad, 1), 0:CH], ps[:, 6, :], ACT.Copy).then_inc(ot_free, 1)

                    between(i, i + 1 if i else None)

        def ident_b():
            return identb[:]

        def layers(call):
            with ExitStack() as local:
                def lb(name, shape, dt=F32):
                    return sb(f"l{call}_{name}", shape, dt, local)

                xa = lb("xa", [P, BATCH, XW_COLS])
                xb = lb("xb", [P, BATCH, XW_COLS])
                wqk = lb("wqk", [P, 2 * INNER])
                wvt = lb("wvt", [P, LH // 2, P])
                wo = lb("wo", [P, LH // 2, P])
                mh = lb("mh", [P, LH, P])
                w1 = lb("w1", [P, 2 * HID])
                w2 = lb("w2", [P, 3, P])
                b1 = lb("b1", [P, 2, 3])
                gcols = lb("gcols", [P, 3])
                base = lb("base", [P, 4, QT, LD])
                tab = lb("tab", [P, 4, QT, LD])
                sc = lb("sc", [P, 2, LD])
                lmask = lb("lmask", [P, QT, 2 * WIN], BF16)
                sq = lb("sq", [P, 2, INNER])
                rc = lb("rc", [P, 2, INNER])
                rs = lb("rs", [P, 2, INNER])
                turns = [[rc[:, 0, :], rc[:, 1, :]], [lnc[:], lnq[:]]]
                qkn = lb("qkn", [P, 2, INNER])
                ss = lb("ss", [P, 2, LH])
                rn = lb("rn", [P, 2, LH])
                qt_ = lb("qt", [P, 2, LH // 2, P])
                kt_ = lb("kt", [P, LH // 2, WIN + SEQ])
                mx = lb("mx", [P, LH])
                pe_ = lb("pe", [P, LH, 2 * WIN])
                pn = lb("pn", [P, LH, 2 * WIN])
                rl = lb("rl", [P, LH])
                lsum = lb("lsum", [P, LH])
                ptl = lb("ptl", [P, LH // 2, P])
                xw = lb("xw", [P, 4, 2, P])
                yb = lb("yb", [P, LH, CH])
                dev = lb("dev", [P, BATCH, QT])
                rdev = lb("rdev", [P, BATCH, QT])
                ybf = yb[:, :, :].rearrange("p h n -> p (h n)")
                gl, hh = (ybf[:, BATCH * SEQ + x * 6 * CH:BATCH * SEQ + (x + 1) * 6 * CH].rearrange("p (c g n) -> p c g n", c=2, g=3) for x in range(2))

                c = f"l{call}"
                lin = sem(c + "in")
                a_in, m_in = sem(c + "attn_w_in"), sem(c + "mlp_w_in")
                def load_attn(sp, L):
                    sp.dma_start(wqk[:], t["lWqkv"][bass.ds(L, 1), :, 0:2 * INNER]).then_inc(a_in, 16)
                    sp.dma_start(wvt[:, :, :], t["lWvT"][bass.ds(L, 1)]).then_inc(a_in, 16)
                    sp.dma_start(wo[:, :, :], t["lWo"][bass.ds(L, 1)].rearrange("a (g p) o -> p (a g) o", p=P)).then_inc(a_in, 16)
                    sp.dma_start(sc[:, 0, :], t["q_scale"][bass.ds(L, 1), :].to_broadcast([P, LD])).then_inc(a_in, 16)
                    sp.dma_start(sc[:, 1, :], t["k_scale"][bass.ds(L, 1), :].to_broadcast([P, LD])).then_inc(a_in, 16)

                A_IN = 80

                def load_mlp(sp, L):
                    sp.dma_start(w1[:], t["lW1"][bass.ds(L, 1)]).then_inc(m_in, 16)
                    sp.dma_start(w2[:, 0:2, :], t["lW2"][bass.ds(L, 1), 0:2 * P, :].rearrange("a (g p) o -> p (a g) o", p=P)).then_inc(m_in, 16)
                    sp.dma_start(w2[0:85, 2, :], t["lW2"][bass.ds(L, 1), 2 * P:HID, :].rearrange("a p o -> p (a o)")).then_inc(m_in, 16)
                    for half in range(2):
                        for n, (h0, w) in enumerate(HCH):
                            sp.dma_start(b1[0:w, half, n:n + 1], t["lb1"][bass.ds(L, 1), half * HID + h0:half * HID + h0 + w].rearrange("a (p n) -> p (a n)", n=1)).then_inc(m_in, 16)
                    for n, name in enumerate(("lg", "lb", "lb2")):
                        sp.dma_start(gcols[:, n:n + 1], t[name][bass.ds(L, 1)].rearrange("a (p n) -> p (a n)", n=1)).then_inc(m_in, 16)

                M_IN = 12 * 16

                with nc.Block() as block:
                    @block.sync
                    def _(sp):
                        sp.dma_start(base[:, :, :, :], t["rot"]).then_inc(lin, 16)
                        sp.dma_start(lmask[:, :, :], t["lmask"]).then_inc(lin, 16)
                        load_attn(sp, 0)

                    @block.vector
                    def _(dve):
                        nc.vector.memset(xa[:, :, :], 0.0)
                        nc.vector.memset(xb[:, :, :], 0.0)
                        nc.vector.memset(kt_[:, :, 0:WIN], 0.0)
                        nc.vector.memset(xw[:, :, :, :], 0.0)

                M = {n: sem(c + n) for n in (
                    "mean_ready", "centred", "squared", "var_ready", "dev_done", "rdev_done", "diag_done", "spread_ready", "scaled",
                    "xn_done", "gate_ready", "a_ready", "gelu_done", "h_done", "w2_ready", "out_done")}
                S = {n: sem(c + n) for n in (
                    *(what + of for what in "qk" for of in ("_ready", "_squared", "_summed", "_read", "_rotated", "_unit", "_turned", "_placed")),
                    "sd_done", "rmax_done", "rn_done", "s_ready", "mx_done", "s_read", "exp_done", "sum_done", "rl_done", "p_done",
                    "p_turned", "p_placed", "xw_ready", "xw_done", "y_ready", "y_read_a", "y_read_v", "g_ready", "g_read", "mh_ready", "mh_read", "tables_done")}

                def scale_tables(pool):
                    for a in range(2):
                        full = sc[:, a, :].unsqueeze(1).to_broadcast([P, QT, LD])
                        nc.gpsimd.tensor_tensor(tab[:, 2 * a, :, :], base[:, 2 * a, :, :], full, ALU.mult).then_inc(S["tables_done"], 1)
                        for lo, hi in ((0, 32), (32, 0)):
                            part = sc[:, a, hi:hi + 32].unsqueeze(1).to_broadcast([P, QT, 32])
                            nc.gpsimd.tensor_tensor(tab[:, 2 * a + 1, :, lo:lo + 32], base[:, 2 * a + 1, :, lo:lo + 32], part, ALU.mult).then_inc(S["tables_done"], 1)

                with nc.Block() as block:
                    stream_norm(block, (rc[:, 0, :], rc[:, 1, :]),
                                [(xa[0:64, u, WIN:WIN + SEQ], xa[64:P, u, WIN + 1:WIN + 1 + SEQ]) for u in range(BATCH)])

                    @block.gpsimd
                    def _(pool):
                        pool.wait_ge(lin, 32)
                        pool.wait_ge(a_in, A_IN)
                        scale_tables(pool)

                    @block.sync
                    def _(sp):
                        pass

                with nc.Block() as block:
                    @block.gpsimd
                    def _(pool):
                        for one in (*S.values(), *M.values()):
                            pool.sem_inc(one, START)

                def project_qk(pe, done, t, a):
                    pe.wait_ge(*(done("q_read", t + 1) if a else done("k_read", t)))
                    for x in range(2):
                        last = nc.tensor.matmul(ps[:, x, :], xa[:, t // QT, WIN + t % QT * P:WIN + (t % QT + 1) * P],
                                                wqk[:, a * INNER + x * CH:a * INNER + (x + 1) * CH], start=True, stop=True)
                    last.then_inc(S["qk"[a] + "_ready"], 1)

                def square_qk(act, done, t, a):
                    act.wait_ge(*done("qk"[a] + "_ready", t + 1))
                    act.wait_ge(*done("qk"[a] + "_summed", t))
                    nc.scalar.activation(sq[:, a, :].rearrange("p (x n) -> p x n", x=2), ps[:, 0:2, :], ACT.Square).then_inc(S["qk"[a] + "_squared"], 1)

                def deviations(act, done, t):
                    act.wait_ge(*done("q_summed", t + 1))
                    act.wait_ge(*done("k_summed", t + 1))
                    nc.scalar.activation(ss[:, :, :], ss[:, :, :], ACT.Sqrt).then_inc(S["sd_done"], 1)

                def rotate_qk(dve, done, t, a):
                    dve.wait_ge(*done("qk"[a] + "_squared", t + 1))
                    dve.wait_ge(*done("qk"[a] + "_rotated", t))
                    if t >= 2:
                        dve.wait_ge(*done("qk"[a] + "_unit", t - 1))
                    src = ps[:, 0:2, :].rearrange("p x (h d) -> p (x h) d", d=LD)
                    dst = turns[t % 2][a].rearrange("p (h d) -> p h d", d=LD)
                    dsin = rs[:, a, :].rearrange("p (h d) -> p h d", d=LD)
                    nc.vector.tensor_tensor(dst, src, tab[:, 2 * a, t % QT, :].unsqueeze(1).to_broadcast([P, LH, LD]), ALU.mult)
                    for lo, hi in ((0, 32), (32, 0)):
                        ins = nc.vector.tensor_tensor(dsin[:, :, lo:lo + 32], src[:, :, hi:hi + 32],
                                                      tab[:, 2 * a + 1, t % QT, lo:lo + 32].unsqueeze(1).to_broadcast([P, LH, 32]), ALU.mult)
                    ins.then_inc(S["qk"[a] + "_read"], 1)

                def sum_qk(dve, done, t, a):
                    dve.wait_ge(*done("qk"[a] + "_squared", t + 1))
                    nc.vector.tensor_reduce(ss[:, a, :], sq[:, a, :].rearrange("p (h d) -> p h d", d=LD), AX.X, ALU.add).then_inc(S["qk"[a] + "_summed"], 1)

                def reciprocal_norms(dve, done, t):
                    dve.wait_ge(*done("sd_done", t + 1))
                    dve.wait_ge(*done("k_unit", t))
                    dve.wait_ge(*done("q_unit", t))
                    nc.vector.tensor_scalar(rn[:, :, :], ss[:, :, :], 1e-12, None, ALU.max).then_inc(S["rmax_done"], 1)
                    dve.wait_ge(*done("rmax_done", t + 1))
                    nc.vector.reciprocal(rn[:, :, :], rn[:, :, :]).then_inc(S["rn_done"], 1)

                def add_rotated(pool, done, t, a):
                    pool.wait_ge(*done("qk"[a] + "_read", t + 1))
                    nc.gpsimd.tensor_tensor(turns[t % 2][a], turns[t % 2][a], rs[:, a, :], ALU.add).then_inc(S["qk"[a] + "_rotated"], 1)

                def scale_to_unit(pool, done, t, a):
                    pool.wait_ge(*done("qk"[a] + "_rotated", t + 1))
                    pool.wait_ge(*done("rn_done", t + 1))
                    pool.wait_ge(*done("qk"[a] + "_turned", t))
                    nc.gpsimd.tensor_tensor(qkn[:, a, :].rearrange("p (h d) -> p h d", d=LD),
                                            turns[t % 2][a].rearrange("p (h d) -> p h d", d=LD),
                                            rn[:, a, :].unsqueeze(2).to_broadcast([P, LH, LD]), ALU.mult).then_inc(S["qk"[a] + "_unit"], 1)

                def signals(n0):
                    def done(name, n, per_tile=1):
                        return S[name], per_tile * n0 + n + START
                    return done

                with nc.Block() as block:
                    then = signals(0)

                    @block.tensor
                    def _(pe):
                        for a in range(2):
                            project_qk(pe, then, 0, a)

                    @block.scalar
                    def _(act):
                        for a in range(2):
                            square_qk(act, then, 0, a)
                        deviations(act, then, 0)

                    @block.vector
                    def _(dve):
                        for a in range(2):
                            rotate_qk(dve, then, 0, a)
                            sum_qk(dve, then, 0, a)
                        reciprocal_norms(dve, then, 0)

                    @block.gpsimd
                    def _(pool):
                        for stage in (add_rotated, scale_to_unit):
                            for a in range(2):
                                stage(pool, then, 0, a)

                with nc.Fori(0, DEPTH) as L:
                    def count(name, per_layer, n):
                        return M[name], L * per_layer + n + START

                    ln_place = ((rs[:, 0, :], rs[:, 1, :], 0), (lnc[:], lnq[:], 2))

                    def mean(pe, u):
                        if u:
                            pe.wait_ge(*count("scaled", BATCH, u))
                        for cc in range(2):
                            last = nc.tensor.matmul(ps[:, cc, :], mean_w[:], xb[:, u, WIN + cc * CH:WIN + (cc + 1) * CH], start=True, stop=True)
                        last.then_inc(M["mean_ready"], 1)

                    def centre(dve, u):
                        dve.wait_ge(*count("mean_ready", BATCH, u + 1))
                        nc.vector.tensor_tensor(ln_place[u][0], xb[:, u, WIN:WIN + SEQ], pair(0), ALU.subtract).then_inc(M["centred"], 1)

                    def squares_ln(act, u):
                        act.wait_ge(*count("centred", BATCH, u + 1))
                        nc.scalar.activation(ln_place[u][1], ln_place[u][0], ACT.Square).then_inc(M["squared"], 1)

                    def variance(pe, u):
                        pe.wait_ge(*count("squared", BATCH, u + 1))
                        for x in range(QT):
                            last = nc.tensor.matmul(ps[:, ln_place[u][2], x:x + 1], ln_place[u][1][:, x * P:(x + 1) * P], mean_w[:, 0:1], start=True, stop=True)
                        last.then_inc(M["var_ready"], 1)

                    def deviation(act, u):
                        act.wait_ge(*count("var_ready", BATCH, u + 1))
                        nc.scalar.activation(dev[:, u, :], ps[:, ln_place[u][2], 0:QT], ACT.Sqrt, bias=eps_col[:, 0:1]).then_inc(M["dev_done"], 1)

                    def factors(dve, u):
                        dve.wait_ge(*count("dev_done", BATCH, u + 1))
                        nc.vector.reciprocal(rdev[:, u, :], dev[:, u, :]).then_inc(M["rdev_done"], 1)
                        dve.wait_ge(*count("rdev_done", BATCH, u + 1))
                        nc.vector.tensor_tensor(ln_place[u][1].rearrange("p (x n) -> p x n", n=P), ident[:].unsqueeze(1).to_broadcast([P, QT, P]),
                                                rdev[:, u, :].unsqueeze(2).to_broadcast([P, QT, P]), ALU.mult).then_inc(M["diag_done"], 1)

                    def spread(pe, u):
                        pe.wait_ge(*count("diag_done", BATCH, u + 1))
                        for cc in range(2):
                            last = nc.tensor.matmul(ps[:, cc, :], ones_w[:], ln_place[u][1][:, cc * CH:(cc + 1) * CH], start=True, stop=True)
                        last.then_inc(M["spread_ready"], 1)

                    def normalise_ln(dve, u):
                        dve.wait_ge(m_in, M_IN * (L + 1))
                        dve.wait_ge(*count("spread_ready", BATCH, u + 1))
                        nc.vector.tensor_tensor(ln_place[u][0], ln_place[u][0], pair(0), ALU.mult).then_inc(M["scaled"], 1)
                        dve.wait_ge(*count("scaled", BATCH, u + 1))
                        nc.vector.tensor_scalar(ln_place[u][0], ln_place[u][0], gcols[:, 0:1], gcols[:, 1:2], ALU.mult, ALU.add).then_inc(M["xn_done"], 1)

                    with nc.Block() as block:
                        n0 = L * TILES

                        done = signals(n0)

                        def tile(t, stage, *args):
                            if 0 <= t < TILES:
                                stage(t, *args)

                        TURNS = range(-4, TILES + 1)

                        @block.sync
                        def _(sp):
                            load_mlp(sp, L)

                        @block.tensor
                        def _(pe):
                            shared = []

                            def product(t, a):
                                if t:
                                    project_qk(pe, done, t, a)

                            def transposes(what, t, src):
                                if shared:
                                    pe.wait_ge(*done(*shared[-1]))
                                for x in range(8):
                                    last = nc.tensor.transpose(ps[:, 2 + x // 4, (x % 4) * P:(x % 4 + 1) * P],
                                                               src[:, x * P:(x + 1) * P], ident[:])
                                last.then_inc(S[what + "_turned"], 1)
                                shared.append((what + "_placed", t + 1))

                            def transpose_qk(t, a):
                                pe.wait_ge(*done("qk"[a] + "_unit", t + 1))
                                transposes("qk"[a], t, qkn[:, a, :])

                            def transpose_p(t):
                                pe.wait_ge(*done("p_done", t + 1))
                                transposes("p", t, pn[:, :, :].rearrange("p h j -> p (h j)"))

                            def score(t, part):
                                if part == 0:
                                    pe.wait_ge(S["mh_read"], L + 1 + START)
                                    pe.wait_ge(*done("s_read", t))
                                    pe.wait_ge(*done("q_placed", t + 1))
                                    pe.wait_ge(*done("k_placed", t + 1))
                                    for x in range(2):
                                        nc.tensor.matmul(ps[:, 4 + x, :], identb[:],
                                                         lmask[:, t % QT, :].unsqueeze(1).to_broadcast([P, 8, 2 * WIN]),
                                                         start=True, stop=False, skip_group_check=True)
                                for h in range(8 * part, 8 * part + 8):
                                    e = 64 * (h % 2)
                                    for w in range(4):
                                        last = nc.tensor.matmul(
                                            ps[32 * w:32 * w + 32, 4 + h % 2, (h // 2) * 64:(h // 2 + 1) * 64],
                                            qt_[e:e + 64, t % 2, h // 2, 32 * w:32 * w + 32],
                                            kt_[e:e + 64, h // 2, t % QT * P + 32 * w:t % QT * P + 32 * w + 64],
                                            start=False, stop=True, skip_group_check=True)
                                if part == 1:
                                    last.then_inc(S["s_ready"], 1)

                            def windows(t):
                                pe.wait_ge(S["mh_read"], L + 1 + START)
                                pe.wait_ge(*done("y_read_a", 2 * t, 2))
                                for w in range(2):
                                    o = t % QT * P + 32 * w
                                    last = nc.tensor.transpose(ps[:, 6, w * P:(w + 1) * P], xa[:, t // QT, o:o + P], ident[:])
                                last.then_inc(S["xw_ready"], 1)

                            def mix(t, half):
                                if half == 0:
                                    pe.wait_ge(*done("xw_done", t + 1))
                                    pe.wait_ge(*done("p_placed", t + 1))
                                pe.wait_ge(*done("y_read_v", 2 * t + half, 2))
                                pe.wait_ge(*done("y_read_a", 2 * t + half, 2))
                                for w in range(2):
                                    for e in range(2):
                                        ww = 2 * half + w
                                        last = nc.tensor.matmul(ps[:, 6 + e, w * 256:(w + 1) * 256], xw[:, ww, e, :],
                                                                ptl[:, :, 32 * ww:32 * ww + 32], start=True, stop=True)
                                last.then_inc(S["y_ready"], 1)

                            def project(t):
                                if t % 4 != 3:
                                    return
                                pe.wait_ge(*done("y_read_v", 2 * t + 2, 2))
                                pe.wait_ge(*done("y_read_a", 2 * t + 2, 2))
                                pe.wait_ge(*done(*shared[-1]))
                                for h in range(LH):
                                    last = nc.tensor.matmul(ps[:, 2, :], mh[:, h, :], yb[:, h, :], start=h == 0, stop=h == LH - 1)
                                last.then_inc(S["g_ready"], 1)
                                shared.append(("g_read", t + 1))

                            def ln_mean(t):
                                if t == TILES - 1:
                                    pe.wait_ge(*done("k_read", TILES))
                                    mean(pe, 0)

                            def ln_variance(t):
                                if t == TILES - 1:
                                    variance(pe, 0)

                            def ln_spread(t):
                                if t == TILES - 1:
                                    spread(pe, 0)

                            def head_weights():
                                for h in range(LH):
                                    e = 64 * (h % 2)
                                    last = nc.tensor.matmul(ps[:, 4 + h // 8 * 2 + h % 2, h % 8 // 2 * P:(h % 8 // 2 + 1) * P],
                                                            wvt[e:e + 64, h // 2, :], wo[e:e + 64, h // 2, :], start=True, stop=True)
                                last.then_inc(S["mh_ready"], 1)

                            pe.wait_ge(a_in, A_IN * (L + 1))
                            for i in TURNS:
                                if i == -2:
                                    head_weights()
                                tile(i + 1, ln_mean)
                                tile(i, ln_variance)
                                tile(i - 1, mix, 1)
                                tile(i + 1, score, 0)
                                tile(i, windows)
                                tile(i, transpose_p)
                                tile(i + 1, score, 1)
                                tile(i, ln_spread)
                                tile(i - 1, project)
                                tile(i + 3, product, 1)
                                tile(i + 2, transpose_qk, 0)
                                tile(i, mix, 0)
                                tile(i + 2, transpose_qk, 1)
                                tile(i + 4, product, 0)

                        @block.scalar
                        def _(act):
                            def squares(t, a):
                                if t:
                                    square_qk(act, done, t, a)

                            def norms(t):
                                if t:
                                    deviations(act, done, t)

                            def place_q(t):
                                act.wait_ge(*done("q_turned", t + 1))
                                act.wait_ge(*done("s_ready", max(t - 1, 0)))
                                nc.scalar.activation(qt_[:, t % 2, :, :].rearrange("p (x g) n -> p x (g n)", x=2), ps[:, 2:4, :], ACT.Copy).then_inc(S["q_placed"], 1)

                            def place_k(t):
                                act.wait_ge(*done("k_turned", t + 1))
                                if t >= QT:
                                    act.wait_ge(*done("s_ready", t - QT + 2))
                                for x in range(2):
                                    ins = nc.scalar.activation(kt_[:, 4 * x:4 * x + 4, WIN + t % QT * P:WIN + (t % QT + 1) * P],
                                                               ps[:, 2 + x, :].rearrange("p (g n) -> p g n", n=P), ACT.Copy)
                                ins.then_inc(S["k_placed"], 1)

                            def place_p(t):
                                act.wait_ge(*done("p_turned", t + 1))
                                act.wait_ge(*done("y_ready", 2 * t, 2))
                                nc.scalar.activation(ptl[:, :, :].rearrange("p (x g) n -> p x (g n)", x=2), ps[:, 2:4, :], ACT.Copy).then_inc(S["p_placed"], 1)

                            def place_windows(t):
                                act.wait_ge(*done("xw_ready", t + 1))
                                act.wait_ge(*done("y_ready", 2 * t, 2))
                                for r in range(2):
                                    src = ps[64 * r:64 * r + 64, 6, 0:2 * P].rearrange("p (w n) -> p w n", n=P)
                                    for e in range(2):
                                        ins = nc.scalar.activation(xw[64 * e:64 * e + 64, 2 * r:2 * r + 2, e, :], src, ACT.Copy)
                                ins.then_inc(S["xw_done"], 1)

                            def exponentials(t):
                                act.wait_ge(*done("s_read", t + 1))
                                nc.scalar.activation(pe_[:, :, :], pe_[:, :, :], ACT.Exp, scale=8.0).then_inc(S["exp_done"], 1)

                            def take_mixed(t, half):
                                act.wait_ge(*done("y_ready", 2 * t + half + 1, 2))
                                act.wait_ge(S["g_ready"], L * (TILES // 4) + t // 4 + START)
                                o = (t % 4) * P + half * 64
                                for w in range(2):
                                    ins = nc.scalar.activation(
                                        yb[:, :, o + 32 * w:o + 32 * w + 32].rearrange("p (g e) n -> p e g n", e=2)[:, 0],
                                        ps[:, 6, w * 256:(w + 1) * 256].rearrange("p (g n) -> p g n", n=WIN), ACT.Copy)
                                ins.then_inc(S["y_read_a"], 1)

                            def ln_square(t):
                                if t == TILES - 1:
                                    squares_ln(act, 0)

                            def ln_deviation(t):
                                if t == TILES - 1:
                                    deviation(act, 0)

                            def take_head_weights():
                                act.wait_ge(S["mh_ready"], L + 1 + START)
                                for g in range(2):
                                    ins = nc.scalar.activation(mh[:, 8 * g:8 * g + 8, :].rearrange("p (r e) n -> p e r n", e=2),
                                                               ps[:, 4 + 2 * g:6 + 2 * g, :].rearrange("p e (r n) -> p e r n", n=P), ACT.Copy)
                                ins.then_inc(S["mh_read"], 1)

                            for i in TURNS:
                                if i == -2:
                                    take_head_weights()
                                tile(i, place_p)
                                tile(i + 3, squares, 1)
                                tile(i + 2, place_q)
                                tile(i + 1, ln_square)
                                tile(i + 1, exponentials)
                                tile(i, take_mixed, 0)
                                tile(i + 2, place_k)
                                tile(i + 4, squares, 0)
                                tile(i + 1, ln_deviation)
                                tile(i, take_mixed, 1)
                                tile(i + 3, norms)
                                tile(i + 1, place_windows)

                        @block.gpsimd
                        def _(pool):
                            def add(t, a):
                                if t:
                                    add_rotated(pool, done, t, a)

                            def unit(t, a):
                                if t:
                                    scale_to_unit(pool, done, t, a)

                            for i in TURNS:
                                tile(i + 1, unit, 0)
                                tile(i + 1, unit, 1)
                                tile(i + 2, add, 0)
                                tile(i + 2, add, 1)

                        @block.vector
                        def _(dve):
                            def rotate(t, a):
                                if t:
                                    rotate_qk(dve, done, t, a)

                            def sum_squares(t, a):
                                if t:
                                    sum_qk(dve, done, t, a)

                            def norms(t):
                                if t:
                                    reciprocal_norms(dve, done, t)

                            def subtract_maxima(t):
                                dve.wait_ge(*done("s_ready", t + 1))
                                sc_ps = ps[:, 4:6, :].rearrange("p e (g j) -> p e g j", j=2 * WIN)
                                mxv = mx[:].rearrange("p (e g) -> p e g", e=2)
                                nc.vector.tensor_reduce(mxv, sc_ps, AX.X, ALU.max).then_inc(S["mx_done"], 1)
                                dve.wait_ge(*done("mx_done", t + 1))
                                nc.vector.tensor_tensor(pe_[:, :, :].rearrange("p (g e) j -> p e g j", e=2), sc_ps,
                                                        mxv.unsqueeze(3).to_broadcast([P, 2, LH // 2, 2 * WIN]), ALU.subtract).then_inc(S["s_read"], 1)

                            def sums(t):
                                dve.wait_ge(*done("exp_done", t + 1))
                                nc.vector.tensor_reduce(lsum[:], pe_[:, :, :], AX.X, ALU.add).then_inc(S["sum_done"], 1)
                                dve.wait_ge(*done("sum_done", t + 1))
                                nc.vector.reciprocal(rl[:], lsum[:]).then_inc(S["rl_done"], 1)

                            def normalise(t):
                                dve.wait_ge(*done("rl_done", t + 1))
                                dve.wait_ge(*done("p_turned", t))
                                nc.vector.tensor_tensor(pn[:, :, :], pe_[:, :, :], rl[:].unsqueeze(2).to_broadcast([P, LH, 2 * WIN]), ALU.mult).then_inc(S["p_done"], 1)

                            def take_mixed(t, half):
                                dve.wait_ge(*done("y_ready", 2 * t + half + 1, 2))
                                dve.wait_ge(S["g_ready"], L * (TILES // 4) + t // 4 + START)
                                o = (t % 4) * P + half * 64
                                for w in range(2):
                                    ins = nc.vector.tensor_copy(
                                        yb[:, :, o + 32 * w:o + 32 * w + 32].rearrange("p (g e) n -> p e g n", e=2)[:, 1],
                                        ps[:, 7, w * 256:(w + 1) * 256].rearrange("p (g n) -> p g n", n=WIN))
                                ins.then_inc(S["y_read_v"], 1)

                            def take_projected(t):
                                if t % 4 != 3:
                                    return
                                dve.wait_ge(S["g_ready"], L * (TILES // 4) + t // 4 + 1 + START)
                                o = WIN + (t % QT // 4) * CH
                                nc.vector.tensor_tensor(xb[0:64, t // QT, o:o + CH], ps[0:64, 2, :], xa[0:64, t // QT, o:o + CH], ALU.add)
                                nc.vector.tensor_tensor(xb[64:P, t // QT, o + 1:o + 1 + CH], ps[64:P, 2, :], xa[64:P, t // QT, o + 1:o + 1 + CH], ALU.add).then_inc(S["g_read"], 4)

                            def ln_centre(t):
                                if t == TILES - 1:
                                    dve.wait_ge(*done("q_rotated", TILES))
                                    dve.wait_ge(*done("k_rotated", TILES))
                                    centre(dve, 0)

                            def ln_factors(t):
                                if t == TILES - 1:
                                    factors(dve, 0)

                            def ln_scale(t):
                                if t == TILES - 1:
                                    normalise_ln(dve, 0)

                            for i in TURNS:
                                tile(i, take_mixed, 0)
                                tile(i + 1, sums)
                                tile(i + 3, sum_squares, 1)
                                tile(i + 2, ln_centre)
                                tile(i + 1, normalise)
                                tile(i + 1, ln_factors)
                                tile(i + 4, rotate, 0)
                                tile(i + 3, norms)
                                tile(i, take_mixed, 1)
                                tile(i, ln_scale)
                                tile(i + 4, sum_squares, 0)
                                tile(i + 2, subtract_maxima)
                                tile(i, take_projected)
                                tile(i + 4, rotate, 1)

                    with nc.Block() as block:
                        then = signals((L + 1) * TILES)

                        def ahead(pool):
                            for stage in (add_rotated, scale_to_unit):
                                for a in range(2):
                                    stage(pool, then, 0, a)

                        @block.sync
                        def _(sp):
                            load_attn(sp, L + 1)

                        @block.gpsimd
                        def _(pool):
                            pool.wait_ge(a_in, A_IN * (L + 2))
                            scale_tables(pool)
                            ahead(pool)

                        @block.tensor
                        def _(pe):
                            def hidden(c, g):
                                n = 3 * c + g
                                h0, w = HCH[g]
                                if g == 0:
                                    pe.wait_ge(*count("xn_done", BATCH, c // 2 + 1))
                                if n >= 2:
                                    pe.wait_ge(*count("h_done", 12, n - 1))
                                for half in (1, 0):
                                    last = nc.tensor.matmul(ps[0:w, 3 + 2 * (n % 2) + half, :], w1[:, half * HID + h0:half * HID + h0 + w],
                                                            ln_place[c // 2][0][:, (c % 2) * CH:(c % 2 + 1) * CH], start=True, stop=True)
                                    last.then_inc(M["gate_ready" if half else "a_ready"], 1)

                            def output(c):
                                pe.wait_ge(*count("h_done", 12, 3 * c + 3))
                                if c:
                                    pe.wait_ge(*count("out_done", 4, c))
                                for g, (h0, w) in enumerate(HCH):
                                    last = nc.tensor.matmul(ps[:, 7, :], w2[0:w, g, :], hh[0:w, c % 2, g, :], start=g == 0, stop=g == 2)
                                last.then_inc(M["w2_ready"], 1)

                            pe.wait_ge(m_in, M_IN * (L + 1))
                            mean(pe, 1)
                            for g in range(3):
                                hidden(0, g)
                            variance(pe, 1)
                            hidden(1, 0)
                            output(0)
                            spread(pe, 1)
                            hidden(1, 1)
                            hidden(1, 2)
                            output(1)
                            pe.wait_ge(a_in, A_IN * (L + 2))
                            pe.wait_ge(*count("scaled", BATCH, 2))
                            pe.wait_ge(*count("out_done", 4, 1))
                            project_qk(pe, then, 0, 0)
                            hidden(2, 0)
                            hidden(2, 1)
                            hidden(2, 2)
                            project_qk(pe, then, 0, 1)
                            hidden(3, 0)
                            output(2)
                            hidden(3, 1)
                            hidden(3, 2)
                            output(3)

                        @block.scalar
                        def _(act):
                            def gate(c, g):
                                w = HCH[g][1]
                                act.wait_ge(*count("gate_ready", 12, 3 * c + g + 1))
                                nc.scalar.activation(gl[0:w, c % 2, g, :], ps[0:w, 4 + 2 * ((3 * c + g) % 2), :], ACT.Gelu, bias=b1[0:w, 1, g:g + 1]).then_inc(M["gelu_done"], 1)

                            act.wait_ge(m_in, M_IN * (L + 1))
                            squares_ln(act, 1)
                            for g in range(3):
                                gate(0, g)
                            deviation(act, 1)
                            for g in range(3):
                                gate(1, g)
                            square_qk(act, then, 0, 0)
                            for g in range(3):
                                gate(2, g)
                            square_qk(act, then, 0, 1)
                            gate(3, 0)
                            deviations(act, then, 0)
                            gate(3, 1)
                            gate(3, 2)

                        @block.vector
                        def _(dve):
                            def products(c, first, end):
                                for g in range(first, end):
                                    n, w = 3 * c + g, HCH[g][1]
                                    dve.wait_ge(*count("gelu_done", 12, n + 1))
                                    dve.wait_ge(*count("a_ready", 12, n + 1))
                                    nc.vector.scalar_tensor_tensor(hh[0:w, c % 2, g, :], ps[0:w, 3 + 2 * (n % 2), :], b1[0:w, 0, g:g + 1], gl[0:w, c % 2, g, :], ALU.add, ALU.mult).then_inc(M["h_done"], 1)

                            def stream(c):
                                u, o = c // 2, WIN + (c % 2) * CH
                                dve.wait_ge(*count("w2_ready", 4, c + 1))
                                nc.vector.scalar_tensor_tensor(xa[0:64, u, o:o + CH], ps[0:64, 7, :], gcols[0:64, 2:3], xb[0:64, u, o:o + CH], ALU.add, ALU.add)
                                nc.vector.scalar_tensor_tensor(xa[64:P, u, o + 1:o + 1 + CH], ps[64:P, 7, :], gcols[64:P, 2:3], xb[64:P, u, o + 1:o + 1 + CH], ALU.add, ALU.add).then_inc(M["out_done"], 1)

                            dve.wait_ge(m_in, M_IN * (L + 1))
                            centre(dve, 1)
                            products(0, 0, 3)
                            factors(dve, 1)
                            products(1, 0, 1)
                            stream(0)
                            normalise_ln(dve, 1)
                            products(1, 1, 3)
                            stream(1)
                            dve.wait_ge(S["tables_done"], 6 * (L + 2) + START)
                            rotate_qk(dve, then, 0, 0)
                            sum_qk(dve, then, 0, 0)
                            products(2, 0, 3)
                            rotate_qk(dve, then, 0, 1)
                            sum_qk(dve, then, 0, 1)
                            products(3, 0, 1)
                            stream(2)
                            reciprocal_norms(dve, then, 0)
                            products(3, 1, 3)
                            stream(3)

                with nc.Block() as block:
                    @block.sync
                    def _(sp):
                        sp.wait_ge(a_in, A_IN * (DEPTH + 1))

                    @block.vector
                    def _(dve):
                        r = res[:, :].rearrange("p (b n) -> p b n", b=BATCH)
                        nc.vector.tensor_tensor(r[0:64], r[0:64], xa[0:64, :, WIN:WIN + SEQ], ALU.add)
                        nc.vector.tensor_tensor(r[64:P], r[64:P], xa[64:P, :, WIN + 1:WIN + 1 + SEQ], ALU.add)

        for stage, which in PLAN:
            (causal if stage == "causal" else layers)(which)

        with nc.Block() as block:
            @block.sync
            def _(sp):
                sp.dma_start(out, res[:]).then_inc(out_done, 16)
                sp.wait_ge(out_done, 16)


def constants():
    f = np.float32

    def bf(a):
        u = np.asarray(a, f).view(np.uint32)
        return ((u + 0x7FFF + ((u >> 16) & 1)) >> 16).astype(np.uint16)

    def parts(a):
        a = np.asarray(a, f)
        out = []
        for _ in range(3):
            out.append((bf(a).astype(np.uint32) << 16).view(f))
            a = a - out[-1]
        return out

    n = np.arange(P)
    mask_q = bf(np.where(n[None, :] > n[:, None], NEG, 0.0))
    crow = {}
    pos = np.arange(SEQ)
    hi = pos // 32 * 32
    for kind in "ab":
        q = np.zeros((CROWS, HEADS, SEQ), f)
        k = np.zeros((CROWS, HEADS, SEQ), f)
        k[0:3] = 1.0
        if kind == "b":
            start = 2.0 ** (-(8.0 / HEADS))
            slopes = np.asarray([start * start ** i for i in range(HEADS)], f)
            for i, part in enumerate(parts(slopes)):
                q[3 + 2 * i] = q[4 + 2 * i] = part[:, None]
                k[3 + 2 * i] = hi
                k[4 + 2 * i] = pos - hi
        crow["crow_q" + kind], crow["crow_k" + kind] = bf(q), bf(k)
    half = np.arange(0, LD, 2, dtype=f)
    freqs = np.arange(SEQ, dtype=f)[:, None] * (f(1.0) / f(10000.0) ** (half / f(LD)))[None, :]
    freqs = np.concatenate([freqs, freqs], -1)
    base_scale = (half + f(0.4 * LD)) / f(1.4 * LD)
    power = (np.arange(SEQ, dtype=f) - SEQ // 2) / f(WIN // 2)
    scale = base_scale[None, :] ** power[:, None]
    scale = np.concatenate([scale, scale], -1)
    sign = np.concatenate([-np.ones(LD // 2, f), np.ones(LD // 2, f)])
    cos, sin = np.cos(freqs), np.sin(freqs) * sign
    rot = np.stack([cos * scale, sin * scale, cos / scale, sin / scale]).astype(f)
    rot = np.ascontiguousarray(rot.reshape(4, QT, P, LD).transpose(2, 0, 1, 3))
    i = n % WIN
    j = np.arange(2 * WIN)
    ok = (j[None, :] >= i[:, None]) & (j[None, :] <= i[:, None] + WIN)
    lmask = np.repeat(np.where(ok, 0.0, NEG)[:, None, :], QT, 1)
    lmask[:WIN, 0, :WIN] = NEG
    return {"ident": np.eye(P, dtype=f), "identb": bf(np.eye(P)), "mask_q": mask_q,
            "mask_k": np.ascontiguousarray(mask_q.T), "rot": rot, "lmask": bf(lmask),
            **crow}


BF16_CONSTANTS = ("identb", "mask_q", "mask_k", "lmask", "crow_qa", "crow_ka", "crow_qb", "crow_kb")


def arrays(inputs):
    g = {k.replace("L0_", ""): np.asarray(v) for k, v in inputs.items()}

    def tr(a):
        return np.ascontiguousarray(np.swapaxes(a, -1, -2))

    def wrap(a):
        return np.concatenate([a, a[:1]])

    wv = g["ffn_Wqkv"][:, :, 2 * INNER:]
    wvt = np.ascontiguousarray(wv.reshape(DEPTH, P, LH // 2, P).transpose(0, 3, 2, 1))
    d = {"x": tr(g["attn_a_x"].reshape(TOK, P)),
         "WqT": tr(g["attn_a_Wq"]), "WkT": tr(g["attn_a_Wk"]), "WvT": tr(g["attn_a_Wv"]), "WoT": tr(g["attn_a_Wo"]),
         "bq": g["attn_a_bq"], "bk": g["attn_a_bk"], "bv": g["attn_a_bv"], "bo": g["attn_a_bo"],
         "ln_g": g["attn_a_ln_g"], "ln_b": g["attn_a_ln_b"], "WoutT": tr(g["attn_a_Wout"]),
         "bout": g["attn_a_bout"], "ln2_g": g["attn_a_ln2_g"], "ln2_b": g["attn_a_ln2_b"],
         "bWqkv": g["attn_b_Wqkv"], "bWout": g["attn_b_Wout"],
         "lWqkv": wrap(g["ffn_Wqkv"]), "lWvT": wrap(wvt), "lWo": wrap(g["ffn_Wo"]),
         "q_scale": wrap(g["ffn_q_scale"]), "k_scale": wrap(g["ffn_k_scale"]),
         "lg": g["ffn_ln_g"], "lb": g["ffn_ln_b"], "lW1": g["ffn_W1"], "lb1": g["ffn_b1"],
         "lW2": g["ffn_W2"], "lb2": g["ffn_b2"]}
    return {**d, **constants()}


def kernel(**inputs):
    import concourse.bacc as bacc
    from concourse.bass_utils import run_bass_kernel_spmd

    nc = bacc.Bacc("TRN2", target_bir_lowering=False, num_devices=1)
    data = {"in_" + k: np.ascontiguousarray(v) for k, v in arrays(inputs).items()}
    t = {k[3:]: nc.dram_tensor(k, v.shape, mybir.dt.from_np(v.dtype), kind="ExternalInput").ap() for k, v in data.items()}
    out = nc.dram_tensor("out", (P, TOK), F32, kind="ExternalOutput").ap()
    scratch = nc.dram_tensor("scratch", (2, 2, 3, P, SEQ), BF16, kind="Internal").ap()
    t = {k: ap.bitcast(BF16) if k in BF16_CONSTANTS else ap for k, ap in t.items()}
    build(nc, t, out, scratch)
    r = run_bass_kernel_spmd(nc, [data], core_ids=[0])
    y = r.results[0]["out"]
    return np.ascontiguousarray(y.T).reshape(BATCH, SEQ, P)
```
